# Optimizing a Trainium2 kernel written in Bass

```python
import numpy as np
import jax
import jax.numpy as jnp

def _softmax(x, axis=-1):
    return jax.nn.softmax(x, axis=axis)

def _gelu(x):
    return jax.nn.gelu(x, approximate=True)

def _silu(x):
    return jax.nn.silu(x)

def _sigmoid(x):
    return jax.nn.sigmoid(x)

def _layernorm(x, axis=-1, eps=1e-05):
    m = jnp.mean(x, axis=axis, keepdims=True)
    v = jnp.var(x, axis=axis, keepdims=True)
    return (x - m) / jnp.sqrt(v + eps)

def _scatter_add(tgt, idx, src, axis=0):
    return tgt.at[idx].add(src)

def _segment_sum(src, seg, n):
    return jax.ops.segment_sum(src, seg, n)
kernel_name = 'mk_cond_seq_d4_seqx_r4_4fd675'

def setup_inputs(seed: int=0):
    np.random.seed(seed)
    _w = jnp.asarray

    def _rec_inputs():
        import jax
        import jax.numpy as jnp
        _rk = jax.random.key(seed)
        x = -0.0003482 + 1 * jax.random.normal(jax.random.fold_in(_rk, 1), (8, 256, 288), jnp.float32)
        _lenS = 256 - jax.random.randint(jax.random.fold_in(_rk, 7), (8,), 0, max(1, 256 // 4) + 1, jnp.int32)
        _lenS2 = 256 - jax.random.randint(jax.random.fold_in(_rk, 8), (8,), 0, max(1, 256 // 4) + 1, jnp.int32)
        cond_1152 = 0.00257642 + 1.0011 * jax.random.normal(jax.random.fold_in(_rk, 11), (8, 288), jnp.float32)
        return (x, cond_1152)
    x, cond_1152 = _rec_inputs()

    def _L0_cond_setup():
        import jax, jax.numpy as jnp
        import numpy as np
        from jax.scipy.linalg import expm
        N, D, COND_DIM = (288, 64, 288)
        B, T = (16, 256)

        def _rotation(cond, W, b):
            v = jax.nn.silu(cond) @ W.T + b
            iu, ju = jnp.triu_indices(D, k=1)
            A = jnp.zeros((cond.shape[0], D, D), dtype=v.dtype)
            A = A.at[:, iu, ju].set(v).at[:, ju, iu].set(-v)
            return expm(A)
        key = jax.random.key(seed)
        k1, k2, k3, k4, k5 = jax.random.split(key, 5)
        x = jax.random.normal(k1, (B, T, N), dtype=jnp.float32)
        cond = jax.random.normal(k2, (B, COND_DIM), dtype=jnp.float32)
        P = jax.random.normal(k3, (N, D), dtype=jnp.float32)
        n_skew = D * (D - 1) // 2
        bound = 1.0 / np.sqrt(COND_DIM)
        W = jax.random.uniform(k4, (n_skew, COND_DIM), minval=-bound, maxval=bound, dtype=jnp.float32)
        b = jax.random.uniform(k5, (n_skew,), minval=-bound, maxval=bound, dtype=jnp.float32)
        return {'x': x, 'cond': cond, 'P': P, 'W': W, 'b': b}
    _L0_cond_all = _L0_cond_setup()
    _L0_cond_in = {k: v for k, v in _L0_cond_all.items() if k in ('P', 'W', 'b')}
    del _L0_cond_all

    def _L1_cond_setup():
        import jax, jax.numpy as jnp
        import numpy as np
        B, L, C = (8, 256, 288)
        H = 16
        D = C // H
        FF = int(C * 4.0)
        EPS = 1e-06

        def _layernorm(x):
            mu = jnp.mean(x, axis=-1, keepdims=True)
            var = jnp.mean(jnp.square(x - mu), axis=-1, keepdims=True)
            return (x - mu) * jax.lax.rsqrt(var + EPS)

        def _modulate(x, shift, scale):
            return x * (1.0 + scale) + shift

        def _attention(h, W_qkv, b_qkv, W_proj, b_proj):
            b, l, c = h.shape
            qkv = h @ W_qkv + b_qkv
            qkv = qkv.reshape(b, l, 3, H, D)
            q, k, v = (qkv[:, :, 0], qkv[:, :, 1], qkv[:, :, 2])
            scale = D ** (-0.5)
            scores = jnp.einsum('blhd,bmhd->bhlm', q * scale, k)
            attn = jax.nn.softmax(scores, axis=-1)
            o = jnp.einsum('bhlm,bmhd->blhd', attn, v).reshape(b, l, c)
            return o @ W_proj + b_proj
        key = jax.random.key(seed)
        ks = jax.random.split(key, 12)
        s = 0.02
        return {'x': jax.random.normal(ks[0], (B, L, C), jnp.float32), 'c': jax.random.normal(ks[1], (B, 1, C), jnp.float32), 'W_qkv': jax.random.normal(ks[2], (C, 3 * C), jnp.float32) * s, 'b_qkv': jnp.zeros((3 * C,), jnp.float32), 'W_proj': jax.random.normal(ks[3], (C, C), jnp.float32) * s, 'b_proj': jnp.zeros((C,), jnp.float32), 'W_fc1': jax.random.normal(ks[4], (C, FF), jnp.float32) * s, 'b_fc1': jnp.zeros((FF,), jnp.float32), 'W_fc2': jax.random.normal(ks[5], (FF, C), jnp.float32) * s, 'b_fc2': jnp.zeros((C,), jnp.float32), 'W_ada': jax.random.normal(ks[6], (C, 6 * C), jnp.float32) * s, 'b_ada': jnp.zeros((6 * C,), jnp.float32)}
    _L1_cond_all = _L1_cond_setup()
    _L1_cond_in = {k: v for k, v in _L1_cond_all.items() if k in ('W_qkv', 'b_qkv', 'W_proj', 'b_proj', 'W_fc1', 'b_fc1', 'W_fc2', 'b_fc2', 'W_ada', 'b_ada')}
    del _L1_cond_all

    def _L2_cond_setup():
        import math
        import jax, jax.numpy as jnp
        import numpy as np
        B, T, D = (8, 256, 288)
        H = 16
        E = 4
        EPS = 1e-06

        def _layer_norm(x):
            mu = jnp.mean(x, axis=-1, keepdims=True)
            var = jnp.mean(jnp.square(x - mu), axis=-1, keepdims=True)
            return (x - mu) * jax.lax.rsqrt(var + EPS)

        def _modulate(x, shift, scale):
            return x * (1.0 + scale) + shift

        def _attention(y, qkv_w, qkv_b, out_w, out_b):
            b, t, d = y.shape
            hd = d // H
            qkv = y @ qkv_w + qkv_b
            q, k, v = jnp.split(qkv, 3, axis=-1)
            q = q.reshape(b, t, H, hd).transpose(0, 2, 1, 3)
            k = k.reshape(b, t, H, hd).transpose(0, 2, 1, 3)
            v = v.reshape(b, t, H, hd).transpose(0, 2, 1, 3)
            scores = jnp.einsum('bhqd,bhkd->bhqk', q, k) / math.sqrt(hd)
            attn = jax.nn.softmax(scores, axis=-1)
            out = jnp.einsum('bhqk,bhkd->bhqd', attn, v)
            out = out.transpose(0, 2, 1, 3).reshape(b, t, d)
            return out @ out_w + out_b
        key = jax.random.key(seed)
        ks = jax.random.split(key, 12)
        std = 0.02
        return {'x': jax.random.normal(ks[0], (B, T, D), dtype=jnp.float32), 'c': jax.random.normal(ks[1], (B, D), dtype=jnp.float32), 'qkv_w': jax.random.normal(ks[2], (D, 3 * D), dtype=jnp.float32) * std, 'qkv_b': jnp.zeros((3 * D,), dtype=jnp.float32), 'out_w': jax.random.normal(ks[3], (D, D), dtype=jnp.float32) * std, 'out_b': jnp.zeros((D,), dtype=jnp.float32), 'w1': jax.random.normal(ks[4], (D, E * D), dtype=jnp.float32) * std, 'b1': jnp.zeros((E * D,), dtype=jnp.float32), 'w2': jax.random.normal(ks[5], (E * D, D), dtype=jnp.float32) * std, 'b2': jnp.zeros((D,), dtype=jnp.float32), 'ada_w': jax.random.normal(ks[6], (D, 6 * D), dtype=jnp.float32) * std, 'ada_b': jnp.zeros((6 * D,), dtype=jnp.float32)}
    _L2_cond_all = _L2_cond_setup()
    _L2_cond_in = {k: v for k, v in _L2_cond_all.items() if k in ('qkv_w', 'qkv_b', 'out_w', 'out_b', 'w1', 'b1', 'w2', 'b2', 'ada_w', 'ada_b')}
    del _L2_cond_all

    def _L3_cond_setup():
        import jax, jax.numpy as jnp
        import numpy as np
        NUM_HEADS = 16
        NUM_EXPERTS = 4
        TOP_K = 2
        LN_EPS = 1e-06

        def _ln(h):
            mu = jnp.mean(h, axis=-1, keepdims=True)
            var = jnp.var(h, axis=-1, keepdims=True)
            return (h - mu) * jax.lax.rsqrt(var + LN_EPS)

        def _modulate(h, shift, scale):
            return h * (1.0 + scale[:, None, :]) + shift[:, None, :]
        key = jax.random.key(seed)
        ks = jax.random.split(key, 12)
        B, N, C = (8, 256, 288)
        H = 4 * C
        E = NUM_EXPERTS
        s = 0.02
        return {'x': jax.random.normal(ks[0], (B, N, C), jnp.float32), 'c': jax.random.normal(ks[1], (B, C), jnp.float32), 'w_adaln': jax.random.normal(ks[2], (C, 6 * C), jnp.float32) * s, 'b_adaln': jnp.zeros((6 * C,), jnp.float32), 'w_qkv': jax.random.normal(ks[3], (C, 3 * C), jnp.float32) * s, 'b_qkv': jnp.zeros((3 * C,), jnp.float32), 'w_proj': jax.random.normal(ks[4], (C, C), jnp.float32) * s, 'b_proj': jnp.zeros((C,), jnp.float32), 'w_gate': jax.random.normal(ks[5], (C, E), jnp.float32) * s, 'w1': jax.random.normal(ks[6], (E, C, H), jnp.float32) * s, 'b1': jnp.zeros((E, H), jnp.float32), 'w2': jax.random.normal(ks[7], (E, H, C), jnp.float32) * s, 'b2': jnp.zeros((E, C), jnp.float32)}
    _L3_cond_all = _L3_cond_setup()
    _L3_cond_in = {k: v for k, v in _L3_cond_all.items() if k in ('w_adaln', 'b_adaln', 'w_qkv', 'b_qkv', 'w_proj', 'b_proj', 'w_gate', 'w1', 'b1', 'w2', 'b2')}
    del _L3_cond_all
    return {'x': x, 'cond_1152': cond_1152, 'L0_cond_P': _L0_cond_in['P'], 'L0_cond_W': _L0_cond_in['W'], 'L0_cond_b': _L0_cond_in['b'], 'L1_cond_W_qkv': _L1_cond_in['W_qkv'], 'L1_cond_b_qkv': _L1_cond_in['b_qkv'], 'L1_cond_W_proj': _L1_cond_in['W_proj'], 'L1_cond_b_proj': _L1_cond_in['b_proj'], 'L1_cond_W_fc1': _L1_cond_in['W_fc1'], 'L1_cond_b_fc1': _L1_cond_in['b_fc1'], 'L1_cond_W_fc2': _L1_cond_in['W_fc2'], 'L1_cond_b_fc2': _L1_cond_in['b_fc2'], 'L1_cond_W_ada': _L1_cond_in['W_ada'], 'L1_cond_b_ada': _L1_cond_in['b_ada'], 'L2_cond_qkv_w': _L2_cond_in['qkv_w'], 'L2_cond_qkv_b': _L2_cond_in['qkv_b'], 'L2_cond_out_w': _L2_cond_in['out_w'], 'L2_cond_out_b': _L2_cond_in['out_b'], 'L2_cond_w1': _L2_cond_in['w1'], 'L2_cond_b1': _L2_cond_in['b1'], 'L2_cond_w2': _L2_cond_in['w2'], 'L2_cond_b2': _L2_cond_in['b2'], 'L2_cond_ada_w': _L2_cond_in['ada_w'], 'L2_cond_ada_b': _L2_cond_in['ada_b'], 'L3_cond_w_adaln': _L3_cond_in['w_adaln'], 'L3_cond_b_adaln': _L3_cond_in['b_adaln'], 'L3_cond_w_qkv': _L3_cond_in['w_qkv'], 'L3_cond_b_qkv': _L3_cond_in['b_qkv'], 'L3_cond_w_proj': _L3_cond_in['w_proj'], 'L3_cond_b_proj': _L3_cond_in['b_proj'], 'L3_cond_w_gate': _L3_cond_in['w_gate'], 'L3_cond_w1': _L3_cond_in['w1'], 'L3_cond_b1': _L3_cond_in['b1'], 'L3_cond_w2': _L3_cond_in['w2'], 'L3_cond_b2': _L3_cond_in['b2']}

def reference(x, cond_1152, L0_cond_P, L0_cond_W, L0_cond_b, L1_cond_W_qkv, L1_cond_b_qkv, L1_cond_W_proj, L1_cond_b_proj, L1_cond_W_fc1, L1_cond_b_fc1, L1_cond_W_fc2, L1_cond_b_fc2, L1_cond_W_ada, L1_cond_b_ada, L2_cond_qkv_w, L2_cond_qkv_b, L2_cond_out_w, L2_cond_out_b, L2_cond_w1, L2_cond_b1, L2_cond_w2, L2_cond_b2, L2_cond_ada_w, L2_cond_ada_b, L3_cond_w_adaln, L3_cond_b_adaln, L3_cond_w_qkv, L3_cond_b_qkv, L3_cond_w_proj, L3_cond_b_proj, L3_cond_w_gate, L3_cond_w1, L3_cond_b1, L3_cond_w2, L3_cond_b2):
    import jax
    import jax.numpy as jnp

    def _L0_cond_ref(x, cond, P, W, b):
        import jax, jax.numpy as jnp
        import numpy as np
        from jax.scipy.linalg import expm
        N, D, COND_DIM = (288, 64, 288)
        B, T = (16, 256)

        def _rotation(cond, W, b):
            v = jax.nn.silu(cond) @ W.T + b
            iu, ju = jnp.triu_indices(D, k=1)
            A = jnp.zeros((cond.shape[0], D, D), dtype=v.dtype)
            A = A.at[:, iu, ju].set(v).at[:, ju, iu].set(-v)
            return expm(A)
        U, _ = jnp.linalg.qr(P)
        R = _rotation(cond, W, b)
        z = jnp.einsum('btn,nd->btd', x, U)
        z_rot = jnp.einsum('btd,bde->bte', z, R)
        x_rot = x + jnp.einsum('btd,nd->btn', z_rot - z, U)
        return x_rot

    def _L1_cond_ref(x, c, W_qkv, b_qkv, W_proj, b_proj, W_fc1, b_fc1, W_fc2, b_fc2, W_ada, b_ada):
        import jax, jax.numpy as jnp
        import numpy as np
        B, L, C = (8, 256, 288)
        H = 16
        D = C // H
        FF = int(C * 4.0)
        EPS = 1e-06

        def _layernorm(x):
            mu = jnp.mean(x, axis=-1, keepdims=True)
            var = jnp.mean(jnp.square(x - mu), axis=-1, keepdims=True)
            return (x - mu) * jax.lax.rsqrt(var + EPS)

        def _modulate(x, shift, scale):
            return x * (1.0 + scale) + shift

        def _attention(h, W_qkv, b_qkv, W_proj, b_proj):
            b, l, c = h.shape
            qkv = h @ W_qkv + b_qkv
            qkv = qkv.reshape(b, l, 3, H, D)
            q, k, v = (qkv[:, :, 0], qkv[:, :, 1], qkv[:, :, 2])
            scale = D ** (-0.5)
            scores = jnp.einsum('blhd,bmhd->bhlm', q * scale, k)
            attn = jax.nn.softmax(scores, axis=-1)
            o = jnp.einsum('bhlm,bmhd->blhd', attn, v).reshape(b, l, c)
            return o @ W_proj + b_proj
        ada = jax.nn.silu(c) @ W_ada + b_ada
        shift_msa, scale_msa, gate_msa, shift_mlp, scale_mlp, gate_mlp = jnp.split(ada, 6, axis=-1)
        h = _modulate(_layernorm(x), shift_msa, scale_msa)
        x = x + gate_msa * _attention(h, W_qkv, b_qkv, W_proj, b_proj)
        h = _modulate(_layernorm(x), shift_mlp, scale_mlp)
        mlp = jax.nn.gelu(h @ W_fc1 + b_fc1, approximate=True) @ W_fc2 + b_fc2
        x = x + gate_mlp * mlp
        return x

    def _L2_cond_ref(x, c, qkv_w, qkv_b, out_w, out_b, w1, b1, w2, b2, ada_w, ada_b):
        import math
        import jax, jax.numpy as jnp
        import numpy as np
        B, T, D = (8, 256, 288)
        H = 16
        E = 4
        EPS = 1e-06

        def _layer_norm(x):
            mu = jnp.mean(x, axis=-1, keepdims=True)
            var = jnp.mean(jnp.square(x - mu), axis=-1, keepdims=True)
            return (x - mu) * jax.lax.rsqrt(var + EPS)

        def _modulate(x, shift, scale):
            return x * (1.0 + scale) + shift

        def _attention(y, qkv_w, qkv_b, out_w, out_b):
            b, t, d = y.shape
            hd = d // H
            qkv = y @ qkv_w + qkv_b
            q, k, v = jnp.split(qkv, 3, axis=-1)
            q = q.reshape(b, t, H, hd).transpose(0, 2, 1, 3)
            k = k.reshape(b, t, H, hd).transpose(0, 2, 1, 3)
            v = v.reshape(b, t, H, hd).transpose(0, 2, 1, 3)
            scores = jnp.einsum('bhqd,bhkd->bhqk', q, k) / math.sqrt(hd)
            attn = jax.nn.softmax(scores, axis=-1)
            out = jnp.einsum('bhqk,bhkd->bhqd', attn, v)
            out = out.transpose(0, 2, 1, 3).reshape(b, t, d)
            return out @ out_w + out_b
        mods = (jax.nn.silu(c) @ ada_w + ada_b)[:, None, :]
        m0, m1, m2, m3, m4, m5 = jnp.split(mods, 6, axis=-1)
        y = _modulate(_layer_norm(x), m0, m1)
        x = x + m2 * _attention(y, qkv_w, qkv_b, out_w, out_b)
        y = _modulate(_layer_norm(x), m3, m4)
        y = jax.nn.gelu(y @ w1 + b1, approximate=True)
        x = x + m5 * (y @ w2 + b2)
        return x

    def _L3_cond_ref(x, c, w_adaln, b_adaln, w_qkv, b_qkv, w_proj, b_proj, w_gate, w1, b1, w2, b2):
        import jax, jax.numpy as jnp
        import numpy as np
        NUM_HEADS = 16
        NUM_EXPERTS = 4
        TOP_K = 2
        LN_EPS = 1e-06

        def _ln(h):
            mu = jnp.mean(h, axis=-1, keepdims=True)
            var = jnp.var(h, axis=-1, keepdims=True)
            return (h - mu) * jax.lax.rsqrt(var + LN_EPS)

        def _modulate(h, shift, scale):
            return h * (1.0 + scale[:, None, :]) + shift[:, None, :]
        B, N, C = x.shape
        nh = NUM_HEADS
        hd = C // nh
        mod = jax.nn.silu(c) @ w_adaln + b_adaln
        sh_msa, sc_msa, g_msa, sh_mlp, sc_mlp, g_mlp = jnp.split(mod, 6, axis=-1)
        h = _modulate(_ln(x), sh_msa, sc_msa)
        qkv = (h @ w_qkv + b_qkv).reshape(B, N, 3, nh, hd).transpose(2, 0, 3, 1, 4)
        q, k, v = (qkv[0], qkv[1], qkv[2])
        attn = jax.nn.softmax(jnp.einsum('bhqd,bhkd->bhqk', q, k) * hd ** (-0.5), axis=-1)
        o = jnp.einsum('bhqk,bhkd->bhqd', attn, v).transpose(0, 2, 1, 3).reshape(B, N, C)
        o = o @ w_proj + b_proj
        x = x + g_msa[:, None, :] * o
        xn = _modulate(_ln(x), sh_mlp, sc_mlp)
        xf = xn.reshape(-1, C)
        gate_logits = xf @ w_gate
        topk_logits, topk_idx = jax.lax.top_k(gate_logits, TOP_K)
        gates = jax.nn.softmax(topk_logits, axis=-1)
        cw = jnp.sum(jax.nn.one_hot(topk_idx, NUM_EXPERTS, dtype=xf.dtype) * gates[..., None], axis=1)
        hmid = jax.nn.gelu(jnp.einsum('tc,ech->eth', xf, w1) + b1[:, None, :], approximate=True)
        eo = jnp.einsum('eth,ehc->etc', hmid, w2) + b2[:, None, :]
        moe = jnp.einsum('te,etc->tc', cw, eo).reshape(B, N, C)
        return x + g_mlp[:, None, :] * moe
    x = _L0_cond_ref(x, cond_1152, L0_cond_P, L0_cond_W, L0_cond_b)
    x = _L1_cond_ref(x, cond_1152[:, None, :], L1_cond_W_qkv, L1_cond_b_qkv, L1_cond_W_proj, L1_cond_b_proj, L1_cond_W_fc1, L1_cond_b_fc1, L1_cond_W_fc2, L1_cond_b_fc2, L1_cond_W_ada, L1_cond_b_ada)
    x = _L2_cond_ref(x, cond_1152, L2_cond_qkv_w, L2_cond_qkv_b, L2_cond_out_w, L2_cond_out_b, L2_cond_w1, L2_cond_b1, L2_cond_w2, L2_cond_b2, L2_cond_ada_w, L2_cond_ada_b)
    x = _L3_cond_ref(x, cond_1152, L3_cond_w_adaln, L3_cond_b_adaln, L3_cond_w_qkv, L3_cond_b_qkv, L3_cond_w_proj, L3_cond_b_proj, L3_cond_w_gate, L3_cond_w1, L3_cond_b1, L3_cond_w2, L3_cond_b2)
    return x

_drawn_inputs = setup_inputs


def setup_inputs(seed=0):
    import zlib

    import numpy as np

    out = dict(_drawn_inputs(seed))
    spreads = {'L1_cond_b_qkv': (0.0, 0.8),
     'L1_cond_b_proj': (0.0, 0.35),
     'L1_cond_b_fc1': (0.0, 0.8),
     'L1_cond_b_fc2': (0.0, 0.357),
     'L1_cond_b_ada': (0.0, 0.376),
     'L2_cond_qkv_b': (0.0, 0.8),
     'L2_cond_out_b': (0.0, 0.351),
     'L2_cond_b1': (0.0, 0.8),
     'L2_cond_b2': (0.0, 0.367),
     'L2_cond_ada_b': (0.0, 0.371),
     'L3_cond_b_adaln': (0.0, 0.454),
     'L3_cond_b_qkv': (0.0, 0.8),
     'L3_cond_b_proj': (0.0, 0.366),
     'L3_cond_b1': (0.0, 2.0),
     'L3_cond_b2': (0.0, 0.495)}
    factors = {'L1_cond_W_qkv': 8.0,
     'L1_cond_W_proj': 5.535,
     'L2_cond_qkv_w': 8.0,
     'L2_cond_out_w': 5.953,
     'L3_cond_w_qkv': 8.0,
     'L3_cond_w_proj': 5.726,
     'L3_cond_w_gate': 2.898,
     'L3_cond_w1': 2.781}
    for name, (base, spread) in spreads.items():
        noise = np.random.default_rng([zlib.crc32(name.encode()), seed]).standard_normal(out[name].shape)
        drawn = base * np.exp(spread * noise) if base else spread * noise
        out[name] = jnp.asarray(drawn.astype(out[name].dtype))
    for name, factor in factors.items():
        out[name] = (out[name] * factor).astype(out[name].dtype)
    return out
```

```python
from contextlib import ExitStack

import concourse.bass as bass
from concourse import mybir

F32 = mybir.dt.float32
F32R = mybir.dt.float32r
I32 = mybir.dt.int32
ALU = mybir.AluOpType
ACT = mybir.ActivationFunctionType
AX = mybir.AxisListType

B, T, C = 8, 256, 288
P = 128
KC = 96
KT = C // KC
H, HD, HP = 16, 18, 32
G = H * HP // P
HJ = P // HP
LT = T // P
F = 4 * C
FT = F // P
E = 4
LAYERS = 3
D = 64
NSK = D * (D - 1) // 2
CB = 2
CHUNKS = B // CB
CT = CB * LT
CN = CB * T
LN_EPS = 1e-6
SCALE = float(HD) ** -0.5
ONE = HD
WTILE, WROWS = 16, NSK // 16
TAYLOR = 14
EXP_NORM = 2.0
SQUARINGS = 17
RSQRT_SEED = 1597463007.0
MODS = 6 * C
SCRATCH_E = FT * C + KT * F


def build(nc, a):
    ctx = ExitStack()
    with ctx:
        def sb(name, shape, dt=F32):
            return ctx.enter_context(nc.sbuf_tensor(name, shape, dt))

        def sem(name):
            return ctx.enter_context(nc.semaphore(name))

        x_sb = sb("x_sb", [P, (B + CB) * LT, C])
        wexp = sb("wexp", [P, E * SCRATCH_E])
        wq = sb("wq", [KC, KT, H, HP])
        wk = sb("wk", [KC, KT, H, HP])
        wv = sb("wv", [KC + 1, KT, C])
        wp = sb("wp", [KC + 1, KT, C])
        work = sb("work", [P, FT * CN])
        q_r = sb("q_r", [P, G, T], F32R)
        k_r = sb("k_r", [P, G, T], F32R)
        v_sb = sb("v_sb", [P, LT, H, HP])
        nmax = sb("nmax", [P, LT, H, HP])
        o_pad = sb("o_pad", [P, G, T])
        o_tok = sb("o_tok", [P, LT, C])
        o_t = sb("o_t", [KC + 1, KT, T])
        xn = sb("xn", [P, CT, C])
        h_t = sb("h_t", [KC + 1, KT, CN])
        acc = sb("acc", [P, CT, C])
        gate = sb("gate", [P, CB, C])
        upd = sb("upd", [P, C])
        ident = sb("ident", [P, P])
        mod_t = sb("mod_t", [KC, LAYERS, 4, KT, B + CB])
        bqk = sb("bqk", [P, 2, G])
        kone = sb("kone", [P, 1])
        b1_sb = sb("b1_sb", [P, E, FT])
        b2_sb = sb("b2_sb", [1, E, C])
        ones = sb("ones", [1, P])
        wg_sb = sb("wg_sb", [KC, KT, E])
        ln = sb("ln", [P, 12, CT])
        st = sb("st", [P, CT, 6])
        rcp = sb("rcp", [P, LT, H])
        gm = sb("gm", [P, 12, CT, E])
        cmp_ = sb("cmp", [P, CT, E, E])
        s_t = sb("s_t", [KC, KT, B])
        sc_small = sb("sc_small", [D, 24])

        lg4 = o_pad[0:E, 0:2, :].rearrange("p g t -> p (g t)")
        q_t = work[:, 0:G * T].rearrange("p (g t) -> p g t", g=G)
        k_t = work[:, G * T:2 * G * T].rearrange("p (g t) -> p g t", g=G)
        p_t = work[:, 2 * G * T:2 * G * T + HJ * LT * T].rearrange("p (r m t) -> p r m t", r=HJ, m=LT)
        mid = work[:, :].rearrange("p (f n) -> p f n", f=FT)
        w1_sb = [wexp[0:KC, e * SCRATCH_E:e * SCRATCH_E + KT * F].rearrange("p (k f) -> p k f", k=KT) for e in range(E)]
        w2_sb = [wexp[:, e * SCRATCH_E + KT * F:(e + 1) * SCRATCH_E].rearrange("p (f c) -> p f c", f=FT) for e in range(E)]

        pos = [SCRATCH_E]

        def early(parts, n):
            v = wexp[0:parts, pos[0]:pos[0] + n]
            pos[0] += n
            assert pos[0] <= E * SCRATCH_E
            return v

        w0_nat = early(WROWS, WTILE * C).rearrange("p (t c) -> p t c", t=WTILE)
        w0_t = early(KC, KT * NSK).rearrange("p (k n) -> p k n", k=KT)
        ada_w = early(KC, KT * MODS).rearrange("p (k n) -> p k n", k=KT)
        bias_b = early(B, NSK)
        v0 = w0_nat[0:B, 0:NSK // C, :].rearrange("p t c -> p (t c)")

        def early2(parts, n, at=[0]):
            v = work[0:parts, at[0]:at[0] + n]
            at[0] += n
            return v

        def square8(v):
            return v.rearrange("p a c -> p (a c)")[:, 0:B * D]

        cond_sb = early2(B, C)
        silu_sb = early2(B, C)
        mods_sb = early2(B, MODS)
        at_q = early2(D, C)
        p_nat = early2(KC, KT * D).rearrange("p (k d) -> p k d", k=KT)
        v_nat = early2(KC, KT * D).rearrange("p (k d) -> p k d", k=KT)
        u_nat = early2(KC, KT * D).rearrange("p (k d) -> p k d", k=KT)
        u_t = early2(D, C)
        vt_q = early2(D, C)
        aup = square8(xn[0:D, 0:2, :])
        ant = square8(xn[0:D, 2:4, :])
        ex = square8(acc[0:D, 0:2, :])
        ex_t = square8(acc[0:D, 2:4, :])
        ident8 = o_pad[0:D, 0:2, :].rearrange("p g t -> p (g t)")
        smask = o_pad[0:D, 2, 0:D]
        nsm = o_tok[0:D, :, :].rearrange("p l c -> p (l c)")
        nn, nnt, pmt, tv1, nscr, vd1 = [nsm[:, i * D:(i + 1) * D] for i in range(6)]
        sq_junk = h_t[0:D, 0, 0:C]
        dot_junk = h_t[0:D, 1, 0:C]
        z_sb = h_t[0:D, 0, T:2 * T]
        zr_sb = h_t[0:D, 1, T:2 * T]
        rmi = h_t[0:D, 2, T:T + P]
        q_small = [sc_small[:, i:i + 1] for i in range(24)]
        (esel, piv, rcol, sdot, sn, y0, sgn2, ry, nb2, nbeta, dd, tau, uu, ww, nbv, tauv, kcol, krec, dg, rd) = q_small[:20]
        e_small = gm[0:D, :, :, :].rearrange("p a b c -> p (a b c)")
        nrow, cur, cur2, esc, eflag = [e_small[:, i * B:(i + 1) * B] for i in range(5)]
        nmx8 = e_small[0:B, 40:41]
        nrep = e_small[0:B, 48:48 + D]
        emask = ctx.enter_context(nc.sbuf_tensor("emask", [D, B], I32))

        ps = ctx.enter_context(nc.psum_tensor("ps", [P, 8, 512], F32))

        mods_d = nc.dram_tensor("mods_scratch", (LAYERS, B, MODS), F32).ap()


        def hps(unit_k):
            return ps[0:KC, unit_k // 2, (unit_k % 2) * T:(unit_k % 2 + 1) * T]

        names = """l_x l_p l_w0 l_b0 l_cond l_aw l_ab l_aup l_attnw l_bqk l_mlpw0 l_mlpw1 l_mlpw2 l_mlpw3 l_mlpw4 l_mlpw5 l_gate l_mods l_out l_wg
            m_tanh c_ident c_init c_fix d_chain
            e_silu e_sT e_sTo e_wT e_wTo e_v e_vo e_mod e_modo e_modT e_modTo
            q_pT q_va q_vb q_sq q_at q_vT q_vTo q_g q_no q_n q_u q_uo q_rt q_rtd
            x_up x_ant x_nr x_nro x_h x_ho x_rT x_sq x_sqo
            z_in z_xT z_xTo z_z z_zo z_zr z_zro z_d z_x
            n_xn n_T n_h
            t_q t_k t_qe t_v t_ve t_mx t_mxd t_nm t_nma t_s t_exp t_pv t_pve t_o t_on t_oT t_oTe t_pr t_xd
            m_f1 m_gelu m_f2 m_upd m_lg m_lge m_lt m_cw""".split()
        s = {n: sem(n) for n in names}
        N_INIT = 12

        block = ctx.enter_context(nc.Block())

        L = [dict(ada="L1_cond_W_ada", adab="L1_cond_b_ada", qkv="L1_cond_W_qkv", qkvb="L1_cond_b_qkv",
                  proj="L1_cond_W_proj", projb="L1_cond_b_proj", w1="L1_cond_W_fc1", b1="L1_cond_b_fc1",
                  w2="L1_cond_W_fc2", b2="L1_cond_b_fc2"),
             dict(ada="L2_cond_ada_w", adab="L2_cond_ada_b", qkv="L2_cond_qkv_w", qkvb="L2_cond_qkv_b",
                  proj="L2_cond_out_w", projb="L2_cond_out_b", w1="L2_cond_w1", b1="L2_cond_b1",
                  w2="L2_cond_w2", b2="L2_cond_b2"),
             dict(ada="L3_cond_w_adaln", adab="L3_cond_b_adaln", qkv="L3_cond_w_qkv", qkvb="L3_cond_b_qkv",
                  proj="L3_cond_w_proj", projb="L3_cond_b_proj", w1="L3_cond_w1", b1="L3_cond_b1",
                  w2="L3_cond_w2", b2="L3_cond_b2")]
        experts = [[0], [1], [0, 1, 2, 3]]
        passes = [CHUNKS * sum(len(experts[i]) for i in range(l)) for l in range(LAYERS + 1)]
        units_a = [l * ((B + 1) + CB * (CHUNKS + 1)) for l in range(LAYERS)]
        units_m = [u + B + 1 for u in units_a]
        ATTN_DMAS = 2 * KT + 4
        MLP_DMAS = 4
        order_mlp = [(0, 0, 0), (1, 0, 1), (2, 2, 2), (2, 3, 3), (2, 0, 0), (2, 1, 1)]

        @block.sync
        def _(sp):
            sp.dma_start(cond_sb, a["cond_1152"]).then_inc(s["l_cond"], 16)
            sp.dma_start(p_nat, a["L0_cond_P"].rearrange("(k p) d -> p k d", p=KC)).then_inc(s["l_p"], 16)
            sp.dma_start(w0_nat, a["L0_cond_W"].rearrange("(t p) c -> p t c", p=WROWS)).then_inc(s["l_w0"], 16)
            sp.dma_start(bias_b, a["L0_cond_b"].partition_broadcast(B)).then_inc(s["l_b0"], 16)
            sp.dma_start(ada_w, a[L[0]["ada"]].rearrange("(k p) n -> p k n", p=KC)).then_inc(s["l_aw"], 16)
            sp.dma_start(x_sb[:, 0:B * LT, :], a["x"].rearrange("b (l p) c -> p (b l) c", p=P)).then_inc(s["l_x"], 16)

            def attention_weights(l):
                qkv = a[L[l]["qkv"]]
                for k in range(KT):
                    for which, w in ((0, wq), (1, wk)):
                        sp.dma_start(w[:, k, :, 0:HD],
                                     qkv[k * KC:(k + 1) * KC, which * C:(which + 1) * C].rearrange("p (h d) -> p h d", d=HD)
                                     ).then_inc(s["l_attnw"], 16)
                sp.dma_start(wv[0:KC, :, :], qkv[:, 2 * C:3 * C].rearrange("(k p) n -> p k n", p=KC)).then_inc(s["l_attnw"], 16)
                sp.dma_start(wv[KC:KC + 1, KT - 1, :], a[L[l]["qkvb"]][2 * C:3 * C].rearrange("(o n) -> o n", o=1)
                             ).then_inc(s["l_attnw"], 16)
                sp.dma_start(wp[0:KC, :, :], a[L[l]["proj"]].rearrange("(k p) n -> p k n", p=KC)).then_inc(s["l_attnw"], 16)
                sp.dma_start(wp[KC:KC + 1, KT - 1, :], a[L[l]["projb"]].rearrange("(o n) -> o n", o=1)
                             ).then_inc(s["l_attnw"], 16)
                for j in range(HJ):
                    for which in range(2):
                        src = a[L[l]["qkvb"]][which * C:(which + 1) * C].rearrange("(g j d) -> j d g", g=G, j=HJ)[j]
                        sp.dma_start(bqk[j * HP:j * HP + HD, which, :], src, allow_slow_non_contiguous=True
                                     ).then_inc(s["l_bqk"], 16)

            def mlp_weights(n):
                l, e, buf = order_mlp[n]
                w1, w2, b1, b2 = (a[L[l][n]] for n in ("w1", "w2", "b1", "b2"))
                if l == 2:
                    w1, w2, b1, b2 = w1[e], w2[e], b1[e], b2[e]
                sp.dma_start(w1_sb[buf], w1.rearrange("(k p) f -> p k f", p=KC)).then_inc(s[f"l_mlpw{n}"], 16)
                sp.dma_start(w2_sb[buf], w2.rearrange("(f p) c -> p f c", p=P)).then_inc(s[f"l_mlpw{n}"], 16)
                sp.dma_start(b1_sb[:, buf, :], b1.rearrange("(f p) -> p f", p=P), allow_slow_non_contiguous=True
                             ).then_inc(s[f"l_mlpw{n}"], 16)
                sp.dma_start(b2_sb[:, buf, :], b2.rearrange("(o n) -> o n", o=1)).then_inc(s[f"l_mlpw{n}"], 16)

            sp.wait_ge(s["c_init"], N_INIT)
            sp.wait_ge(s["c_fix"], 2)
            attention_weights(0)
            mlp_weights(0)
            sp.dma_start(wg_sb[:], a["L3_cond_w_gate"].rearrange("(k p) e -> p k e", p=KC)).then_inc(s["l_wg"], 16)

            sp.wait_ge(s["e_vo"], 4)
            at = 0
            for i in range(D - 1):
                n = D - 1 - i
                sp.dma_start(aup[i:i + 1, :].rearrange("p (b d) -> p b d", b=B)[:, :, i + 1:D], v0[:, at:at + n],
                             allow_slow_non_contiguous=True).then_inc(s["l_aup"], 16)
                at += n

            for l in range(LAYERS):
                if l:
                    sp.wait_ge(s["e_mod"], 4 * l)
                    sp.dma_start(ada_w, a[L[l]["ada"]].rearrange("(k p) n -> p k n", p=KC)).then_inc(s["l_aw"], 16)
                    sp.wait_ge(s["e_modo"], 4 * l)
                sp.dma_start(bias_b[:, 0:MODS], a[L[l]["adab"]].partition_broadcast(B)).then_inc(s["l_ab"], 16)
                sp.wait_ge(s["e_modo"], 4 * (l + 1))
                sp.dma_start(mods_d[l], mods_sb).then_inc(s["l_mods"], 16)
            sp.wait_ge(s["l_mods"], 16 * LAYERS)
            sp.wait_ge(s["z_d"], LT * B)
            for n in (1, 2, 3):
                mlp_weights(n)

            for l in range(LAYERS):
                with sp.Fori(0, B) as b:
                    sp.wait_ge(s["t_xd"], (b + l * B) * LT + 1)
                    if l:
                        sp.wait_ge(s["m_upd"], passes[l] * CT + 2)
                    sp.dma_start(gate[:, 0, :], mods_d[l, b, 2 * C:3 * C].partition_broadcast(P)).then_inc(s["l_gate"], 16)
                sp.wait_ge(s["t_xd"], (l + 1) * B * LT + 1)
                if l + 1 < LAYERS:
                    attention_weights(l + 1)
                ne = len(experts[l])
                with sp.Fori(0, CHUNKS) as c:
                    if l < 2:
                        sp.wait_ge(s["m_upd"], (c * ne + passes[l]) * CT + 2)
                    else:
                        sp.wait_ge(s["z_x"], c * CT + B * LT)
                    for i in range(CB):
                        sp.dma_start(gate[:, i, :], mods_d[l, c * CB + i, 5 * C:6 * C].partition_broadcast(P)
                                     ).then_inc(s["l_gate"], 16)
                sp.wait_ge(s["m_upd"], passes[l + 1] * CT + 2)
                if l + 1 < LAYERS:
                    mlp_weights(4 + l)
            sp.wait_ge(s["z_x"], 2 * B * LT)
            sp.dma_start(a["out"].rearrange("b (l p) c -> p (b l) c", p=P), x_sb[:, 0:B * LT, :]).then_inc(s["l_out"], 16)
            sp.wait_ge(s["l_out"], 16)

        mlp_loads = [[0], [1], [2, 3, 4, 5]]

        @block.gpsimd
        def _(pool):
            pool.memset(ident[:], 0.0).then_inc(s["c_ident"], 1)
            pool.memset(smask, 1.0).then_inc(s["c_ident"], 1)
            pool.wait_ge(s["c_ident"], 2)
            pool.affine_select(out=ident[:], in_=ident[:], compare_op=ALU.not_equal, fill=1.0, base=0,
                               pattern=[[-1, P]], channel_multiplier=1).then_inc(s["c_init"], 1)
            pool.affine_select(out=smask, in_=smask, compare_op=ALU.is_gt, fill=0.0, base=0,
                               pattern=[[1, D]], channel_multiplier=-1).then_inc(s["c_init"], 1)
            pool.memset(x_sb[:, B * LT:, :], 0.0).then_inc(s["c_init"], 1)
            pool.memset(wq[:], 0.0).then_inc(s["c_init"], 1)
            pool.memset(wk[:], 0.0).then_inc(s["c_init"], 1)
            pool.memset(v_sb[:], 0.0).then_inc(s["c_init"], 1)
            pool.memset(nmax[:], 0.0).then_inc(s["c_init"], 1)
            pool.memset(bqk[:], 0.0).then_inc(s["c_init"], 1)
            pool.memset(aup, 0.0).then_inc(s["c_init"], 1)
            pool.memset(vt_q, 0.0).then_inc(s["c_init"], 1)
            pool.memset(mod_t[:], 0.0).then_inc(s["c_init"], 1)
            pool.memset(sc_small[:], 0.0).then_inc(s["c_init"], 1)

        @block.scalar
        def _(act):
            act.wait_ge(s["c_init"], N_INIT)
            act.wait_ge(s["l_cond"], 16)
            act.activation(silu_sb, cond_sb, ACT.Silu).then_inc(s["e_silu"], 1)
            for n in range(12):
                act.wait_ge(s["e_wT"], n + 1)
                act.activation(w0_t[:, n // 4, (n % 4) * 4 * WROWS:(n % 4 + 1) * 4 * WROWS],
                               ps[0:KC, 1 + n % 4, 0:4 * WROWS], ACT.Copy).then_inc(s["e_wTo"], 1)
            with act.Fori(0, D // 2) as m:
                for half in range(2):
                    j = m * 2 + half
                    act.wait_ge(s["q_va"], j + 1)
                    act.activation(sq_junk, ps[0:D, 2 + half, 0:C], ACT.Square, accum_out=sn).then_inc(s["q_sq"], 1)
                    act.wait_ge(s["q_sq"], j * 2 + 1)
                    act.activation(y0, sn, ACT.Sqrt).then_inc(s["q_sq"], 1)
            act.wait_ge(s["q_rt"], 1)
            act.activation(tauv, tauv, ACT.Sqrt).then_inc(s["q_rtd"], 1)
            with act.Fori(0, B) as b:
                act.wait_ge(s["z_xT"], b + 1)
                for k in range(KT):
                    last = act.activation(h_t[0:KC, k, 0:T], hps(k), ACT.Copy)
                last.then_inc(s["z_xTo"], 1)
                act.wait_ge(s["z_z"], b + 1)
                act.activation(z_sb, ps[0:D, 2, 0:T], ACT.Copy).then_inc(s["z_zo"], 1)
                act.wait_ge(s["z_zr"], b + 1)
                act.activation(zr_sb, ps[0:D, 3, 0:T], ACT.Copy).then_inc(s["z_zro"], 1)

            def modulate(l, phase, unit, idx, cb):
                act.wait_ge(s["n_T"], unit + 1)
                for k in range(KT):
                    last = act.activation(h_t[0:KC, k, cb * T:(cb + 1) * T], hps(k), ACT.Identity,
                                          bias=mod_t[:, l, 2 * phase, k, bass.ds(idx, 1)],
                                          scale=mod_t[:, l, 2 * phase + 1, k, bass.ds(idx, 1)])
                last.then_inc(s["n_h"], 1)

            for l in range(LAYERS):
                if l == 0:
                    act.wait_ge(s["e_modTo"], 2 * LAYERS)
                    act.wait_ge(s["l_mods"], 16 * LAYERS)
                act.wait_ge(s["l_bqk"], 16 * 2 * HJ * (l + 1))
                modulate(l, 0, units_a[l], 0, 0)
                with act.Fori(0, B) as b:
                    t = b + l * B
                    for which, tile, rounded, done in ((0, q_t, q_r[:], "t_q"), (1, k_t, k_r[:], "t_k")):
                        for g in range(G):
                            if g % 2 == 0:
                                act.wait_ge(s[done], t * 2 + g // 2 + 1)
                            for to in (rounded, tile):
                                last = act.activation(to[:, g, :], ps[:, 2 + 2 * which + g // 2, (g % 2) * T:(g % 2 + 1) * T],
                                                      ACT.Identity, bias=bqk[:, which, g:g + 1], scale=1.0)
                        last.then_inc(s["t_qe"], 1)
                    for lt in range(LT):
                        act.wait_ge(s["t_v"], t * LT + lt + 1)
                        act.activation(v_sb[:, lt, :, 0:HD], ps[:, 6 + lt, 0:C].rearrange("p (h d) -> p h d", h=H), ACT.Copy
                                       ).then_inc(s["t_ve"], 1)
                    modulate(l, 0, b + units_a[l] + 1, b + 1, 0)
                    for h in range(H):
                        act.wait_ge(s["t_s"], t * H + h + 1)
                        if h >= HJ:
                            act.wait_ge(s["t_pv"], t * H + h - HJ + 1)
                        act.activation(p_t[:, h % HJ, :, :], ps[:, 2 + h % HJ, :].rearrange("p (m t) -> p m t", m=LT),
                                       ACT.Exp, scale=SCALE).then_inc(s["t_exp"], 1)
                        if h == H // 2 + 3:
                            act.wait_ge(s["t_pv"], t * H + H // 2)
                            act.activation(o_pad[:, 0:2, :].rearrange("p g t -> p (g t)"), ps[:, 6, :], ACT.Copy
                                           ).then_inc(s["t_pve"], 1)
                    act.wait_ge(s["t_pv"], t * H + H)
                    act.activation(o_pad[:, 2:4, :].rearrange("p g t -> p (g t)"), ps[:, 7, :], ACT.Copy
                                   ).then_inc(s["t_pve"], 1)
                    for i in range(2):
                        act.wait_ge(s["t_oT"], t * 2 + i + 1)
                        for k in ((0, 1), (2,))[i]:
                            last = act.activation(o_t[0:KC, k, :], ps[0:KC, 4 + i, (k % 2) * T:(k % 2 + 1) * T], ACT.Copy)
                        last.then_inc(s["t_oTe"], 1)
                ne = len(experts[l])
                for n in mlp_loads[l]:
                    act.wait_ge(s[f"l_mlpw{n}"], 16 * MLP_DMAS)
                for i in range(CB):
                    modulate(l, 1, units_m[l] + i, i, i)
                with act.Fori(0, CHUNKS) as c:
                    if l == 2:
                        act.wait_ge(s["m_lg"], c + 1)
                        act.activation(lg4, ps[0:E, 7, :], ACT.Copy).then_inc(s["m_lge"], 1)
                        act.wait_ge(s["m_cw"], c + 1)
                        act.activation(gm[:, 5, :, 0], gm[:, 4, :, 0], ACT.Tanh, scale=0.5).then_inc(s["m_tanh"], 1)
                    for ei, e in enumerate(experts[l]):
                        n = c * ne + passes[l] + ei
                        for m in range(FT):
                            act.wait_ge(s["m_f1"], n * FT + m + 1)
                            act.activation(mid[:, m, :], ps[:, 2 + m % 3, :], ACT.Gelu_apprx_tanh,
                                           bias=b1_sb[:, e, m:m + 1], scale=1.0).then_inc(s["m_gelu"], 1)
                    for i in range(CB):
                        modulate(l, 1, c * CB + units_m[l] + CB + i, c * CB + CB + i, i)

        @block.vector
        def _(dve):
            V = nc.vector
            chain = {"base": 0, "n": 0}

            def link(ins):
                chain["n"] += 1
                ins.then_inc(s["d_chain"], 1)
                dve.wait_ge(s["d_chain"], chain["base"] + chain["n"])

            class Turns:
                def __init__(self, n, per):
                    self.n, self.per = n, per

                def __enter__(self):
                    self.start = chain["base"] + chain["n"]
                    self.loop = dve.Fori(0, self.n)
                    i = self.loop.__enter__()
                    chain["base"], chain["n"] = i * self.per + self.start, 0
                    return i

                def __exit__(self, *e):
                    if e[0] is None:
                        assert chain["n"] == self.per, (chain["n"], self.per)
                    r = self.loop.__exit__(*e)
                    chain["base"], chain["n"] = self.start + self.n * self.per, 0
                    return r

            dve.wait_ge(s["c_init"], N_INIT)
            V.memset(v_sb[:, :, :, HD:HD + 1], 1.0).then_inc(s["c_fix"], 1)
            link(V.tensor_reduce(kone[:], ident[:, ONE::HP], AX.X, ALU.add))
            V.tensor_scalar(bqk[:, 1, :], bqk[:, 1, :], kone[:, 0:1], None, ALU.add).then_inc(s["c_fix"], 1)
            V.memset(o_t[KC:KC + 1, :, :], 1.0).then_inc(s["c_fix"], 1)
            V.memset(h_t[KC:KC + 1, :, :], 1.0).then_inc(s["c_fix"], 1)
            V.memset(ones[:], 1.0).then_inc(s["c_fix"], 1)
            V.memset(cmp_[:], 0.0).then_inc(s["c_fix"], 1)
            for b in range(B):
                last = V.tensor_copy(ident8[:, b * D:(b + 1) * D], ident[0:D, 0:D])
            last.then_inc(s["c_fix"], 1)
            dve.sem_inc(s["t_xd"], 1)
            dve.sem_inc(s["m_upd"], 2)

            dve.wait_ge(s["e_sT"], 1)
            V.tensor_copy(s_t[:], ps[0:KC, 0, 0:KT * B].rearrange("p (k b) -> p k b", k=KT)).then_inc(s["e_sTo"], 1)
            dve.wait_ge(s["l_b0"], 16)
            for q in range(4):
                dve.wait_ge(s["e_v"], q + 1)
                V.tensor_tensor(v0[:, q * 504:(q + 1) * 504], ps[0:B, 1 + q, 0:504], bias_b[:, q * 504:(q + 1) * 504],
                                ALU.add).then_inc(s["e_vo"], 1)

            def ada(l):
                dve.wait_ge(s["l_ab"], 16 * (l + 1))
                if l:
                    dve.wait_ge(s["l_mods"], 16 * l)
                for q in range(4):
                    dve.wait_ge(s["e_mod"], 4 * l + q + 1)
                    V.tensor_tensor(mods_sb[:, q * 432:(q + 1) * 432], ps[0:B, 1 + q, 0:432],
                                    bias_b[:, q * 432:(q + 1) * 432], ALU.add).then_inc(s["e_modo"], 1)
                dve.wait_ge(s["e_modT"], l + 1)
                mp = ps[0:KC, 5, 0:4 * KT * B].rearrange("p (a k b) -> p a k b", a=4, k=KT)
                for a_ in range(4):
                    last = V.tensor_scalar(mod_t[:, l, a_, :, 0:B], mp[:, a_, :, :], float(a_ % 2), None, ALU.add)
                    if a_ % 2:
                        last.then_inc(s["e_modTo"], 1)

            ada(0)

            dve.wait_ge(s["q_pT"], 1)
            V.tensor_copy(at_q, ps[0:D, 0, 0:C]).then_inc(s["q_at"], 1)
            V.tensor_copy(esel, ident[0:D, 0:1]).then_inc(s["q_at"], 1)
            with Turns(D // 2, 2 * 16) as m:
                for half in range(2):
                    j = m * 2 + half
                    vb = ps[0:D, 6 + half, 0:C]
                    pj = bass.ds(j, 1)
                    dve.wait_ge(s["q_vb"], j + 1)
                    link(V.tensor_copy(piv, ps[0:D, 6 + half, pj]))
                    link(V.tensor_copy(rcol, at_q[:, pj]))
                    link(V.tensor_tensor_reduce(dot_junk, vb, at_q, 1.0, 0.0, ALU.mult, ALU.add, sdot))
                    link(V.tensor_scalar(sgn2, piv, 0.0, 2.0, ALU.is_ge, ALU.mult))
                    dve.wait_ge(s["q_sq"], j * 2 + 2)
                    link(V.tensor_scalar(y0, y0, 1e-18, None, ALU.max))
                    link(V.reciprocal(ry, y0))
                    link(V.scalar_tensor_tensor(nb2, sn, ry, y0, ALU.mult, ALU.add))
                    link(V.scalar_tensor_tensor(nb2, sgn2, -1.0, nb2, ALU.add, ALU.mult))
                    link(V.tensor_scalar(nbeta, nb2, 0.5, None, ALU.mult))
                    link(V.scalar_tensor_tensor(dd, piv, nbeta, sn, ALU.mult, ALU.add))
                    link(V.tensor_scalar(dd, dd, 1e-36, None, ALU.max))
                    link(V.reciprocal(tau, dd))
                    link(V.tensor_copy(esel, ident[0:D, bass.ds(j + 1, 1)]))
                    link(V.scalar_tensor_tensor(uu, rcol, nbeta, sdot, ALU.mult, ALU.add))
                    link(V.tensor_scalar(ww, uu, tau, -1.0, ALU.mult, ALU.mult))
                    V.scalar_tensor_tensor(at_q, vb, ww, at_q, ALU.mult, ALU.add).then_inc(s["q_at"], 1)
                    dve.wait_ge(s["q_at"], j * 2 + 3)
                    V.tensor_scalar(at_q[:, pj], at_q[:, pj], 0.0, None, ALU.mult).then_inc(s["q_at"], 1)
                    V.scalar_tensor_tensor(vt_q, vb, ident[0:D, pj], vt_q, ALU.mult, ALU.add)
                    V.scalar_tensor_tensor(nbv, nbeta, ident[0:D, pj], nbv, ALU.mult, ALU.add)
                    link(V.scalar_tensor_tensor(tauv, tau, ident[0:D, pj], tauv, ALU.mult, ALU.add))
            link(V.scalar_tensor_tensor(vt_q[:, 0:D], ident[0:D, 0:D], nbv, vt_q[:, 0:D], ALU.mult, ALU.add))
            V.tensor_copy(kcol, ident[0:D, 64:65]).then_inc(s["q_rt"], 1)
            dve.wait_ge(s["q_rtd"], 1)
            V.tensor_scalar(vt_q, vt_q, tauv, None, ALU.mult).then_inc(s["q_vTo"], 1)
            dve.wait_ge(s["q_vT"], 1)
            V.tensor_copy(v_nat, ps[0:KC, 0, 0:KT * D].rearrange("p (k d) -> p k d", k=KT)).then_inc(s["q_vTo"], 1)
            dve.wait_ge(s["q_g"], 1)
            gq = ps[0:D, 1, 0:D]
            link(V.tensor_tensor(nscr, gq, ident[0:D, 0:D], ALU.mult))
            link(V.tensor_reduce(dg, nscr, AX.X, ALU.add))
            link(V.tensor_scalar(dg, dg, 0.5, None, ALU.mult))
            link(V.reciprocal(rd, dg))
            link(V.scalar_tensor_tensor(nn, gq, rd, smask, ALU.mult, ALU.mult))
            V.tensor_scalar(vd1, vt_q[:, 0:D], rd, None, ALU.mult).then_inc(s["q_no"], 1)
            dve.wait_ge(s["q_n"], 1)
            link(V.tensor_copy(nnt, ps[0:D, 1, 0:D]))
            V.tensor_tensor(pmt, ident[0:D, 0:D], nnt, ALU.subtract).then_inc(s["q_no"], 1)
            for r in range(5):
                dve.wait_ge(s["q_n"], 2 + 2 * r)
                V.tensor_copy(nsm[:, 0:2 * D], ps[0:D, 1, 0:2 * D]).then_inc(s["q_no"], 1)
                dve.wait_ge(s["q_n"], 3 + 2 * r)
                V.tensor_tensor(pmt, ps[0:D, 2, 0:D], pmt, ALU.add).then_inc(s["q_no"], 1)
            dve.wait_ge(s["q_u"], 1)
            V.tensor_copy(tv1, ps[0:D, 1, 0:D]).then_inc(s["q_uo"], 1)
            dve.wait_ge(s["q_u"], 2)
            link(V.tensor_scalar(u_t, ps[0:D, 2, 0:C], -1.0, None, ALU.mult))
            V.tensor_tensor(u_t[:, 0:D], u_t[:, 0:D], ident[0:D, 0:D], ALU.add).then_inc(s["q_uo"], 1)
            dve.wait_ge(s["q_u"], 3)
            V.tensor_copy(u_nat, ps[0:KC, 0, 0:KT * D].rearrange("p (k d) -> p k d", k=KT)).then_inc(s["q_uo"], 1)

            ada(1)

            dve.wait_ge(s["l_aup"], 16 * (D - 1))
            dve.wait_ge(s["x_up"], 1)
            link(V.tensor_tensor(ant, ps[0:D, 3, :], aup, ALU.subtract))
            V.tensor_reduce(nrow, ant.rearrange("p (b d) -> p b d", b=B), AX.X, ALU.add, apply_absolute_value=True
                            ).then_inc(s["x_ant"], 1)
            dve.wait_ge(s["x_nr"], 1)
            link(V.tensor_reduce(nmx8, ps[0:B, 4, 0:D], AX.X, ALU.max))
            V.tensor_scalar(nrep, silu_sb[:, 0:D], 0.0, nmx8, ALU.mult, ALU.add).then_inc(s["x_ant"], 1)
            dve.wait_ge(s["x_nr"], 2)
            link(V.tensor_copy(cur, ps[0:D, 4, 0:B]))
            link(V.tensor_copy(cur2, cur))
            link(V.tensor_scalar(esc, cur, 0.0, 1.0, ALU.mult, ALU.add))
            with Turns(SQUARINGS, 3):
                link(V.tensor_scalar(eflag, cur, EXP_NORM, -0.5, ALU.is_gt, ALU.mult))
                link(V.scalar_tensor_tensor(cur, eflag, 1.0, cur, ALU.add, ALU.mult))
                link(V.scalar_tensor_tensor(esc, eflag, 1.0, esc, ALU.add, ALU.mult))
            for b in range(B):
                last = V.tensor_scalar(ant[:, b * D:(b + 1) * D], ant[:, b * D:(b + 1) * D], esc[:, b:b + 1], None, ALU.mult)
            link(last)
            link(V.memset(kcol, float(TAYLOR)))
            V.tensor_copy(ex, ident8).then_inc(s["x_ho"], 1)
            with Turns(TAYLOR, 2) as i:
                dve.wait_ge(s["x_ho"], i + 1)
                link(V.reciprocal(krec, kcol))
                link(V.tensor_scalar(kcol, kcol, -1.0, None, ALU.add))
                dve.wait_ge(s["x_h"], i + 1)
                V.scalar_tensor_tensor(ex, ps[0:D, 3, :], krec, ident8, ALU.mult, ALU.add).then_inc(s["x_ho"], 1)
            dve.wait_ge(s["x_rT"], 1)
            V.tensor_copy(ex_t, ps[0:D, 4, :]).then_inc(s["x_sqo"], 1)
            with Turns(SQUARINGS, 2) as i:
                dve.wait_ge(s["x_sqo"], i + 1)
                link(V.tensor_scalar(emask[:], cur2, EXP_NORM, None, ALU.is_gt))
                dve.wait_ge(s["x_sq"], i + 1)
                halved = V.tensor_scalar(cur2, cur2, 0.5, None, ALU.mult)
                mask = emask[:].unsqueeze(2).broadcast_to((D, B, D))
                V.copy_predicated(ex.rearrange("p (b d) -> p b d", b=B), mask,
                                  ps[0:D, 3, :].rearrange("p (b d) -> p b d", b=B))
                V.copy_predicated(ex_t.rearrange("p (b d) -> p b d", b=B), mask,
                                  ps[0:D, 4, :].rearrange("p (b d) -> p b d", b=B)).then_inc(s["x_sqo"], 1)
                link(halved)
            dve.wait_ge(s["x_sqo"], SQUARINGS + 1)
            link(V.tensor_tensor(ex, ex, ident8, ALU.subtract))

            ada(2)

            dve.wait_ge(s["l_x"], 16)
            with dve.Fori(0, B) as b:
                V.tensor_copy(xn[:, 0:LT, :], x_sb[:, bass.ds(b * LT, LT), :]).then_inc(s["z_in"], 1)
                V.tensor_copy(rmi[:, 0:D], ex[:, bass.ds(b * D, D)])
                V.tensor_copy(rmi[:, D:P], ex[:, bass.ds(b * D, D)]).then_inc(s["z_in"], 1)
                for lt in range(LT):
                    dve.wait_ge(s["z_d"], b * LT + lt + 1)
                    xt = x_sb[:, bass.ds(b * LT + lt, 1), :].rearrange("p o c -> p (o c)")
                    V.tensor_tensor(xt, ps[:, 4 + lt, 0:C], xt, ALU.add).then_inc(s["z_x"], 1)
            dve.wait_ge(s["z_x"], LT * B)

            def layer_norm(tile, n, unit):
                dm, m2, q, v, y, y2, z, nmr = [ln[:, i, 0:n] for i in range(8)]
                for i in range(n):
                    ins = V.bn_stats(st[:, i, :], x_sb[:, bass.ds(tile + i, 1), :].rearrange("p o c -> p (o c)"))
                link(ins)
                link(V.tensor_tensor(dm, st[:, 0:n, 1], st[:, 0:n, 4], ALU.subtract))
                link(V.tensor_tensor(m2, st[:, 0:n, 1], st[:, 0:n, 4], ALU.add))
                link(V.tensor_tensor(q, st[:, 0:n, 2], st[:, 0:n, 5], ALU.add))
                link(V.tensor_tensor(dm, dm, dm, ALU.mult))
                link(V.scalar_tensor_tensor(v, q, 4.0 / C, dm, ALU.mult, ALU.add))
                link(V.tensor_scalar(v, v, 0.25, LN_EPS, ALU.mult, ALU.add))
                link(V.tensor_scalar(y.bitcast(I32), v.bitcast(I32), -0.5, RSQRT_SEED, ALU.mult, ALU.add))
                for _ in range(3):
                    link(V.tensor_tensor(y2, y, y, ALU.mult))
                    link(V.scalar_tensor_tensor(z, v, -0.5, y2, ALU.mult, ALU.mult))
                    link(V.scalar_tensor_tensor(y, z, 1.5, y, ALU.add, ALU.mult))
                link(V.scalar_tensor_tensor(nmr, m2, -0.5, y, ALU.mult, ALU.mult))
                for i in range(n):
                    ins = V.tensor_scalar(xn[:, i, :], x_sb[:, bass.ds(tile + i, 1), :].rearrange("p o c -> p (o c)"),
                                          y[:, i:i + 1], nmr[:, i:i + 1], ALU.mult, ALU.add)
                    if i % LT == LT - 1:
                        ins.then_inc(s["n_xn"], 1)

            LN_LINKS = 18

            for l in range(LAYERS):
                layer_norm(0, LT, units_a[l])
                with Turns(B, LN_LINKS + 2 + 2) as b:
                    t = b + l * B
                    dve.wait_ge(s["n_T"], b + units_a[l] + 1)
                    layer_norm((b + 1) * LT, LT, b + units_a[l] + 1)
                    for h in range(H):
                        dve.wait_ge(s["t_mx"], t * H + h + 1)
                        V.tensor_reduce(nmax[:, :, h, ONE], ps[:, 2 + h % HJ, :].rearrange("p (l t) -> p l t", l=LT),
                                        AX.X, ALU.max, negate=True).then_inc(s["t_mxd"], 1)
                    for i in range(2):
                        dve.wait_ge(s["t_nm"], t * 2 + i + 1)
                        qq = q_t[:, 2 * i:2 * i + 2, :].rearrange("p g t -> p (g t)")
                        V.tensor_tensor(qq, ps[:, 6 + i, :], qq, ALU.add).then_inc(s["t_nma"], 1)
                    for lt in range(LT):
                        dve.wait_ge(s["t_o"], t * LT + lt + 1)
                        op = ps[:, 2 + lt, :].rearrange("p (h e) -> p h e", h=H)
                        link(V.reciprocal(rcp[:, lt, :], op[:, :, ONE]))
                        V.tensor_tensor(o_tok[:, lt, :].rearrange("p (h d) -> p h d", h=H), op[:, :, 0:HD],
                                        rcp[:, lt, :].unsqueeze(2).broadcast_to((P, H, HD)), ALU.mult
                                        ).then_inc(s["t_on"], 1)
                    dve.wait_ge(s["l_gate"], (b + l * (B + B)) * 16 + 16)
                    for lt in range(LT):
                        dve.wait_ge(s["t_pr"], t * LT + lt + 1)
                        xt = x_sb[:, bass.ds(b * LT + lt, 1), :].rearrange("p o c -> p (o c)")
                        dve.wait_ge(s["t_xd"], t * LT + lt + 1)
                        link(V.tensor_tensor(upd[:], ps[:, 6 + lt, 0:C], gate[:, 0, :], ALU.mult))
                        V.tensor_tensor(xt, xt, upd[:], ALU.add).then_inc(s["t_xd"], 1)
                dve.wait_ge(s["t_xd"], (l + 1) * B * LT + 1)
                ne = len(experts[l])
                dve.wait_ge(s["n_T"], units_a[l] + B + 1)
                layer_norm(0, CT, units_m[l])
                with Turns(CHUNKS, LN_LINKS + (CT if l < 2 else CT + GATE_LINKS)) as c:
                    dve.wait_ge(s["n_T"], c * CB + units_m[l] + CB)
                    layer_norm((c + 1) * CT, CT, c * CB + units_m[l] + CB)
                    if l == 2:
                        expert_gates = True
                        dve.wait_ge(s["m_lt"], c + 1)
                        lgt = gm[:, 0, :, :]
                        rank, s1, s2, tmp, m1, m2_ = gm[:, 1, :, :], gm[:, 2, :, :], gm[:, 3, :, :], gm[:, 6, :, :], gm[:, 7, :, 0], gm[:, 8, :, 0]
                        link(V.tensor_copy(lgt, ps[:, 7, 0:CT * E].rearrange("p (i e) -> p i e", i=CT)))
                        for j in range(E):
                            for lo, hi, op in ((0, j, ALU.is_gt), (j + 1, E, ALU.is_ge)):
                                if lo < hi:
                                    lj = lgt[:, :, j:j + 1].broadcast_to((P, CT, hi - lo))
                                    ins = V.tensor_tensor(cmp_[:, :, j, lo:hi], lj, lgt[:, :, lo:hi], op)
                        link(ins)
                        link(V.tensor_reduce(rank, cmp_[:].rearrange("p t j i -> p t i j"), AX.X, ALU.add))
                        link(V.tensor_scalar(s1, rank, 0.0, None, ALU.is_equal))
                        link(V.tensor_scalar(s2, rank, 1.0, None, ALU.is_equal))
                        link(V.tensor_tensor(tmp, s1, s2, ALU.subtract))
                        link(V.tensor_tensor(tmp, tmp, lgt, ALU.mult))
                        V.tensor_reduce(gm[:, 4, :, 0:1], tmp, AX.X, ALU.add).then_inc(s["m_cw"], 1)
                        dve.wait_ge(s["m_tanh"], c + 1)
                        link(V.tensor_tensor(tmp, s1, s2, ALU.subtract))
                        link(V.tensor_tensor(tmp, tmp, gm[:, 5, :, 0:1].broadcast_to((P, CT, E)), ALU.mult))
                        link(V.tensor_tensor(tmp, tmp, s1, ALU.add))
                        link(V.tensor_tensor(tmp, tmp, s2, ALU.add))
                        link(V.tensor_scalar(tmp, tmp, 0.5, None, ALU.mult))
                    if l == 2:
                        dve.wait_ge(s["z_x"], c * CT + B * LT)
                    dve.wait_ge(s["l_gate"], (c * CB + l * 2 * B + B + CB) * 16)
                    for ei, e in enumerate(experts[l]):
                        n = c * ne + passes[l] + ei
                        for i in range(CT):
                            dve.wait_ge(s["m_f2"], n * CT + i + 1)
                            src = ps[:, 5 + i % 2, 0:C]
                            xt = x_sb[:, bass.ds(c * CT + i, 1), :].rearrange("p o c -> p (o c)")
                            if l < 2:
                                dve.wait_ge(s["m_upd"], n * CT + i + 2)
                                link(V.tensor_tensor(upd[:], src, gate[:, i // LT, :], ALU.mult))
                                V.tensor_tensor(xt, xt, upd[:], ALU.add).then_inc(s["m_upd"], 1)
                            elif ei == 0:
                                V.tensor_scalar(acc[:, i, :], src, gm[:, 6, i, e:e + 1], None, ALU.mult).then_inc(s["m_upd"], 1)
                            else:
                                dve.wait_ge(s["m_upd"], n * CT + i + 2 - CT + 1)
                                V.scalar_tensor_tensor(acc[:, i, :], src, gm[:, 6, i, e:e + 1], acc[:, i, :], ALU.mult, ALU.add
                                                       ).then_inc(s["m_upd"], 1)
                    if l == 2:
                        dve.wait_ge(s["m_upd"], (c + 1) * ne * CT + passes[l] * CT + 2)
                        for i in range(CT):
                            xt = x_sb[:, bass.ds(c * CT + i, 1), :].rearrange("p o c -> p (o c)")
                            link(V.tensor_tensor(acc[:, i, :], acc[:, i, :], gate[:, i // LT, :], ALU.mult))
                            V.tensor_tensor(xt, xt, acc[:, i, :], ALU.add).then_inc(s["z_x"], 1)
                if l < 2:
                    dve.wait_ge(s["m_upd"], passes[l + 1] * CT + 2)
                    dve.wait_ge(s["n_T"], units_m[l] + CB * (CHUNKS + 1))

        @block.tensor
        def _(pe):
            pe.wait_ge(s["c_init"], N_INIT)
            pe.wait_ge(s["c_fix"], 7)
            pe.wait_ge(s["e_silu"], 1)
            for k in range(KT):
                last = pe.transpose(ps[0:KC, 0, k * B:(k + 1) * B], silu_sb[:, k * KC:(k + 1) * KC], ident[0:B, 0:B])
            last.then_inc(s["e_sT"], 1)
            pe.wait_ge(s["l_w0"], 16)
            for n in range(12):
                if n >= 4:
                    pe.wait_ge(s["e_wTo"], n - 3)
                for i in range(4):
                    last = pe.transpose(ps[0:KC, 1 + n % 4, i * WROWS:(i + 1) * WROWS],
                                        w0_nat[:, (n % 4) * 4 + i, (n // 4) * KC:(n // 4 + 1) * KC], ident[0:WROWS, 0:WROWS])
                last.then_inc(s["e_wT"], 1)
            pe.wait_ge(s["e_wTo"], 12)
            pe.wait_ge(s["e_sTo"], 1)
            for q in range(4):
                for k in range(KT):
                    last = pe.matmul(ps[0:B, 1 + q, 0:504], s_t[:, k, :], w0_t[:, k, q * 504:(q + 1) * 504],
                                     start=(k == 0), stop=(k == KT - 1))
                last.then_inc(s["e_v"], 1)

            def ada(l):
                pe.wait_ge(s["l_aw"], 16 * (l + 1))
                if l == 0:
                    pe.wait_ge(s["e_vo"], 4)
                for q in range(4):
                    for k in range(KT):
                        last = pe.matmul(ps[0:B, 1 + q, 0:432], s_t[:, k, :], ada_w[:, k, q * 432:(q + 1) * 432],
                                         start=(k == 0), stop=(k == KT - 1))
                    last.then_inc(s["e_mod"], 1)
                pe.wait_ge(s["e_modo"], 4 * (l + 1))
                for a_, part in enumerate((0, 1, 3, 4)):
                    for k in range(KT):
                        last = pe.transpose(ps[0:KC, 5, (a_ * KT + k) * B:(a_ * KT + k + 1) * B],
                                            mods_sb[:, part * C + k * KC:part * C + (k + 1) * KC], ident[0:B, 0:B])
                last.then_inc(s["e_modT"], 1)
                pe.wait_ge(s["e_modTo"], 2 * (l + 1))

            ada(0)

            pe.wait_ge(s["l_p"], 16)
            for k in range(KT):
                last = pe.transpose(ps[0:D, 0, k * KC:(k + 1) * KC], p_nat[:, k, :], ident[0:KC, 0:KC])
            last.then_inc(s["q_pT"], 1)
            with pe.Fori(0, D // 2) as m:
                for half in range(2):
                    j = m * 2 + half
                    pe.wait_ge(s["q_at"], j * 2 + 2)
                    pe.matmul(ps[:, 6 + half, 0:C], esel.broadcast_to((D, P)), at_q, start=True, stop=True
                              ).then_inc(s["q_vb"], 1)
                    pe.matmul(ps[:, 2 + half, 0:C], esel.broadcast_to((D, P)), at_q, start=True, stop=True
                              ).then_inc(s["q_va"], 1)
            pe.wait_ge(s["q_vTo"], 1)
            for k in range(KT):
                last = pe.transpose(ps[0:KC, 0, k * D:(k + 1) * D], vt_q[:, k * KC:(k + 1) * KC], ident[0:D, 0:D])
            last.then_inc(s["q_vT"], 1)
            pe.wait_ge(s["q_vTo"], 2)
            for k in range(KT):
                last = pe.matmul(ps[0:D, 1, 0:D], v_nat[:, k, :], v_nat[:, k, :], start=(k == 0), stop=(k == KT - 1))
            last.then_inc(s["q_g"], 1)
            pe.wait_ge(s["q_no"], 1)
            pe.transpose(ps[0:D, 1, 0:D], nn, ident[0:D, 0:D]).then_inc(s["q_n"], 1)
            for r in range(5):
                pe.wait_ge(s["q_no"], 2 + 2 * r)
                pe.matmul(ps[0:D, 1, 0:D], nnt, nn, start=True, stop=True)
                pe.matmul(ps[0:D, 1, D:2 * D], nn, nnt, start=True, stop=True).then_inc(s["q_n"], 1)
                pe.wait_ge(s["q_no"], 3 + 2 * r)
                pe.matmul(ps[0:D, 2, 0:D], nn, pmt, start=True, stop=True).then_inc(s["q_n"], 1)
            pe.wait_ge(s["q_no"], 12)
            pe.matmul(ps[0:D, 1, 0:D], pmt, vd1, start=True, stop=True).then_inc(s["q_u"], 1)
            pe.wait_ge(s["q_uo"], 1)
            pe.matmul(ps[0:D, 2, 0:C], tv1, vt_q, start=True, stop=True).then_inc(s["q_u"], 1)
            pe.wait_ge(s["q_uo"], 2)
            for k in range(KT):
                last = pe.transpose(ps[0:KC, 0, k * D:(k + 1) * D], u_t[:, k * KC:(k + 1) * KC], ident[0:D, 0:D])
            last.then_inc(s["q_u"], 1)
            pe.wait_ge(s["q_uo"], 3)

            ada(1)

            pe.wait_ge(s["l_aup"], 16 * (D - 1))
            for b in range(B):
                last = pe.transpose(ps[0:D, 3, b * D:(b + 1) * D], aup[:, b * D:(b + 1) * D], ident[0:D, 0:D])
            last.then_inc(s["x_up"], 1)
            pe.wait_ge(s["x_ant"], 1)
            pe.transpose(ps[0:B, 4, 0:D], nrow, ident[0:D, 0:D]).then_inc(s["x_nr"], 1)
            pe.wait_ge(s["x_ant"], 2)
            pe.matmul(ps[0:D, 4, 0:B], nrep, ident[0:B, 0:B], start=True, stop=True).then_inc(s["x_nr"], 1)
            with pe.Fori(0, TAYLOR) as i:
                pe.wait_ge(s["x_ho"], i + 1)
                pe.matmul(ps[:, 3, 0:D], ant[:, 0:P], ex[:, 0:D], start=True, stop=True)
                for b in range(1, B):
                    bb = slice(b * D, (b + 1) * D)
                    last = pe.matmul(ps[0:D, 3, bb], ant[:, bb], ex[:, bb], start=True, stop=True)
                last.then_inc(s["x_h"], 1)
            pe.wait_ge(s["x_ho"], TAYLOR + 1)
            for b in range(B):
                last = pe.transpose(ps[0:D, 4, b * D:(b + 1) * D], ex[:, b * D:(b + 1) * D], ident[0:D, 0:D])
            last.then_inc(s["x_rT"], 1)
            with pe.Fori(0, SQUARINGS) as i:
                pe.wait_ge(s["x_sqo"], i + 1)
                pe.matmul(ps[:, 3, 0:D], ex_t[:, 0:P], ex[:, 0:D], start=True, stop=True)
                for b in range(1, B):
                    bb = slice(b * D, (b + 1) * D)
                    pe.matmul(ps[0:D, 3, bb], ex_t[:, bb], ex[:, bb], start=True, stop=True)
                for b in range(B):
                    bb = slice(b * D, (b + 1) * D)
                    last = pe.matmul(ps[0:D, 4, bb], ex[:, bb], ex_t[:, bb], start=True, stop=True)
                last.then_inc(s["x_sq"], 1)
            pe.wait_ge(s["x_sqo"], SQUARINGS + 1)

            ada(2)

            with pe.Fori(0, B) as b:
                pe.wait_ge(s["z_in"], b * 2 + 2)
                for k in range(KT):
                    for lt in range(LT):
                        last = pe.transpose(ps[0:KC, k // 2, (k % 2) * T + lt * P:(k % 2) * T + (lt + 1) * P],
                                            xn[:, lt, k * KC:(k + 1) * KC], ident[:])
                last.then_inc(s["z_xT"], 1)
                pe.wait_ge(s["z_xTo"], b + 1)
                for k in range(KT):
                    last = pe.matmul(ps[0:D, 2, 0:T], u_nat[:, k, :], h_t[0:KC, k, 0:T], start=(k == 0), stop=(k == KT - 1))
                last.then_inc(s["z_z"], 1)
                pe.wait_ge(s["z_zo"], b + 1)
                pe.matmul(ps[:, 3, 0:T], rmi, z_sb, start=True, stop=True).then_inc(s["z_zr"], 1)
                pe.wait_ge(s["z_zro"], b + 1)
                for lt in range(LT):
                    pe.matmul(ps[:, 4 + lt, 0:C], zr_sb[:, lt * P:(lt + 1) * P], u_t, start=True, stop=True
                              ).then_inc(s["z_d"], 1)

            def transposes(unit, cb):
                pe.wait_ge(s["n_xn"], unit + 1)
                for k in range(KT):
                    for lt in range(LT):
                        last = pe.transpose(ps[0:KC, k // 2, (k % 2) * T + lt * P:(k % 2) * T + (lt + 1) * P],
                                            xn[:, cb * LT + lt, k * KC:(k + 1) * KC], ident[:])
                last.then_inc(s["n_T"], 1)

            for l in range(LAYERS):
                transposes(units_a[l], 0)
                pe.wait_ge(s["l_attnw"], 16 * ATTN_DMAS * (l + 1))
                with pe.Fori(0, B) as b:
                    t = b + l * B
                    pe.wait_ge(s["n_h"], b + units_a[l] + 1)
                    for which, w, done in ((0, wq, "t_q"), (1, wk, "t_k")):
                        for g in range(G):
                            for k in range(KT):
                                last = pe.matmul(ps[:, 2 + 2 * which + g // 2, (g % 2) * T:(g % 2 + 1) * T],
                                                 w[:, k, g * HJ:(g + 1) * HJ, :].rearrange("p h d -> p (h d)"),
                                                 h_t[0:KC, k, 0:T], start=(k == 0), stop=(k == KT - 1))
                            if g % 2 == 1:
                                last.then_inc(s[done], 1)
                    pe.wait_ge(s["t_xd"], t * LT + 1)
                    if l:
                        pe.wait_ge(s["m_upd"], passes[l] * CT + 2)
                    for lt in range(LT):
                        for k in range(KT):
                            kk = KC + (k == KT - 1)
                            last = pe.matmul(ps[:, 6 + lt, 0:C], h_t[0:kk, k, lt * P:(lt + 1) * P], wv[0:kk, k, :],
                                             start=(k == 0), stop=(k == KT - 1))
                        last.then_inc(s["t_v"], 1)
                    transposes(b + units_a[l] + 1, 0)
                    pe.wait_ge(s["t_qe"], t * 2 + 2)
                    for h in range(H):
                        g, r = h // HJ, slice(h % HJ * HP, (h % HJ + 1) * HP)
                        if h >= HJ:
                            pe.wait_ge(s["t_mxd"], t * H + h - HJ + 1)
                        for lt in range(LT):
                            last = pe.matmul(ps[:, 2 + h % HJ, lt * T:(lt + 1) * T], q_r[r, g, lt * P:(lt + 1) * P],
                                             k_r[r, g, :], start=True, stop=True)
                        last.then_inc(s["t_mx"], 1)
                    pe.wait_ge(s["t_mxd"], t * H + H)
                    pe.wait_ge(s["t_ve"], t * LT + LT)
                    for g in range(G):
                        for lt in range(LT):
                            last = pe.transpose(ps[:, 6 + g // 2, (g % 2) * T + lt * P:(g % 2) * T + (lt + 1) * P],
                                                nmax[:, lt, g * HJ:(g + 1) * HJ, :].rearrange("p h e -> p (h e)"), ident[:])
                        if g % 2 == 1:
                            last.then_inc(s["t_nm"], 1)

                    def values(h):
                        g, r = h // HJ, slice(h % HJ * HP, (h % HJ + 1) * HP)
                        pe.wait_ge(s["t_exp"], t * H + h + 1)
                        for m in range(LT):
                            last = pe.matmul(ps[r, 6 + g // 2, (g % 2) * T:(g % 2 + 1) * T], v_sb[:, m, h, :],
                                             p_t[:, h % HJ, m, :], start=(m == 0), stop=(m == LT - 1))
                        last.then_inc(s["t_pv"], 1)

                    for h in range(H):
                        g, r = h // HJ, slice(h % HJ * HP, (h % HJ + 1) * HP)
                        if h % 8 == 0:
                            pe.wait_ge(s["t_nma"], t * 2 + h // 8 + 1)
                        if h >= HJ:
                            pe.wait_ge(s["t_exp"], t * H + h - HJ + 1)
                        for m in range(LT):
                            last = pe.matmul(ps[:, 2 + h % HJ, m * T:(m + 1) * T], k_t[r, g, m * P:(m + 1) * P],
                                             q_t[r, g, :], start=True, stop=True)
                        last.then_inc(s["t_s"], 1)
                        if h >= 2:
                            values(h - 2)
                    values(H - 2)
                    values(H - 1)
                    pe.wait_ge(s["t_pve"], t * 2 + 2)
                    for lt in range(LT):
                        for g in range(G):
                            last = pe.transpose(ps[:, 2 + lt, g * P:(g + 1) * P], o_pad[:, g, lt * P:(lt + 1) * P], ident[:])
                        last.then_inc(s["t_o"], 1)
                    pe.wait_ge(s["t_on"], t * LT + LT)
                    for k in range(KT):
                        for lt in range(LT):
                            last = pe.transpose(ps[0:KC, 4 + k // 2, (k % 2) * T + lt * P:(k % 2) * T + (lt + 1) * P],
                                                o_tok[:, lt, k * KC:(k + 1) * KC], ident[:])
                        if k:
                            last.then_inc(s["t_oT"], 1)
                    pe.wait_ge(s["t_oTe"], t * 2 + 2)
                    for lt in range(LT):
                        for k in range(KT):
                            kk = KC + (k == KT - 1)
                            last = pe.matmul(ps[:, 6 + lt, 0:C], o_t[0:kk, k, lt * P:(lt + 1) * P], wp[0:kk, k, :],
                                             start=(k == 0), stop=(k == KT - 1))
                        last.then_inc(s["t_pr"], 1)
                ne = len(experts[l])
                pe.wait_ge(s["n_h"], units_a[l] + B + 1)
                pe.wait_ge(s["t_xd"], (l + 1) * B * LT + 1)
                transposes(units_m[l], 0)
                pe.wait_ge(s["n_h"], units_m[l] + 1)
                transposes(units_m[l] + 1, 1)
                for n in mlp_loads[l]:
                    pe.wait_ge(s[f"l_mlpw{n}"], 16 * MLP_DMAS)
                if l == 2:
                    pe.wait_ge(s["l_wg"], 16)
                with pe.Fori(0, CHUNKS) as c:
                    pe.wait_ge(s["n_h"], c * CB + units_m[l] + CB)
                    if l == 2:
                        for k in range(KT):
                            last = pe.matmul(ps[0:E, 7, :], wg_sb[:, k, :], h_t[0:KC, k, :], start=(k == 0), stop=(k == KT - 1))
                        last.then_inc(s["m_lg"], 1)
                        pe.wait_ge(s["m_lge"], c + 1)
                        for i in range(CT):
                            last = pe.matmul(ps[:, 7, i * E:(i + 1) * E], lg4[:, i * P:(i + 1) * P], ident[0:E, 0:E],
                                             start=True, stop=True)
                        last.then_inc(s["m_lt"], 1)
                    for ei, e in enumerate(experts[l]):
                        n = c * ne + passes[l] + ei
                        for m in range(FT):
                            if m >= 3:
                                pe.wait_ge(s["m_gelu"], n * FT + m - 2)
                            for k in range(KT):
                                last = pe.matmul(ps[:, 2 + m % 3, :], w1_sb[e][:, k, m * P:(m + 1) * P], h_t[0:KC, k, :],
                                                 start=(k == 0), stop=(k == KT - 1))
                            last.then_inc(s["m_f1"], 1)
                        if ei == ne - 1:
                            transposes(c * CB + units_m[l] + CB, 0)
                        pe.wait_ge(s["m_gelu"], n * FT + FT)
                        for i in range(CT):
                            pe.wait_ge(s["m_upd"], n * CT + i + 1)
                            pe.matmul(ps[:, 5 + i % 2, 0:C], ones[0:1, :], b2_sb[0:1, e, :], start=True, stop=False)
                            for m in range(FT):
                                last = pe.matmul(ps[:, 5 + i % 2, 0:C], mid[:, m, i * P:(i + 1) * P], w2_sb[e][:, m, :],
                                                 start=False, stop=(m == FT - 1))
                            last.then_inc(s["m_f2"], 1)
                            if ei == ne - 1 and i == 1:
                                pe.wait_ge(s["n_h"], c * CB + units_m[l] + CB + 1)
                                transposes(c * CB + units_m[l] + CB + 1, 1)
                pe.wait_ge(s["n_h"], units_m[l] + CB * (CHUNKS + 1))


GATE_LINKS = 12


_INS = ['x', 'cond_1152', 'L0_cond_P', 'L0_cond_W', 'L0_cond_b', 'L1_cond_W_qkv', 'L1_cond_b_qkv', 'L1_cond_W_proj',
        'L1_cond_b_proj', 'L1_cond_W_fc1', 'L1_cond_b_fc1', 'L1_cond_W_fc2', 'L1_cond_b_fc2', 'L1_cond_W_ada',
        'L1_cond_b_ada', 'L2_cond_qkv_w', 'L2_cond_qkv_b', 'L2_cond_out_w', 'L2_cond_out_b', 'L2_cond_w1',
        'L2_cond_b1', 'L2_cond_w2', 'L2_cond_b2', 'L2_cond_ada_w', 'L2_cond_ada_b', 'L3_cond_w_adaln',
        'L3_cond_b_adaln', 'L3_cond_w_qkv', 'L3_cond_b_qkv', 'L3_cond_w_proj', 'L3_cond_b_proj', 'L3_cond_w_gate',
        'L3_cond_w1', 'L3_cond_b1', 'L3_cond_w2', 'L3_cond_b2']
_OUTS = [((B, T, C), 'float32')]


def kernel(**inputs):
    import numpy as _np
    import concourse.bacc as _bacc
    from concourse import mybir as _mybir
    from concourse.bass_utils import run_bass_kernel_spmd as _run

    nc = _bacc.Bacc("TRN2", target_bir_lowering=False, num_devices=1)
    arrays, args = {}, {}
    for name in _INS:
        a = _np.ascontiguousarray(inputs[name])
        arrays[f"in_{name}_dram"] = a
        args[name] = nc.dram_tensor(f"in_{name}_dram", a.shape, _mybir.dt.from_np(a.dtype), kind="ExternalInput").ap()
    for i, (shape, dtype) in enumerate(_OUTS):
        dt = _mybir.dt.from_np(_np.dtype(dtype))
        args["out"] = nc.dram_tensor(f"out_{i}_dram", shape, dt, kind="ExternalOutput").ap()
    build(nc, args)
    r = _run(nc, [arrays], core_ids=[0])
    got = tuple(r.results[0][f"out_{i}_dram"] for i in range(len(_OUTS)))
    return got[0]
```

```python
from contextlib import ExitStack

import concourse.bass as bass
from concourse import mybir

F32 = mybir.dt.float32
F32R = mybir.dt.float32r
I32 = mybir.dt.int32
ALU = mybir.AluOpType
ACT = mybir.ActivationFunctionType
AX = mybir.AxisListType

B, T, C = 8, 256, 288
P = 128
KC = 96
KT = C // KC
H, HD, HP = 16, 18, 32
G = H * HP // P
HJ = P // HP
LT = T // P
NEXT_AT = 8
PSLOTS = 3
F = 4 * C
FT = F // P
E = 4
LAYERS = 3
D = 64
NSK = D * (D - 1) // 2
CB = 2
CHUNKS = B // CB
CT = CB * LT
CN = CB * T
LN_EPS = 1e-6
SCALE = float(HD) ** -0.5
ONE = HD
WTILE, WROWS = 16, NSK // 16
TAYLOR = 14
EXP_NORM = 2.0
SQUARINGS = 17
QR_ALONE = 8
QR_SERIES = TAYLOR
QR_SQUARED = D // 2 - QR_ALONE - QR_SERIES
QR_C1, QR_C2 = 2 * QR_ALONE, 2 * (QR_ALONE + QR_SERIES)
RSQRT_SEED = 1597463007.0
MODS = 6 * C
SCRATCH_E = FT * C + KT * F


def build(nc, a):
    ctx = ExitStack()
    with ctx:
        def sb(name, shape, dt=F32):
            return ctx.enter_context(nc.sbuf_tensor(name, shape, dt))

        def sem(name):
            return ctx.enter_context(nc.semaphore(name))

        x_sb = sb("x_sb", [P, (B + CB) * LT, C])
        wexp = sb("wexp", [P, E * SCRATCH_E])
        wq = sb("wq", [KC, KT, H, HP])
        wk = sb("wk", [KC, KT, H, HP])
        wv = sb("wv", [KC + 1, KT, C])
        wp = sb("wp", [KC + 1, KT, C])
        work = sb("work", [P, FT * CN])
        q_r = sb("q_r", [P, G, T], F32R)
        k_r = sb("k_r", [P, G, T], F32R)
        v_sb = sb("v_sb", [P, LT, H, HP])
        nmax = sb("nmax", [P, LT, H, HP])
        o_pad = sb("o_pad", [P, G, T])
        o_tok = sb("o_tok", [P, LT, C])
        o_t = sb("o_t", [KC + 1, KT, T])
        xn = sb("xn", [P, CT, C])
        h_t = sb("h_t", [KC + 1, KT, CN])
        acc = sb("acc", [P, CT, C])
        gate = sb("gate", [P, CB, C])
        upd = sb("upd", [P, C])
        ident = sb("ident", [P, P])
        mod_t = sb("mod_t", [KC, LAYERS, 4, KT, B + CB])
        bqk = sb("bqk", [P, 2, G])
        kone = sb("kone", [P, 1])
        b1_sb = sb("b1_sb", [P, E, FT])
        b2_sb = sb("b2_sb", [P, E, C])
        wg_sb = sb("wg_sb", [KC, KT, E])
        ln = sb("ln", [P, 12, CT])
        st = sb("st", [P, CT, 6])
        rcp = sb("rcp", [P, LT, H])
        gm = sb("gm", [P, 12, CT, E])
        cmp_ = sb("cmp", [P, CT, E, E])
        s_t = sb("s_t", [KC, KT, B])
        sc_small = sb("sc_small", [D, 26])

        lg4 = o_pad[0:E, 0:2, :].rearrange("p g t -> p (g t)")
        q_t = work[:, 0:G * T].rearrange("p (g t) -> p g t", g=G)
        k_t = work[:, G * T:2 * G * T].rearrange("p (g t) -> p g t", g=G)
        p_t = work[:, 2 * G * T:2 * G * T + PSLOTS * LT * T].rearrange("p (r m t) -> p r m t", r=PSLOTS, m=LT)
        kz = [acc[:, :, :].rearrange("p a c -> p (a c)")[:, 0:HJ * T], work[:, FT * CN - HJ * T:FT * CN]]
        assert 2 * G * T + PSLOTS * LT * T + HJ * T <= FT * CN
        mid = work[:, :].rearrange("p (f n) -> p f n", f=FT)
        w1_sb = [wexp[0:KC, e * SCRATCH_E:e * SCRATCH_E + KT * F].rearrange("p (k f) -> p k f", k=KT) for e in range(E)]
        w2_sb = [wexp[:, e * SCRATCH_E + KT * F:(e + 1) * SCRATCH_E].rearrange("p (f c) -> p f c", f=FT) for e in range(E)]

        pos = [SCRATCH_E]

        def early(parts, n):
            v = wexp[0:parts, pos[0]:pos[0] + n]
            pos[0] += n
            assert pos[0] <= E * SCRATCH_E
            return v

        w0_nat = early(WROWS, WTILE * C).rearrange("p (t c) -> p t c", t=WTILE)
        w0_t = early(KC, KT * NSK).rearrange("p (k n) -> p k n", k=KT)
        ada_w = early(KC, KT * MODS).rearrange("p (k n) -> p k n", k=KT)
        bias_b = early(B, NSK)
        v0 = w0_nat[0:B, 0:NSK // C, :].rearrange("p t c -> p (t c)")

        def early2(parts, n, at=[0]):
            v = work[0:parts, at[0]:at[0] + n]
            at[0] += n
            return v

        def square8(v):
            return v.rearrange("p a c -> p (a c)")[:, 0:B * D]

        cond_sb = early2(B, C)
        silu_sb = early2(B, C)
        mods_sb = early2(B, MODS)
        at_q = early2(D, C)
        p_nat = early2(KC, KT * D).rearrange("p (k d) -> p k d", k=KT)
        v_nat = early2(KC, KT * D).rearrange("p (k d) -> p k d", k=KT)
        u_nat = early2(KC, KT * D).rearrange("p (k d) -> p k d", k=KT)
        u_t = early2(D, C)
        vt_q = early2(D, C)
        aup = square8(xn[0:D, 0:2, :])
        ant = square8(xn[0:D, 2:4, :])
        ex = square8(acc[0:D, 0:2, :])
        ex_t = square8(acc[0:D, 2:4, :])
        ident8 = o_pad[0:D, 0:2, :].rearrange("p g t -> p (g t)")
        smask = o_pad[0:D, 2, 0:D]
        nsm = o_tok[0:D, :, :].rearrange("p l c -> p (l c)")
        nn, nnt, pmt, tv1, nscr, vd1 = [nsm[:, i * D:(i + 1) * D] for i in range(6)]
        sq_junk = h_t[0:D, 0, 0:C]
        dot_junk = h_t[0:D, 1, 0:C]
        l0_x = [h_t[0:KC, :, 0:T], o_t[0:KC, :, :]]
        l0_z = [h_t[0:D, 0, T:2 * T], nsm[:, 0:T]]
        l0_zr = [h_t[0:D, 1, T:2 * T], nsm[:, T:2 * T]]
        rmi = [h_t[0:D, 2, T:T + P], gate[0:D, 0, 0:P]]
        q_small = [sc_small[:, i:i + 1] for i in range(26)]
        (esel, piv, rcol, sdot, sn, sng, y0, sgnh, nb2, pivh, dd, vpiv, uu, ww, nbv, ddv, kcol, krec, dg, rd, ry, rdd, zero, unused, tiny, rcolh) = q_small[:26]
        e_small = gm[0:D, :, :, :].rearrange("p a b c -> p (a b c)")
        nrow, cur, cur2, esc, eflag = [e_small[:, i * B:(i + 1) * B] for i in range(5)]
        nmx8 = e_small[0:B, 40:41]
        nrep = e_small[0:B, 48:48 + D]
        emask = ctx.enter_context(nc.sbuf_tensor("emask", [D, B], I32))

        ps = ctx.enter_context(nc.psum_tensor("ps", [P, 8, 512], F32))

        mods_d = nc.dram_tensor("mods_scratch", (LAYERS, B, MODS), F32).ap()


        def hps(unit_k):
            return ps[0:KC, unit_k // 2, (unit_k % 2) * T:(unit_k % 2 + 1) * T]

        def l0_ps(u, k):
            return ps[0:KC, 6 * u + k // 2, (k % 2) * T:(k % 2 + 1) * T]

        max_bank = [(2, 4)[h % 2] if h < H // 2 else 2 + h % 4 for h in range(H)]
        max_before = [max([i for i in range(h) if max_bank[i] == max_bank[h]], default=None) for h in range(H)]

        names = """l_x l_p l_w0 l_b0 l_cond l_aw l_ab l_aup l_attnw l_bqk l_mlpw0 l_mlpw1 l_mlpw2 l_mlpw3 l_mlpw4 l_mlpw5 l_gate l_mods l_out l_wg
            m_tanh c_ident c_init c_fix d_chain
            e_silu e_sT e_sTo e_wT e_wTo e_v e_vo e_mod e_modo e_modT e_modTo
            q_pT q_vb q_sn q_sq q_at q_vT q_vTo q_g q_no q_n q_u q_uo q_rt q_rtd
            x_up x_ant x_nr x_nro x_h x_ho x_rT x_sq x_sqo
            z_in z_xT z_xTo z_z z_zo z_zr z_zro z_d z_x z_rm
            n_xn n_T n_h
            t_qk t_qe t_v t_ve t_mx t_mxd t_nm t_nma t_s t_exp t_pv t_pve t_o t_on t_oT t_oTe t_pr t_xd kz_zero kz_even kz_odd
            m_f1 m_gelu m_f2 m_upd m_lg m_lge m_lt m_cw""".split()
        s = {n: sem(n) for n in names}
        N_INIT = 12

        block = ctx.enter_context(nc.Block())

        L = [dict(ada="L1_cond_W_ada", adab="L1_cond_b_ada", qkv="L1_cond_W_qkv", qkvb="L1_cond_b_qkv",
                  proj="L1_cond_W_proj", projb="L1_cond_b_proj", w1="L1_cond_W_fc1", b1="L1_cond_b_fc1",
                  w2="L1_cond_W_fc2", b2="L1_cond_b_fc2"),
             dict(ada="L2_cond_ada_w", adab="L2_cond_ada_b", qkv="L2_cond_qkv_w", qkvb="L2_cond_qkv_b",
                  proj="L2_cond_out_w", projb="L2_cond_out_b", w1="L2_cond_w1", b1="L2_cond_b1",
                  w2="L2_cond_w2", b2="L2_cond_b2"),
             dict(ada="L3_cond_w_adaln", adab="L3_cond_b_adaln", qkv="L3_cond_w_qkv", qkvb="L3_cond_b_qkv",
                  proj="L3_cond_w_proj", projb="L3_cond_b_proj", w1="L3_cond_w1", b1="L3_cond_b1",
                  w2="L3_cond_w2", b2="L3_cond_b2")]
        experts = [[0], [1], [0, 1, 2, 3]]
        passes = [CHUNKS * sum(len(experts[i]) for i in range(l)) for l in range(LAYERS + 1)]
        units_a = [l * ((B + 1) + CB * (CHUNKS + 1)) for l in range(LAYERS)]
        units_m = [u + B + 1 for u in units_a]
        ATTN_DMAS = 2 * KT + 4
        MLP_DMAS = 4
        order_mlp = [(0, 0, 0), (1, 0, 1), (2, 2, 2), (2, 3, 3), (2, 0, 0), (2, 1, 1)]

        @block.sync
        def _(sp):
            sp.dma_start(cond_sb, a["cond_1152"]).then_inc(s["l_cond"], 16)
            sp.dma_start(p_nat, a["L0_cond_P"].rearrange("(k p) d -> p k d", p=KC)).then_inc(s["l_p"], 16)
            sp.dma_start(w0_nat, a["L0_cond_W"].rearrange("(t p) c -> p t c", p=WROWS)).then_inc(s["l_w0"], 16)
            sp.dma_start(bias_b, a["L0_cond_b"].partition_broadcast(B)).then_inc(s["l_b0"], 16)
            sp.dma_start(ada_w, a[L[0]["ada"]].rearrange("(k p) n -> p k n", p=KC)).then_inc(s["l_aw"], 16)
            sp.dma_start(x_sb[:, 0:B * LT, :], a["x"].rearrange("b (l p) c -> p (b l) c", p=P)).then_inc(s["l_x"], 16)

            def attention_weights(l):
                qkv = a[L[l]["qkv"]]
                for k in range(KT):
                    for which, w in ((0, wq), (1, wk)):
                        sp.dma_start(w[:, k, :, 0:HD],
                                     qkv[k * KC:(k + 1) * KC, which * C:(which + 1) * C].rearrange("p (h d) -> p h d", d=HD)
                                     ).then_inc(s["l_attnw"], 16)
                sp.dma_start(wv[0:KC, :, :], qkv[:, 2 * C:3 * C].rearrange("(k p) n -> p k n", p=KC)).then_inc(s["l_attnw"], 16)
                sp.dma_start(wv[KC:KC + 1, KT - 1, :], a[L[l]["qkvb"]][2 * C:3 * C].rearrange("(o n) -> o n", o=1)
                             ).then_inc(s["l_attnw"], 16)
                sp.dma_start(wp[0:KC, :, :], a[L[l]["proj"]].rearrange("(k p) n -> p k n", p=KC)).then_inc(s["l_attnw"], 16)
                sp.dma_start(wp[KC:KC + 1, KT - 1, :], a[L[l]["projb"]].rearrange("(o n) -> o n", o=1)
                             ).then_inc(s["l_attnw"], 16)
                for j in range(HJ):
                    for which in range(2):
                        src = a[L[l]["qkvb"]][which * C:(which + 1) * C].rearrange("(g j d) -> j d g", g=G, j=HJ)[j]
                        sp.dma_start(bqk[j * HP:j * HP + HD, which, :], src, allow_slow_non_contiguous=True
                                     ).then_inc(s["l_bqk"], 16)

            def mlp_weights(n):
                l, e, buf = order_mlp[n]
                w1, w2, b1, b2 = (a[L[l][n]] for n in ("w1", "w2", "b1", "b2"))
                if l == 2:
                    w1, w2, b1, b2 = w1[e], w2[e], b1[e], b2[e]
                sp.dma_start(w1_sb[buf], w1.rearrange("(k p) f -> p k f", p=KC)).then_inc(s[f"l_mlpw{n}"], 16)
                sp.dma_start(w2_sb[buf], w2.rearrange("(f p) c -> p f c", p=P)).then_inc(s[f"l_mlpw{n}"], 16)
                sp.dma_start(b1_sb[:, buf, :], b1.rearrange("(f p) -> p f", p=P), allow_slow_non_contiguous=True
                             ).then_inc(s[f"l_mlpw{n}"], 16)
                sp.dma_start(b2_sb[:, buf, :], b2.partition_broadcast(P)).then_inc(s[f"l_mlpw{n}"], 16)

            sp.wait_ge(s["c_init"], N_INIT)
            sp.wait_ge(s["e_vo"], 4)
            at = 0
            for i in range(D - 1):
                n = D - 1 - i
                sp.dma_start(aup[i:i + 1, :].rearrange("p (b d) -> p b d", b=B)[:, :, i + 1:D], v0[:, at:at + n],
                             allow_slow_non_contiguous=True).then_inc(s["l_aup"], 16)
                at += n

            sp.dma_start(bias_b[:, 0:MODS], a[L[0]["adab"]].partition_broadcast(B)).then_inc(s["l_ab"], 16)
            sp.wait_ge(s["c_fix"], 2)
            attention_weights(0)
            mlp_weights(0)
            sp.dma_start(wg_sb[:], a["L3_cond_w_gate"].rearrange("(k p) e -> p k e", p=KC)).then_inc(s["l_wg"], 16)

            for l in range(LAYERS):
                if l:
                    sp.wait_ge(s["e_mod"], 4 * l)
                    sp.dma_start(ada_w, a[L[l]["ada"]].rearrange("(k p) n -> p k n", p=KC)).then_inc(s["l_aw"], 16)
                    sp.wait_ge(s["e_modo"], 4 * l)
                    sp.dma_start(bias_b[:, 0:MODS], a[L[l]["adab"]].partition_broadcast(B)).then_inc(s["l_ab"], 16)
                sp.wait_ge(s["e_modo"], 4 * (l + 1))
                sp.dma_start(mods_d[l], mods_sb).then_inc(s["l_mods"], 16)
            sp.wait_ge(s["l_mods"], 16 * LAYERS)
            sp.wait_ge(s["z_d"], LT * B)
            for n in (1, 2, 3):
                mlp_weights(n)

            for l in range(LAYERS):
                sp.wait_ge(s["kz_zero"], 2 * (l + 1))
                if l:
                    sp.wait_ge(s["m_upd"], passes[l] * CT + 2)
                with sp.Fori(0, B) as b:
                    t = b + l * B
                    for g in range(G):
                        if g % 2 == 0:
                            sp.wait_ge(s["t_qe"], t * 4 + g + 2)
                        if g >= 2:
                            sp.wait_ge(s["t_s"], t * H + (g - 1) * HJ)
                        for j in range(HJ):
                            r = slice(j * HP, (j + 1) * HP)
                            sp.dma_start(kz[g % 2][r, j * T:(j + 1) * T], k_t[r, g, :]
                                         ).then_inc(s["kz_odd" if g % 2 else "kz_even"], 16)
                    sp.wait_ge(s["t_xd"], t * LT + 1)
                    sp.dma_start(gate[:, 0, :], mods_d[l, b, 2 * C:3 * C].partition_broadcast(P)).then_inc(s["l_gate"], 16)
                sp.wait_ge(s["t_xd"], (l + 1) * B * LT + 1)
                if l + 1 < LAYERS:
                    attention_weights(l + 1)
                ne = len(experts[l])
                with sp.Fori(0, CHUNKS) as c:
                    if l < 2:
                        sp.wait_ge(s["m_upd"], (c * ne + passes[l]) * CT + 2)
                    else:
                        sp.wait_ge(s["z_x"], c * CT + B * LT)
                    for i in range(CB):
                        sp.dma_start(gate[:, i, :], mods_d[l, c * CB + i, 5 * C:6 * C].partition_broadcast(P)
                                     ).then_inc(s["l_gate"], 16)
                sp.wait_ge(s["m_upd"], passes[l + 1] * CT + 2)
                if l + 1 < LAYERS:
                    mlp_weights(4 + l)
            sp.wait_ge(s["z_x"], 2 * B * LT)
            sp.dma_start(a["out"].rearrange("b (l p) c -> p (b l) c", p=P), x_sb[:, 0:B * LT, :]).then_inc(s["l_out"], 16)
            sp.wait_ge(s["l_out"], 16)

        mlp_loads = [[0], [1], [2, 3, 4, 5]]

        @block.gpsimd
        def _(pool):
            pool.memset(ident[:], 0.0).then_inc(s["c_ident"], 1)
            pool.memset(smask, 1.0).then_inc(s["c_ident"], 1)
            pool.wait_ge(s["c_ident"], 2)
            pool.affine_select(out=ident[:], in_=ident[:], compare_op=ALU.not_equal, fill=1.0, base=0,
                               pattern=[[-1, P]], channel_multiplier=1).then_inc(s["c_init"], 1)
            pool.affine_select(out=smask, in_=smask, compare_op=ALU.is_gt, fill=0.0, base=0,
                               pattern=[[1, D]], channel_multiplier=-1).then_inc(s["c_init"], 1)
            pool.memset(x_sb[:, B * LT:, :], 0.0).then_inc(s["c_init"], 1)
            pool.memset(wq[:], 0.0).then_inc(s["c_init"], 1)
            pool.memset(wk[:], 0.0).then_inc(s["c_init"], 1)
            pool.memset(v_sb[:], 0.0).then_inc(s["c_init"], 1)
            pool.memset(nmax[:], 0.0).then_inc(s["c_init"], 1)
            pool.memset(bqk[:], 0.0).then_inc(s["c_init"], 1)
            pool.memset(aup, 0.0).then_inc(s["c_init"], 1)
            pool.memset(vt_q, 0.0).then_inc(s["c_init"], 1)
            pool.memset(mod_t[:], 0.0).then_inc(s["c_init"], 1)
            pool.memset(sc_small[:], 0.0).then_inc(s["c_init"], 1)
            for l in range(LAYERS):
                if l == 0:
                    pool.wait_ge(s["z_x"], LT * B)
                else:
                    pool.wait_ge(s["m_upd"], passes[l] * CT + 2)
                for tile in kz:
                    pool.memset(tile, 0.0).then_inc(s["kz_zero"], 1)

        @block.scalar
        def _(act):
            act.wait_ge(s["c_init"], N_INIT)
            act.wait_ge(s["l_cond"], 16)
            act.activation(silu_sb, cond_sb, ACT.Silu).then_inc(s["e_silu"], 1)
            for n in range(12):
                act.wait_ge(s["e_wT"], n + 1)
                act.activation(w0_t[:, n // 4, (n % 4) * 4 * WROWS:(n % 4 + 1) * 4 * WROWS],
                               ps[0:KC, 1 + n % 4, 0:4 * WROWS], ACT.Copy).then_inc(s["e_wTo"], 1)
            for turns, c0 in ((QR_ALONE, 0), (QR_SERIES, QR_C1), (QR_SQUARED, QR_C2)):
                with act.Fori(0, turns) as m:
                    act.activation(unused, zero, ACT.Sqrt)
                    for half in range(2):
                        j = m * 2 + c0 + half
                        act.wait_ge(s["q_vb"], j + 1)
                        act.activation(sq_junk[:, c0:C], ps[0:D, 6 + half, c0:C], ACT.Square, accum_out=sn).then_inc(s["q_sn"], 1)
                        act.wait_ge(s["q_sn"], j + 1)
                        act.activation(y0, sn, ACT.Sqrt, bias=tiny, scale=1.0).then_inc(s["q_sq"], 1)
            act.wait_ge(s["q_rt"], 1)
            act.activation(ddv, ddv, ACT.Sqrt).then_inc(s["q_rtd"], 1)
            with act.Fori(0, B // 2) as pair:
                for u in range(2):
                    act.wait_ge(s["z_xT"], pair * 2 + u + 1)
                    for k in range(KT):
                        last = act.activation(l0_x[u][:, k, :], l0_ps(u, k), ACT.Copy)
                    last.then_inc(s["z_xTo"], 1)
                for u in range(2):
                    act.wait_ge(s["z_z"], pair * 2 + u + 1)
                    act.activation(l0_z[u], ps[0:D, 2 + u, 0:T], ACT.Copy).then_inc(s["z_zo"], 1)
                for u in range(2):
                    act.wait_ge(s["z_zr"], pair * 2 + u + 1)
                    act.activation(l0_zr[u], ps[0:D, 4 + u, 0:T], ACT.Copy).then_inc(s["z_zro"], 1)

            def modulate(l, phase, unit, idx, cb):
                act.wait_ge(s["n_T"], unit + 1)
                for k in range(KT):
                    last = act.activation(h_t[0:KC, k, cb * T:(cb + 1) * T], hps(k), ACT.Identity,
                                          bias=mod_t[:, l, 2 * phase, k, bass.ds(idx, 1)],
                                          scale=mod_t[:, l, 2 * phase + 1, k, bass.ds(idx, 1)])
                last.then_inc(s["n_h"], 1)

            for l in range(LAYERS):
                if l == 0:
                    act.wait_ge(s["e_modTo"], 2 * LAYERS)
                    act.wait_ge(s["l_mods"], 16 * LAYERS)
                act.wait_ge(s["l_bqk"], 16 * 2 * HJ * (l + 1))
                modulate(l, 0, units_a[l], 0, 0)

                def output_transposed(t):
                    act.wait_ge(s["t_oT"], t + 1)
                    for k in range(KT):
                        last = act.activation(o_t[0:KC, k, :], hps(k), ACT.Copy)
                    last.then_inc(s["t_oTe"], 1)

                def turn(b, first):
                    t = b + l * B
                    for half in range(2):
                        for which, tile, rounded in ((0, q_t, q_r[:]), (1, k_t, k_r[:])):
                            act.wait_ge(s["t_qk"], t * 4 + half * 2 + which + 1)
                            for g in (2 * half, 2 * half + 1):
                                for to in (rounded, tile):
                                    last = act.activation(to[:, g, :], ps[:, 2 + 2 * which + half, (g % 2) * T:(g % 2 + 1) * T],
                                                          ACT.Identity, bias=bqk[:, which, g:g + 1], scale=1.0)
                            last.then_inc(s["t_qe"], 1)
                            if half == 1 and which == 0 and not first:
                                output_transposed(t - 1)
                    for lt in range(LT):
                        act.wait_ge(s["t_v"], t * LT + lt + 1)
                        act.activation(v_sb[:, lt, :, 0:HD], ps[:, 6 + lt, 0:C].rearrange("p (h d) -> p h d", h=H), ACT.Copy
                                       ).then_inc(s["t_ve"], 1)
                    for h in range(H):
                        act.wait_ge(s["t_s"], t * H + h + 1)
                        if h >= PSLOTS:
                            act.wait_ge(s["t_pv"], t * H + h - PSLOTS + 1)
                        act.activation(p_t[:, h % PSLOTS, :, :], ps[:, 2 + h % HJ, :].rearrange("p (m t) -> p m t", m=LT),
                                       ACT.Exp, scale=SCALE).then_inc(s["t_exp"], 1)
                        if h == NEXT_AT + 1:
                            modulate(l, 0, b + units_a[l] + 1, b + 1, 0)
                        if h == H // 2 + 3:
                            act.wait_ge(s["t_pv"], t * H + H // 2)
                            act.activation(o_pad[:, 0:2, :].rearrange("p g t -> p (g t)"), ps[:, 6, :], ACT.Copy
                                           ).then_inc(s["t_pve"], 1)
                    act.wait_ge(s["t_pv"], t * H + H)
                    act.activation(o_pad[:, 2:4, :].rearrange("p g t -> p (g t)"), ps[:, 7, :], ACT.Copy
                                   ).then_inc(s["t_pve"], 1)

                turn(0, True)
                with act.Fori(1, B) as b:
                    turn(b, False)
                output_transposed((l + 1) * B - 1)
                ne = len(experts[l])
                for n in mlp_loads[l]:
                    act.wait_ge(s[f"l_mlpw{n}"], 16 * MLP_DMAS)
                for i in range(CB):
                    modulate(l, 1, units_m[l] + i, i, i)
                with act.Fori(0, CHUNKS) as c:
                    if l == 2:
                        act.wait_ge(s["m_lg"], c + 1)
                        act.activation(lg4, ps[0:E, 7, :], ACT.Copy).then_inc(s["m_lge"], 1)
                        act.wait_ge(s["m_cw"], c + 1)
                        act.activation(gm[:, 5, :, 0], gm[:, 4, :, 0], ACT.Tanh, scale=0.5).then_inc(s["m_tanh"], 1)
                    for ei, e in enumerate(experts[l]):
                        n = c * ne + passes[l] + ei
                        for m in range(FT):
                            act.wait_ge(s["m_f1"], n * FT + m + 1)
                            act.activation(mid[:, m, :], ps[:, 2 + m % 3, :], ACT.Gelu_apprx_tanh,
                                           bias=b1_sb[:, e, m:m + 1], scale=1.0).then_inc(s["m_gelu"], 1)
                    for i in range(CB):
                        modulate(l, 1, c * CB + units_m[l] + CB + i, c * CB + CB + i, i)

        @block.vector
        def _(dve):
            V = nc.vector
            chain = {"base": 0, "n": 0}

            def link(ins):
                chain["n"] += 1
                ins.then_inc(s["d_chain"], 1)
                dve.wait_ge(s["d_chain"], chain["base"] + chain["n"])

            class Turns:
                def __init__(self, n, per):
                    self.n, self.per = n, per

                def __enter__(self):
                    self.start = chain["base"] + chain["n"]
                    self.loop = dve.Fori(0, self.n)
                    i = self.loop.__enter__()
                    chain["base"], chain["n"] = i * self.per + self.start, 0
                    return i

                def __exit__(self, *e):
                    if e[0] is None:
                        assert chain["n"] == self.per, (chain["n"], self.per)
                    r = self.loop.__exit__(*e)
                    chain["base"], chain["n"] = self.start + self.n * self.per, 0
                    return r

            dve.wait_ge(s["c_init"], N_INIT)
            V.memset(v_sb[:, :, :, HD:HD + 1], 1.0).then_inc(s["c_fix"], 1)
            V.memset(tiny, 1e-36).then_inc(s["c_fix"], 1)
            link(V.tensor_reduce(kone[:], ident[:, ONE::HP], AX.X, ALU.add))
            V.tensor_scalar(bqk[:, 1, :], bqk[:, 1, :], kone[:, 0:1], None, ALU.add).then_inc(s["c_fix"], 1)
            V.memset(o_t[KC:KC + 1, :, :], 1.0).then_inc(s["c_fix"], 1)
            V.memset(h_t[KC:KC + 1, :, :], 1.0).then_inc(s["c_fix"], 1)
            V.memset(cmp_[:], 0.0).then_inc(s["c_fix"], 1)
            for b in range(B):
                last = V.tensor_copy(ident8[:, b * D:(b + 1) * D], ident[0:D, 0:D])
            last.then_inc(s["c_fix"], 1)
            dve.sem_inc(s["t_xd"], 1)
            dve.sem_inc(s["m_upd"], 2)

            dve.wait_ge(s["e_sT"], 1)
            V.tensor_copy(s_t[:], ps[0:KC, 0, 0:KT * B].rearrange("p (k b) -> p k b", k=KT)).then_inc(s["e_sTo"], 1)
            dve.wait_ge(s["l_b0"], 16)
            for q in range(4):
                dve.wait_ge(s["e_v"], q + 1)
                V.tensor_tensor(v0[:, q * 504:(q + 1) * 504], ps[0:B, 1 + q, 0:504], bias_b[:, q * 504:(q + 1) * 504],
                                ALU.add).then_inc(s["e_vo"], 1)

            def ada(l):
                dve.wait_ge(s["l_ab"], 16 * (l + 1))
                if l:
                    dve.wait_ge(s["l_mods"], 16 * l)
                for q in range(4):
                    dve.wait_ge(s["e_mod"], 4 * l + q + 1)
                    V.tensor_tensor(mods_sb[:, q * 432:(q + 1) * 432], ps[0:B, 1 + q, 0:432],
                                    bias_b[:, q * 432:(q + 1) * 432], ALU.add).then_inc(s["e_modo"], 1)
                dve.wait_ge(s["e_modT"], l + 1)
                mp = ps[0:KC, 5, 0:4 * KT * B].rearrange("p (a k b) -> p a k b", a=4, k=KT)
                for a_ in range(4):
                    last = V.tensor_scalar(mod_t[:, l, a_, :, 0:B], mp[:, a_, :, :], float(a_ % 2), None, ALU.add)
                    if a_ % 2:
                        last.then_inc(s["e_modTo"], 1)

            dve.wait_ge(s["q_pT"], 1)
            V.tensor_copy(at_q, ps[0:D, 0, 0:C]).then_inc(s["q_at"], 1)
            V.tensor_copy(esel, ident[0:D, 0:1]).then_inc(s["q_at"], 1)

            def qr_step(j, half, c0=0):
                vb = ps[0:D, 6 + half, c0:C]
                pj = bass.ds(j, 1)
                dve.wait_ge(s["q_sn"], j + 1)
                V.tensor_copy(rcol, at_q[:, pj])
                V.tensor_tensor_reduce(dot_junk[:, c0:C], vb, at_q[:, c0:C], 1.0, 0.0, ALU.mult, ALU.add, sdot)
                V.tensor_copy(piv, ps[0:D, 6 + half, pj])
                link(V.tensor_scalar(sgnh, ps[0:D, 6 + half, pj], 0.0, -0.5, ALU.is_ge, ALU.add))
                dve.wait_ge(s["q_sq"], j + 1)
                link(V.reciprocal(ry, y0))
                V.tensor_scalar(sng, sn, 1e-36, None, ALU.max)
                V.tensor_tensor(pivh, sgnh, piv, ALU.mult)
                V.tensor_tensor(rcolh, sgnh, rcol, ALU.mult)
                link(V.scalar_tensor_tensor(nb2, sn, ry, y0, ALU.mult, ALU.add))
                link(V.scalar_tensor_tensor(dd, pivh, nb2, sng, ALU.mult, ALU.add))
                V.scalar_tensor_tensor(uu, rcolh, nb2, sdot, ALU.mult, ALU.add)
                link(V.reciprocal(rdd, dd))
                link(V.tensor_scalar(ww, uu, rdd, -1.0, ALU.mult, ALU.mult))
                V.tensor_scalar(ps[0:D, 6 + half, pj], piv, 0.0, None, ALU.mult)
                V.tensor_copy(esel, ident[0:D, bass.ds(j + 1, 1)])
                V.tensor_scalar(at_q[:, pj], rcol, 0.0, None, ALU.mult)
                link(V.scalar_tensor_tensor(vpiv, sgnh, nb2, piv, ALU.mult, ALU.add))
                V.scalar_tensor_tensor(at_q[:, c0:C], vb, ww, at_q[:, c0:C], ALU.mult, ALU.add).then_inc(s["q_at"], 1)
                V.scalar_tensor_tensor(vt_q[:, c0:C], vb, ident[0:D, pj], vt_q[:, c0:C], ALU.mult, ALU.add)
                V.scalar_tensor_tensor(nbv, vpiv, ident[0:D, pj], nbv, ALU.mult, ALU.add)
                link(V.scalar_tensor_tensor(ddv, dd, ident[0:D, pj], ddv, ALU.mult, ALU.add))

            QR_LINKS = 2 * 8
            with Turns(QR_ALONE, QR_LINKS) as m:
                for half in range(2):
                    qr_step(m * 2 + half, half)

            ada(0)

            dve.wait_ge(s["l_aup"], 16 * (D - 1))
            dve.wait_ge(s["x_up"], 1)
            link(V.tensor_tensor(ant, ps[0:D, 3, :], aup, ALU.subtract))
            V.tensor_reduce(nrow, ant.rearrange("p (b d) -> p b d", b=B), AX.X, ALU.add, apply_absolute_value=True
                            ).then_inc(s["x_ant"], 1)
            dve.wait_ge(s["x_nr"], 1)
            link(V.tensor_reduce(nmx8, ps[0:B, 4, 0:D], AX.X, ALU.max))
            V.tensor_scalar(nrep, silu_sb[:, 0:D], 0.0, nmx8, ALU.mult, ALU.add).then_inc(s["x_ant"], 1)
            dve.wait_ge(s["x_nr"], 2)
            link(V.tensor_copy(cur, ps[0:D, 4, 0:B]))
            link(V.tensor_copy(cur2, cur))
            link(V.tensor_scalar(esc, cur, 0.0, 1.0, ALU.mult, ALU.add))
            with Turns(SQUARINGS, 3):
                link(V.tensor_scalar(eflag, cur, EXP_NORM, -0.5, ALU.is_gt, ALU.mult))
                link(V.scalar_tensor_tensor(cur, eflag, 1.0, cur, ALU.add, ALU.mult))
                link(V.scalar_tensor_tensor(esc, eflag, 1.0, esc, ALU.add, ALU.mult))
            for b in range(B):
                last = V.tensor_scalar(ant[:, b * D:(b + 1) * D], ant[:, b * D:(b + 1) * D], esc[:, b:b + 1], None, ALU.mult)
            link(last)
            link(V.memset(kcol, float(TAYLOR)))
            V.tensor_copy(ex, ident8).then_inc(s["x_ho"], 1)
            with Turns(QR_SERIES, QR_LINKS + 2) as i:
                for half in range(2):
                    qr_step((i + QR_ALONE) * 2 + half, half, QR_C1)
                link(V.reciprocal(krec, kcol))
                link(V.tensor_scalar(kcol, kcol, -1.0, None, ALU.add))
                dve.wait_ge(s["x_h"], i + 1)
                V.scalar_tensor_tensor(ex, ps[0:D, 3, :], krec, ident8, ALU.mult, ALU.add).then_inc(s["x_ho"], 1)
            dve.wait_ge(s["x_rT"], 1)
            V.tensor_copy(ex_t, ps[0:D, 4, :]).then_inc(s["x_sqo"], 1)

            ada(1)

            def square(i):
                dve.wait_ge(s["x_sqo"], i + 1)
                link(V.tensor_scalar(emask[:], cur2, EXP_NORM, None, ALU.is_gt))
                mask = emask[:].unsqueeze(2).broadcast_to((D, B, D))
                dve.wait_ge(s["x_sq"], i * 2 + 2)
                halved = V.tensor_scalar(cur2, cur2, 0.5, None, ALU.mult)
                V.copy_predicated(ex.rearrange("p (b d) -> p b d", b=B), mask,
                                  ps[0:D, 3, :].rearrange("p (b d) -> p b d", b=B))
                V.copy_predicated(ex_t.rearrange("p (b d) -> p b d", b=B), mask,
                                  ps[0:D, 4, :].rearrange("p (b d) -> p b d", b=B)).then_inc(s["x_sqo"], 1)
                link(halved)

            with Turns(QR_SQUARED, QR_LINKS + 2) as i:
                for half in range(2):
                    qr_step((i + QR_ALONE + QR_SERIES) * 2 + half, half, QR_C2)
                square(i)
            with Turns(SQUARINGS - QR_SQUARED, 2) as i:
                square(i + QR_SQUARED)
            dve.wait_ge(s["x_sqo"], SQUARINGS + 1)
            link(V.tensor_tensor(ex, ex, ident8, ALU.subtract))
            link(V.scalar_tensor_tensor(vt_q[:, 0:D], ident[0:D, 0:D], nbv, vt_q[:, 0:D], ALU.mult, ALU.add))
            V.reciprocal(ddv, ddv).then_inc(s["q_rt"], 1)
            dve.wait_ge(s["q_rtd"], 1)
            V.tensor_scalar(vt_q, vt_q, ddv, None, ALU.mult).then_inc(s["q_vTo"], 1)
            dve.wait_ge(s["q_vT"], 1)
            V.tensor_copy(v_nat, ps[0:KC, 0, 0:KT * D].rearrange("p (k d) -> p k d", k=KT)).then_inc(s["q_vTo"], 1)
            dve.wait_ge(s["q_g"], 1)
            gq = ps[0:D, 1, 0:D]
            link(V.tensor_tensor(nscr, gq, ident[0:D, 0:D], ALU.mult))
            link(V.tensor_reduce(dg, nscr, AX.X, ALU.add))
            link(V.tensor_scalar(dg, dg, 0.5, None, ALU.mult))
            link(V.reciprocal(rd, dg))
            link(V.scalar_tensor_tensor(nn, gq, rd, smask, ALU.mult, ALU.mult))
            V.tensor_scalar(vd1, vt_q[:, 0:D], rd, None, ALU.mult).then_inc(s["q_no"], 1)
            dve.wait_ge(s["q_n"], 1)
            link(V.tensor_copy(nnt, ps[0:D, 1, 0:D]))
            V.tensor_tensor(pmt, ident[0:D, 0:D], nnt, ALU.subtract).then_inc(s["q_no"], 1)
            for r in range(5):
                dve.wait_ge(s["q_n"], 2 + 2 * r)
                V.tensor_copy(nsm[:, 0:2 * D], ps[0:D, 1, 0:2 * D]).then_inc(s["q_no"], 1)
                dve.wait_ge(s["q_n"], 3 + 2 * r)
                V.tensor_tensor(pmt, ps[0:D, 2, 0:D], pmt, ALU.add).then_inc(s["q_no"], 1)
            dve.wait_ge(s["q_u"], 1)
            V.tensor_copy(tv1, ps[0:D, 1, 0:D]).then_inc(s["q_uo"], 1)
            dve.wait_ge(s["q_u"], 2)
            link(V.tensor_scalar(u_t, ps[0:D, 2, 0:C], -1.0, None, ALU.mult))
            V.tensor_tensor(u_t[:, 0:D], u_t[:, 0:D], ident[0:D, 0:D], ALU.add).then_inc(s["q_uo"], 1)
            dve.wait_ge(s["q_u"], 3)
            V.tensor_copy(u_nat, ps[0:KC, 0, 0:KT * D].rearrange("p (k d) -> p k d", k=KT)).then_inc(s["q_uo"], 1)

            ada(2)

            dve.wait_ge(s["l_x"], 16)

            def l0_in(pair):
                for u in range(2):
                    b = pair * 2 + u
                    V.tensor_copy(xn[:, u * LT:(u + 1) * LT, :], x_sb[:, bass.ds(b * LT, LT), :]).then_inc(s["z_in"], 1)
                for u in range(2):
                    V.tensor_copy(rmi[u][:, 0:D], ex[:, bass.ds((pair * 2 + u) * D, D)])
                    V.tensor_copy(rmi[u][:, D:P], ex[:, bass.ds((pair * 2 + u) * D, D)]).then_inc(s["z_rm"], 1)

            with dve.Fori(0, B // 2) as pair:
                l0_in(pair)
                for u in range(2):
                    for lt in range(LT):
                        b = pair * 2 + u
                        dve.wait_ge(s["z_d"], b * LT + lt + 1)
                        xt = x_sb[:, bass.ds(b * LT + lt, 1), :].rearrange("p o c -> p (o c)")
                        V.tensor_tensor(xt, ps[:, 6 * u + lt, 0:C], xt, ALU.add).then_inc(s["z_x"], 1)
            dve.wait_ge(s["z_x"], LT * B)

            def layer_norm(tile, n, unit):
                dm, m2, q, v, y, y2, z, nmr = [ln[:, i, 0:n] for i in range(8)]
                for i in range(n):
                    ins = V.bn_stats(st[:, i, :], x_sb[:, bass.ds(tile + i, 1), :].rearrange("p o c -> p (o c)"))
                link(ins)
                link(V.tensor_tensor(dm, st[:, 0:n, 1], st[:, 0:n, 4], ALU.subtract))
                link(V.tensor_tensor(m2, st[:, 0:n, 1], st[:, 0:n, 4], ALU.add))
                link(V.tensor_tensor(q, st[:, 0:n, 2], st[:, 0:n, 5], ALU.add))
                link(V.tensor_tensor(dm, dm, dm, ALU.mult))
                link(V.scalar_tensor_tensor(v, q, 4.0 / C, dm, ALU.mult, ALU.add))
                link(V.tensor_scalar(v, v, 0.25, LN_EPS, ALU.mult, ALU.add))
                link(V.tensor_scalar(y.bitcast(I32), v.bitcast(I32), -0.5, RSQRT_SEED, ALU.mult, ALU.add))
                for _ in range(3):
                    link(V.tensor_tensor(y2, y, y, ALU.mult))
                    link(V.scalar_tensor_tensor(z, v, -0.5, y2, ALU.mult, ALU.mult))
                    link(V.scalar_tensor_tensor(y, z, 1.5, y, ALU.add, ALU.mult))
                link(V.scalar_tensor_tensor(nmr, m2, -0.5, y, ALU.mult, ALU.mult))
                for i in range(n):
                    ins = V.tensor_scalar(xn[:, i, :], x_sb[:, bass.ds(tile + i, 1), :].rearrange("p o c -> p (o c)"),
                                          y[:, i:i + 1], nmr[:, i:i + 1], ALU.mult, ALU.add)
                    if i % LT == LT - 1:
                        ins.then_inc(s["n_xn"], 1)

            LN_LINKS = 18

            for l in range(LAYERS):
                layer_norm(0, LT, units_a[l])

                def normalise(t):
                    for lt in range(LT):
                        dve.wait_ge(s["t_o"], t * LT + lt + 1)
                        op = ps[:, 6 + lt, :].rearrange("p (h e) -> p h e", h=H)
                        link(V.reciprocal(rcp[:, lt, :], op[:, :, ONE]))
                        V.tensor_tensor(o_tok[:, lt, :].rearrange("p (h d) -> p h d", h=H), op[:, :, 0:HD],
                                        rcp[:, lt, :].unsqueeze(2).broadcast_to((P, H, HD)), ALU.mult
                                        ).then_inc(s["t_on"], 1)

                def update(b):
                    t = b + l * B
                    dve.wait_ge(s["l_gate"], (b + l * (B + B)) * 16 + 16)
                    for lt in range(LT):
                        dve.wait_ge(s["t_pr"], t * LT + lt + 1)
                        xt = x_sb[:, bass.ds(b * LT + lt, 1), :].rearrange("p o c -> p (o c)")
                        dve.wait_ge(s["t_xd"], t * LT + lt + 1)
                        link(V.tensor_tensor(upd[:], ps[:, lt, 0:C], gate[:, 0, :], ALU.mult))
                        V.tensor_tensor(xt, xt, upd[:], ALU.add).then_inc(s["t_xd"], 1)

                def turn(b, first):
                    t = b + l * B
                    dve.wait_ge(s["n_T"], b + units_a[l] + 1)
                    layer_norm((b + 1) * LT, LT, b + units_a[l] + 1)
                    if not first:
                        normalise(t - 1)

                    def add_maxima(i):
                        dve.wait_ge(s["t_nm"], t * 2 + i + 1)
                        qq = q_t[:, 2 * i:2 * i + 2, :].rearrange("p g t -> p (g t)")
                        V.tensor_tensor(qq, ps[:, 6 + i, :], qq, ALU.add).then_inc(s["t_nma"], 1)

                    for h in range(H):
                        dve.wait_ge(s["t_mx"], t * H + h + 1)
                        V.tensor_reduce(nmax[:, :, h, ONE], ps[:, max_bank[h], :].rearrange("p (l t) -> p l t", l=LT),
                                        AX.X, ALU.max, negate=True).then_inc(s["t_mxd"], 1)
                        if h == H - 3:
                            add_maxima(0)
                    add_maxima(1)
                    if not first:
                        update(b - 1)

                turn(0, True)
                with Turns(B - 1, LN_LINKS + 2 + 2) as i:
                    turn(i + 1, False)
                normalise((l + 1) * B - 1)
                update(B - 1)
                dve.wait_ge(s["t_xd"], (l + 1) * B * LT + 1)
                ne = len(experts[l])
                dve.wait_ge(s["n_T"], units_a[l] + B + 1)
                layer_norm(0, CT, units_m[l])
                with Turns(CHUNKS, LN_LINKS + (2 * CT if l < 2 else CT + E * CT + GATE_LINKS)) as c:
                    dve.wait_ge(s["n_T"], c * CB + units_m[l] + CB)
                    layer_norm((c + 1) * CT, CT, c * CB + units_m[l] + CB)
                    if l == 2:
                        expert_gates = True
                        dve.wait_ge(s["m_lt"], c + 1)
                        lgt = gm[:, 0, :, :]
                        rank, s1, s2, tmp, m1, m2_ = gm[:, 1, :, :], gm[:, 2, :, :], gm[:, 3, :, :], gm[:, 6, :, :], gm[:, 7, :, 0], gm[:, 8, :, 0]
                        link(V.tensor_copy(lgt, ps[:, 7, 0:CT * E].rearrange("p (i e) -> p i e", i=CT)))
                        for j in range(E):
                            for lo, hi, op in ((0, j, ALU.is_gt), (j + 1, E, ALU.is_ge)):
                                if lo < hi:
                                    lj = lgt[:, :, j:j + 1].broadcast_to((P, CT, hi - lo))
                                    ins = V.tensor_tensor(cmp_[:, :, j, lo:hi], lj, lgt[:, :, lo:hi], op)
                        link(ins)
                        link(V.tensor_reduce(rank, cmp_[:].rearrange("p t j i -> p t i j"), AX.X, ALU.add))
                        link(V.tensor_scalar(s1, rank, 0.0, None, ALU.is_equal))
                        link(V.tensor_scalar(s2, rank, 1.0, None, ALU.is_equal))
                        link(V.tensor_tensor(tmp, s1, s2, ALU.subtract))
                        link(V.tensor_tensor(tmp, tmp, lgt, ALU.mult))
                        V.tensor_reduce(gm[:, 4, :, 0:1], tmp, AX.X, ALU.add).then_inc(s["m_cw"], 1)
                        dve.wait_ge(s["m_tanh"], c + 1)
                        link(V.tensor_tensor(tmp, s1, s2, ALU.subtract))
                        link(V.tensor_tensor(tmp, tmp, gm[:, 5, :, 0:1].broadcast_to((P, CT, E)), ALU.mult))
                        link(V.tensor_tensor(tmp, tmp, s1, ALU.add))
                        link(V.tensor_tensor(tmp, tmp, s2, ALU.add))
                        link(V.tensor_scalar(tmp, tmp, 0.5, None, ALU.mult))
                    if l == 2:
                        dve.wait_ge(s["z_x"], c * CT + B * LT)
                    dve.wait_ge(s["l_gate"], (c * CB + l * 2 * B + B + CB) * 16)
                    for ei, e in enumerate(experts[l]):
                        n = c * ne + passes[l] + ei
                        for m in mlp_loads[l] if ei == 0 else ():
                            dve.wait_ge(s[f"l_mlpw{m}"], 16 * MLP_DMAS)
                        for i in range(CT):
                            dve.wait_ge(s["m_f2"], n * CT + i + 1)
                            src = ps[:, 5 + i % 2, 0:C]
                            xt = x_sb[:, bass.ds(c * CT + i, 1), :].rearrange("p o c -> p (o c)")
                            if l < 2:
                                dve.wait_ge(s["m_upd"], n * CT + i + 2)
                                link(V.tensor_tensor(upd[:], src, b2_sb[:, e, :], ALU.add))
                                link(V.tensor_tensor(upd[:], upd[:], gate[:, i // LT, :], ALU.mult))
                                V.tensor_tensor(xt, xt, upd[:], ALU.add).then_inc(s["m_upd"], 1)
                            else:
                                dve.wait_ge(s["m_upd"], n * CT + i + 2 - CT + 1)
                                if ei == 0:
                                    link(V.tensor_scalar(acc[:, i, :], b2_sb[:, e, :], gm[:, 6, i, e:e + 1], None, ALU.mult))
                                else:
                                    link(V.scalar_tensor_tensor(acc[:, i, :], b2_sb[:, e, :], gm[:, 6, i, e:e + 1],
                                                                acc[:, i, :], ALU.mult, ALU.add))
                                V.scalar_tensor_tensor(acc[:, i, :], src, gm[:, 6, i, e:e + 1], acc[:, i, :], ALU.mult, ALU.add
                                                       ).then_inc(s["m_upd"], 1)
                    if l == 2:
                        dve.wait_ge(s["m_upd"], (c + 1) * ne * CT + passes[l] * CT + 2)
                        for i in range(CT):
                            xt = x_sb[:, bass.ds(c * CT + i, 1), :].rearrange("p o c -> p (o c)")
                            link(V.tensor_tensor(acc[:, i, :], acc[:, i, :], gate[:, i // LT, :], ALU.mult))
                            V.tensor_tensor(xt, xt, acc[:, i, :], ALU.add).then_inc(s["z_x"], 1)
                if l < 2:
                    dve.wait_ge(s["m_upd"], passes[l + 1] * CT + 2)
                    dve.wait_ge(s["n_T"], units_m[l] + CB * (CHUNKS + 1))

        @block.tensor
        def _(pe):
            pe.wait_ge(s["c_init"], N_INIT)
            pe.wait_ge(s["c_fix"], 7)
            pe.wait_ge(s["e_silu"], 1)
            for k in range(KT):
                last = pe.transpose(ps[0:KC, 0, k * B:(k + 1) * B], silu_sb[:, k * KC:(k + 1) * KC], ident[0:B, 0:B])
            last.then_inc(s["e_sT"], 1)
            pe.wait_ge(s["l_w0"], 16)
            for n in range(12):
                if n >= 4:
                    pe.wait_ge(s["e_wTo"], n - 3)
                for i in range(4):
                    last = pe.transpose(ps[0:KC, 1 + n % 4, i * WROWS:(i + 1) * WROWS],
                                        w0_nat[:, (n % 4) * 4 + i, (n // 4) * KC:(n // 4 + 1) * KC], ident[0:WROWS, 0:WROWS])
                last.then_inc(s["e_wT"], 1)
            pe.wait_ge(s["e_wTo"], 12)
            pe.wait_ge(s["e_sTo"], 1)
            for q in range(4):
                for k in range(KT):
                    last = pe.matmul(ps[0:B, 1 + q, 0:504], s_t[:, k, :], w0_t[:, k, q * 504:(q + 1) * 504],
                                     start=(k == 0), stop=(k == KT - 1))
                last.then_inc(s["e_v"], 1)

            def ada(l):
                pe.wait_ge(s["l_aw"], 16 * (l + 1))
                if l == 0:
                    pe.wait_ge(s["e_vo"], 4)
                for q in range(4):
                    for k in range(KT):
                        last = pe.matmul(ps[0:B, 1 + q, 0:432], s_t[:, k, :], ada_w[:, k, q * 432:(q + 1) * 432],
                                         start=(k == 0), stop=(k == KT - 1))
                    last.then_inc(s["e_mod"], 1)
                pe.wait_ge(s["e_modo"], 4 * (l + 1))
                for a_, part in enumerate((0, 1, 3, 4)):
                    for k in range(KT):
                        last = pe.transpose(ps[0:KC, 5, (a_ * KT + k) * B:(a_ * KT + k + 1) * B],
                                            mods_sb[:, part * C + k * KC:part * C + (k + 1) * KC], ident[0:B, 0:B])
                last.then_inc(s["e_modT"], 1)
                pe.wait_ge(s["e_modTo"], 2 * (l + 1))

            pe.wait_ge(s["l_p"], 16)
            for k in range(KT):
                last = pe.transpose(ps[0:D, 0, k * KC:(k + 1) * KC], p_nat[:, k, :], ident[0:KC, 0:KC])
            last.then_inc(s["q_pT"], 1)

            def qr_step(j, half, c0=0):
                pe.wait_ge(s["q_at"], j + 2)
                pe.matmul(ps[:, 6 + half, c0:C], esel.broadcast_to((D, P)), at_q[:, c0:C], start=True, stop=True).then_inc(s["q_vb"], 1)

            with pe.Fori(0, QR_ALONE) as m:
                for half in range(2):
                    qr_step(m * 2 + half, half)

            ada(0)

            pe.wait_ge(s["l_aup"], 16 * (D - 1))
            for b in range(B):
                last = pe.transpose(ps[0:D, 3, b * D:(b + 1) * D], aup[:, b * D:(b + 1) * D], ident[0:D, 0:D])
            last.then_inc(s["x_up"], 1)
            pe.wait_ge(s["x_ant"], 1)
            pe.transpose(ps[0:B, 4, 0:D], nrow, ident[0:D, 0:D]).then_inc(s["x_nr"], 1)
            pe.wait_ge(s["x_ant"], 2)
            pe.matmul(ps[0:D, 4, 0:B], nrep, ident[0:B, 0:B], start=True, stop=True).then_inc(s["x_nr"], 1)
            with pe.Fori(0, QR_SERIES) as i:
                qr_step((i + QR_ALONE) * 2, 0, QR_C1)
                pe.wait_ge(s["x_ho"], i + 1)
                pe.matmul(ps[:, 3, 0:D], ant[:, 0:P], ex[:, 0:D], start=True, stop=True)
                for b in range(1, B):
                    bb = slice(b * D, (b + 1) * D)
                    last = pe.matmul(ps[0:D, 3, bb], ant[:, bb], ex[:, bb], start=True, stop=True)
                last.then_inc(s["x_h"], 1)
                qr_step((i + QR_ALONE) * 2 + 1, 1, QR_C1)
            pe.wait_ge(s["x_ho"], TAYLOR + 1)
            for b in range(B):
                last = pe.transpose(ps[0:D, 4, b * D:(b + 1) * D], ex[:, b * D:(b + 1) * D], ident[0:D, 0:D])
            last.then_inc(s["x_rT"], 1)

            pe.wait_ge(s["x_sqo"], 1)
            ada(1)

            def square(i):
                pe.wait_ge(s["x_sqo"], i + 1)
                pe.matmul(ps[:, 3, 0:D], ex_t[:, 0:P], ex[:, 0:D], start=True, stop=True)
                for b in range(1, B):
                    bb = slice(b * D, (b + 1) * D)
                    last = pe.matmul(ps[0:D, 3, bb], ex_t[:, bb], ex[:, bb], start=True, stop=True)
                last.then_inc(s["x_sq"], 1)

            def square_t():
                for b in range(B):
                    bb = slice(b * D, (b + 1) * D)
                    last = pe.matmul(ps[0:D, 4, bb], ex[:, bb], ex_t[:, bb], start=True, stop=True)
                last.then_inc(s["x_sq"], 1)

            with pe.Fori(0, QR_SQUARED) as i:
                qr_step((i + QR_ALONE + QR_SERIES) * 2, 0, QR_C2)
                square(i)
                qr_step((i + QR_ALONE + QR_SERIES) * 2 + 1, 1, QR_C2)
                square_t()
            with pe.Fori(0, SQUARINGS - QR_SQUARED) as i:
                square(i + QR_SQUARED)
                square_t()
            pe.wait_ge(s["x_sqo"], SQUARINGS + 1)
            pe.wait_ge(s["q_vTo"], 1)
            for k in range(KT):
                last = pe.transpose(ps[0:KC, 0, k * D:(k + 1) * D], vt_q[:, k * KC:(k + 1) * KC], ident[0:D, 0:D])
            last.then_inc(s["q_vT"], 1)
            pe.wait_ge(s["q_vTo"], 2)
            for k in range(KT):
                last = pe.matmul(ps[0:D, 1, 0:D], v_nat[:, k, :], v_nat[:, k, :], start=(k == 0), stop=(k == KT - 1))
            last.then_inc(s["q_g"], 1)
            pe.wait_ge(s["q_no"], 1)
            pe.transpose(ps[0:D, 1, 0:D], nn, ident[0:D, 0:D]).then_inc(s["q_n"], 1)
            for r in range(5):
                pe.wait_ge(s["q_no"], 2 + 2 * r)
                pe.matmul(ps[0:D, 1, 0:D], nnt, nn, start=True, stop=True)
                pe.matmul(ps[0:D, 1, D:2 * D], nn, nnt, start=True, stop=True).then_inc(s["q_n"], 1)
                pe.wait_ge(s["q_no"], 3 + 2 * r)
                pe.matmul(ps[0:D, 2, 0:D], nn, pmt, start=True, stop=True).then_inc(s["q_n"], 1)
            pe.wait_ge(s["q_no"], 12)
            pe.matmul(ps[0:D, 1, 0:D], pmt, vd1, start=True, stop=True).then_inc(s["q_u"], 1)
            pe.wait_ge(s["q_uo"], 1)
            pe.matmul(ps[0:D, 2, 0:C], tv1, vt_q, start=True, stop=True).then_inc(s["q_u"], 1)
            pe.wait_ge(s["q_uo"], 2)
            for k in range(KT):
                last = pe.transpose(ps[0:KC, 0, k * D:(k + 1) * D], u_t[:, k * KC:(k + 1) * KC], ident[0:D, 0:D])
            last.then_inc(s["q_u"], 1)
            pe.wait_ge(s["q_uo"], 3)

            ada(2)

            with pe.Fori(0, B // 2) as pair:
                for u in range(2):
                    pe.wait_ge(s["z_in"], pair * 2 + u + 1)
                    for k in range(KT):
                        for lt in range(LT):
                            last = pe.transpose(l0_ps(u, k)[:, lt * P:(lt + 1) * P], xn[:, u * LT + lt, k * KC:(k + 1) * KC], ident[:])
                    last.then_inc(s["z_xT"], 1)
                for u in range(2):
                    pe.wait_ge(s["z_xTo"], pair * 2 + u + 1)
                    for k in range(KT):
                        last = pe.matmul(ps[0:D, 2 + u, 0:T], u_nat[:, k, :], l0_x[u][:, k, :], start=(k == 0), stop=(k == KT - 1))
                    last.then_inc(s["z_z"], 1)
                for u in range(2):
                    pe.wait_ge(s["z_rm"], pair * 2 + u + 1)
                    pe.wait_ge(s["z_zo"], pair * 2 + u + 1)
                    pe.matmul(ps[:, 4 + u, 0:T], rmi[u], l0_z[u], start=True, stop=True).then_inc(s["z_zr"], 1)
                for u in range(2):
                    pe.wait_ge(s["z_zro"], pair * 2 + u + 1)
                    for lt in range(LT):
                        pe.matmul(ps[:, 6 * u + lt, 0:C], l0_zr[u][:, lt * P:(lt + 1) * P], u_t, start=True, stop=True
                                  ).then_inc(s["z_d"], 1)

            def transposes(unit, cb):
                pe.wait_ge(s["n_xn"], unit + 1)
                for k in range(KT):
                    for lt in range(LT):
                        last = pe.transpose(ps[0:KC, k // 2, (k % 2) * T + lt * P:(k % 2) * T + (lt + 1) * P],
                                            xn[:, cb * LT + lt, k * KC:(k + 1) * KC], ident[:])
                last.then_inc(s["n_T"], 1)

            for l in range(LAYERS):
                transposes(units_a[l], 0)
                pe.wait_ge(s["l_attnw"], 16 * ATTN_DMAS * (l + 1))
                if l:
                    pe.wait_ge(s["m_upd"], passes[l] * CT + 2)

                def output(t):
                    pe.wait_ge(s["t_pve"], t * 2 + 2)
                    for lt in range(LT):
                        for g in range(G):
                            last = pe.transpose(ps[:, 6 + lt, g * P:(g + 1) * P], o_pad[:, g, lt * P:(lt + 1) * P], ident[:])
                        last.then_inc(s["t_o"], 1)

                def output_transpose(t):
                    pe.wait_ge(s["t_on"], t * LT + LT)
                    for k in range(KT):
                        for lt in range(LT):
                            last = pe.transpose(ps[0:KC, k // 2, (k % 2) * T + lt * P:(k % 2) * T + (lt + 1) * P],
                                                o_tok[:, lt, k * KC:(k + 1) * KC], ident[:])
                    last.then_inc(s["t_oT"], 1)

                def project(t, lt):
                    pe.wait_ge(s["t_oTe"], t + 1)
                    for k in range(KT):
                        kk = KC + (k == KT - 1)
                        last = pe.matmul(ps[:, lt, 0:C], o_t[0:kk, k, lt * P:(lt + 1) * P], wp[0:kk, k, :],
                                         start=(k == 0), stop=(k == KT - 1))
                    last.then_inc(s["t_pr"], 1)

                def turn(b, first):
                    t = b + l * B

                    def qk(which, g):
                        for k in range(KT):
                            last = pe.matmul(ps[:, 2 + 2 * which + g // 2, (g % 2) * T:(g % 2 + 1) * T],
                                             (wq, wk)[which][:, k, g * HJ:(g + 1) * HJ, :].rearrange("p h d -> p (h d)"),
                                             h_t[0:KC, k, 0:T], start=(k == 0), stop=(k == KT - 1))
                        if g % 2 == 1:
                            last.then_inc(s["t_qk"], 1)

                    def v(lt):
                        for k in range(KT):
                            kk = KC + (k == KT - 1)
                            last = pe.matmul(ps[:, 6 + lt, 0:C], h_t[0:kk, k, lt * P:(lt + 1) * P], wv[0:kk, k, :],
                                             start=(k == 0), stop=(k == KT - 1))
                        last.then_inc(s["t_v"], 1)

                    def scores(*heads):
                        for h in heads:
                            g, r = h // HJ, slice(h % HJ * HP, (h % HJ + 1) * HP)
                            if h == 0 or h == H // 2:
                                pe.wait_ge(s["t_qe"], t * 4 + (2 if h == 0 else 4))
                            if max_before[h] is not None:
                                pe.wait_ge(s["t_mxd"], t * H + max_before[h] + 1)
                            for lt in range(LT):
                                last = pe.matmul(ps[:, max_bank[h], lt * T:(lt + 1) * T], q_r[r, g, lt * P:(lt + 1) * P],
                                                 k_r[r, g, :], start=True, stop=True)
                            last.then_inc(s["t_mx"], 1)

                    def maxima(i):
                        pe.wait_ge(s["t_mxd"], t * H + (i + 1) * H // 2)
                        pe.wait_ge(s["t_ve"], t * LT + i + 1)
                        for g in (2 * i, 2 * i + 1):
                            for lt in range(LT):
                                last = pe.transpose(ps[:, 6 + i, (g % 2) * T + lt * P:(g % 2) * T + (lt + 1) * P],
                                                    nmax[:, lt, g * HJ:(g + 1) * HJ, :].rearrange("p h e -> p (h e)"), ident[:])
                        last.then_inc(s["t_nm"], 1)

                    pe.wait_ge(s["n_h"], b + units_a[l] + 1)
                    qk(0, 0)
                    qk(0, 1)
                    if not first:
                        output(t - 1)
                    qk(1, 0)
                    qk(1, 1)
                    qk(0, 2)
                    scores(0)
                    qk(0, 3)
                    scores(1)
                    if not first:
                        output_transpose(t - 1)
                    qk(1, 2)
                    scores(2, 3)
                    qk(1, 3)
                    scores(4, 5)
                    v(0)
                    scores(6, 7)
                    v(1)
                    scores(8, 9, 10, 11)
                    if not first:
                        project(t - 1, 0)
                    scores(12, 13)
                    maxima(0)
                    if not first:
                        project(t - 1, 1)
                    scores(14, 15)

                    def values(h):
                        g, r = h // HJ, slice(h % HJ * HP, (h % HJ + 1) * HP)
                        pe.wait_ge(s["t_exp"], t * H + h + 1)
                        for m in range(LT):
                            last = pe.matmul(ps[r, 6 + g // 2, (g % 2) * T:(g % 2 + 1) * T], v_sb[:, m, h, :],
                                             p_t[:, h % PSLOTS, m, :], start=(m == 0), stop=(m == LT - 1))
                        last.then_inc(s["t_pv"], 1)

                    for h in range(H):
                        g, j = h // HJ, h % HJ
                        if h % 8 == 0:
                            pe.wait_ge(s["t_nma"], t * 2 + h // 8 + 1)
                        if h >= HJ:
                            pe.wait_ge(s["t_exp"], t * H + h - HJ + 1)
                        else:
                            pe.wait_ge(s["t_mxd"], t * H + H - HJ + h + 1)
                        if j == 0:
                            pe.wait_ge(s["kz_odd" if g % 2 else "kz_even"], (t * 2 + g // 2 + 1) * HJ * 16)
                        for m in range(LT):
                            last = pe.matmul(ps[:, 2 + j, m * T:(m + 1) * T], kz[g % 2][:, j * T + m * P:j * T + (m + 1) * P],
                                             q_t[:, g, :], start=True, stop=True)
                        last.then_inc(s["t_s"], 1)
                        if h == 1:
                            maxima(1)
                        if h >= 2:
                            values(h - 2)
                        if h == NEXT_AT:
                            pe.wait_ge(s["t_xd"], t * LT + 1)
                            transposes(b + units_a[l] + 1, 0)
                    values(H - 2)
                    values(H - 1)

                turn(0, True)
                with pe.Fori(1, B) as b:
                    turn(b, False)
                output((l + 1) * B - 1)
                output_transpose((l + 1) * B - 1)
                for lt in range(LT):
                    project((l + 1) * B - 1, lt)
                ne = len(experts[l])
                pe.wait_ge(s["n_h"], units_a[l] + B + 1)
                pe.wait_ge(s["t_xd"], (l + 1) * B * LT + 1)
                transposes(units_m[l], 0)
                pe.wait_ge(s["n_h"], units_m[l] + 1)
                transposes(units_m[l] + 1, 1)
                for n in mlp_loads[l]:
                    pe.wait_ge(s[f"l_mlpw{n}"], 16 * MLP_DMAS)
                if l == 2:
                    pe.wait_ge(s["l_wg"], 16)
                with pe.Fori(0, CHUNKS) as c:
                    pe.wait_ge(s["n_h"], c * CB + units_m[l] + CB)
                    if l == 2:
                        for k in range(KT):
                            last = pe.matmul(ps[0:E, 7, :], wg_sb[:, k, :], h_t[0:KC, k, :], start=(k == 0), stop=(k == KT - 1))
                        last.then_inc(s["m_lg"], 1)
                        pe.wait_ge(s["m_lge"], c + 1)
                        for i in range(CT):
                            last = pe.matmul(ps[:, 7, i * E:(i + 1) * E], lg4[:, i * P:(i + 1) * P], ident[0:E, 0:E],
                                             start=True, stop=True)
                        last.then_inc(s["m_lt"], 1)
                    for ei, e in enumerate(experts[l]):
                        n = c * ne + passes[l] + ei
                        for m in range(FT):
                            if m >= 3:
                                pe.wait_ge(s["m_gelu"], n * FT + m - 2)
                            for k in range(KT):
                                last = pe.matmul(ps[:, 2 + m % 3, :], w1_sb[e][:, k, m * P:(m + 1) * P], h_t[0:KC, k, :],
                                                 start=(k == 0), stop=(k == KT - 1))
                            last.then_inc(s["m_f1"], 1)
                        if ei == ne - 1:
                            transposes(c * CB + units_m[l] + CB, 0)
                        pe.wait_ge(s["m_gelu"], n * FT + FT)
                        for i in range(CT):
                            pe.wait_ge(s["m_upd"], n * CT + i + 1)
                            for m in range(FT):
                                last = pe.matmul(ps[:, 5 + i % 2, 0:C], mid[:, m, i * P:(i + 1) * P], w2_sb[e][:, m, :],
                                                 start=(m == 0), stop=(m == FT - 1))
                            last.then_inc(s["m_f2"], 1)
                            if ei == ne - 1 and i == 1:
                                pe.wait_ge(s["n_h"], c * CB + units_m[l] + CB + 1)
                                transposes(c * CB + units_m[l] + CB + 1, 1)
                pe.wait_ge(s["n_h"], units_m[l] + CB * (CHUNKS + 1))


GATE_LINKS = 12


_INS = ['x', 'cond_1152', 'L0_cond_P', 'L0_cond_W', 'L0_cond_b', 'L1_cond_W_qkv', 'L1_cond_b_qkv', 'L1_cond_W_proj',
        'L1_cond_b_proj', 'L1_cond_W_fc1', 'L1_cond_b_fc1', 'L1_cond_W_fc2', 'L1_cond_b_fc2', 'L1_cond_W_ada',
        'L1_cond_b_ada', 'L2_cond_qkv_w', 'L2_cond_qkv_b', 'L2_cond_out_w', 'L2_cond_out_b', 'L2_cond_w1',
        'L2_cond_b1', 'L2_cond_w2', 'L2_cond_b2', 'L2_cond_ada_w', 'L2_cond_ada_b', 'L3_cond_w_adaln',
        'L3_cond_b_adaln', 'L3_cond_w_qkv', 'L3_cond_b_qkv', 'L3_cond_w_proj', 'L3_cond_b_proj', 'L3_cond_w_gate',
        'L3_cond_w1', 'L3_cond_b1', 'L3_cond_w2', 'L3_cond_b2']
_OUTS = [((B, T, C), 'float32')]


def kernel(**inputs):
    import numpy as _np
    import concourse.bacc as _bacc
    from concourse import mybir as _mybir
    from concourse.bass_utils import run_bass_kernel_spmd as _run

    nc = _bacc.Bacc("TRN2", target_bir_lowering=False, num_devices=1)
    arrays, args = {}, {}
    for name in _INS:
        a = _np.ascontiguousarray(inputs[name])
        arrays[f"in_{name}_dram"] = a
        args[name] = nc.dram_tensor(f"in_{name}_dram", a.shape, _mybir.dt.from_np(a.dtype), kind="ExternalInput").ap()
    for i, (shape, dtype) in enumerate(_OUTS):
        dt = _mybir.dt.from_np(_np.dtype(dtype))
        args["out"] = nc.dram_tensor(f"out_{i}_dram", shape, dt, kind="ExternalOutput").ap()
    build(nc, args)
    r = _run(nc, [arrays], core_ids=[0])
    got = tuple(r.results[0][f"out_{i}_dram"] for i in range(len(_OUTS)))
    return got[0]
```

```python
from contextlib import ExitStack

import concourse.bass as bass
from concourse import mybir

F32 = mybir.dt.float32
F32R = mybir.dt.float32r
I32 = mybir.dt.int32
ALU = mybir.AluOpType
ACT = mybir.ActivationFunctionType
AX = mybir.AxisListType

B, T, C = 8, 256, 288
P = 128
KC = 96
KT = C // KC
H, HD, HP = 16, 18, 32
G = H * HP // P
HJ = P // HP
LT = T // P
NEXT_AT = 10
PSLOTS = 3
F = 4 * C
FT = F // P
E = 4
LAYERS = 3
D = 64
NSK = D * (D - 1) // 2
CB = 2
CHUNKS = B // CB
CT = CB * LT
CN = CB * T
LN_EPS = 1e-6
SCALE = float(HD) ** -0.5
ONE = HD
WTILE, WROWS = 16, NSK // 16
TAYLOR = 14
EXP_NORM = 2.0
SQUARINGS = 17
QR_ALONE = 8
QR_SERIES = TAYLOR // 2
QR_SQUARED = D // 2 - QR_ALONE - QR_SERIES
assert QR_SQUARED == SQUARINGS
ADA_PIECE = 6 * C // 4
QR_C1, QR_C2 = 2 * QR_ALONE, 2 * (QR_ALONE + QR_SERIES)
RSQRT_SEED = 1597463007.0
MODS = 6 * C
SCRATCH_E = FT * C + KT * F


def build(nc, a):
    ctx = ExitStack()
    with ctx:
        def sb(name, shape, dt=F32):
            return ctx.enter_context(nc.sbuf_tensor(name, shape, dt))

        def sem(name):
            return ctx.enter_context(nc.semaphore(name))

        x_sb = sb("x_sb", [P, B * LT, C])
        wexp = sb("wexp", [P, E * SCRATCH_E])
        wq = sb("wq", [KC, KT, H, HP])
        wk = sb("wk", [KC, KT, H, HP])
        wv = sb("wv", [KC + 1, KT, C])
        wp = sb("wp", [KC + 1, KT, C])
        work = sb("work", [P, FT * CN])
        q_r = sb("q_r", [P, G, T], F32R)
        k_r = sb("k_r", [P, G, T], F32R)
        q_lo = sb("q_lo", [P, G, T], F32R)
        kz = sb("kz", [P, HJ, T], F32R)
        kz_lo = sb("kz_lo", [P, HJ, T], F32R)
        v_sb = sb("v_sb", [P, LT, H, HP])
        nmax = sb("nmax", [P, LT, H, HP])
        o_tok = sb("o_tok", [P, LT, C])
        o_t = sb("o_t", [KC + 1, KT, T])
        xn = sb("xn", [P, CT, C])
        h_t = sb("h_t", [KC + 1, KT, CN])
        acc = sb("acc", [P, CT, C])
        gate = sb("gate", [P, CB, C])
        upd = acc[:, 0, :]
        ident = sb("ident", [P, P])
        mod_t = sb("mod_t", [KC, LAYERS, 4, KT, B])
        bqk = sb("bqk", [P, 2, G])
        kone = sb("kone", [P, 1])
        b1_sb = sb("b1_sb", [P, E, FT])
        b2_sb = sb("b2_sb", [P, E, C])
        wg_sb = sb("wg_sb", [KC, KT, E])
        ln = sb("ln", [P, 12, CT])
        st = sb("st", [P, CT, 6])
        rcp = sb("rcp", [P, LT, H])
        gm = sb("gm", [P, 12, CT, E])
        cmp_ = sb("cmp", [P, CT, E, E])
        s_t = sb("s_t", [KC, KT, B])
        sc_small = sb("sc_small", [D, 26])

        lg4 = o_tok[0:E, :, :].rearrange("p l c -> p (l c)")[:, 0:CN]
        q_t = work[:, 0:G * T].rearrange("p (g t) -> p g t", g=G)
        k_t = work[:, G * T:2 * G * T].rearrange("p (g t) -> p g t", g=G)
        p_t = work[:, 2 * G * T:2 * G * T + PSLOTS * LT * T].rearrange("p (r m t) -> p r m t", r=PSLOTS, m=LT)
        o_at = 2 * G * T + PSLOTS * LT * T
        o_pad = work[:, o_at:o_at + G * T].rearrange("p (g t) -> p g t", g=G)
        assert o_at + G * T <= FT * CN
        mid = work[:, :].rearrange("p (f n) -> p f n", f=FT)
        w1_sb = [wexp[0:KC, e * SCRATCH_E:e * SCRATCH_E + KT * F].rearrange("p (k f) -> p k f", k=KT) for e in range(E)]
        w2_sb = [wexp[:, e * SCRATCH_E + KT * F:(e + 1) * SCRATCH_E].rearrange("p (f c) -> p f c", f=FT) for e in range(E)]

        pos = [SCRATCH_E]

        def early(parts, n):
            v = wexp[0:parts, pos[0]:pos[0] + n]
            pos[0] += n
            assert pos[0] <= E * SCRATCH_E
            return v

        w0_nat = early(WROWS, WTILE * C).rearrange("p (t c) -> p t c", t=WTILE)
        w0_t = early(KC, KT * NSK).rearrange("p (k n) -> p k n", k=KT)
        ada_w = early(KC, KT * MODS).rearrange("p (k n) -> p k n", k=KT)
        bias_b = early(B, NSK)
        v0 = w0_nat[0:B, 0:NSK // C, :].rearrange("p t c -> p (t c)")

        def early2(parts, n, at=[0]):
            v = work[0:parts, at[0]:at[0] + n]
            at[0] += n
            return v

        def square8(v):
            return v.rearrange("p a c -> p (a c)")[:, 0:B * D]

        cond_sb = early2(B, C)
        silu_sb = early2(B, C)
        mods_sb = early2(B, MODS)
        at_q = early2(D, C)
        p_nat = early2(KC, KT * D).rearrange("p (k d) -> p k d", k=KT)
        v_nat = early2(KC, KT * D).rearrange("p (k d) -> p k d", k=KT)
        u_nat = early2(KC, KT * D).rearrange("p (k d) -> p k d", k=KT)
        u_t = early2(D, C)
        vt_q = early2(D, C)
        aup = square8(xn[0:D, 0:2, :])
        ant = square8(xn[0:D, 2:4, :])
        ex = square8(acc[0:D, 0:2, :])
        ex_t = square8(acc[0:D, 2:4, :])
        ident8 = early2(D, B * D)
        smask = early2(D, D)
        nsm = o_tok[0:D, :, :].rearrange("p l c -> p (l c)")
        nn, nnt, pmt, tv1, nscr, vd1 = [nsm[:, i * D:(i + 1) * D] for i in range(6)]
        sq_junk = h_t[0:D, 0, 0:C]
        dot_junk = h_t[0:D, 1, 0:C]
        l0_x = [h_t[0:KC, :, 0:T], o_t[0:KC, :, :]]
        l0_z = [h_t[0:D, 0, T:2 * T], nsm[:, 0:T]]
        l0_zr = [h_t[0:D, 1, T:2 * T], nsm[:, T:2 * T]]
        rmi = [h_t[0:D, 2, T:T + P], gate[0:D, 0, 0:P]]
        q_small = [sc_small[:, i:i + 1] for i in range(26)]
        (esel, piv, rcol, sdot, sn, sng, y0, sgnh, nb2, pivh, dd, vpiv, uu, ww, nbv, ddv, kcol, krec, dg, rd, ry, rdd,
         zero, unused, tiny, rcolh) = q_small[:26]
        e_small = gm[0:D, :, :, :].rearrange("p a b c -> p (a b c)")
        nrow, cur, cur2, esc, eflag = [e_small[:, i * B:(i + 1) * B] for i in range(5)]
        nmx8 = e_small[0:B, 40:41]
        nrep = e_small[0:B, 48:48 + D]
        emask = ctx.enter_context(nc.sbuf_tensor("emask", [D, B], I32))

        ps = ctx.enter_context(nc.psum_tensor("ps", [P, 8, 512], F32))

        mods_d = nc.dram_tensor("mods_scratch", (LAYERS, B, MODS), F32).ap()


        def hps(unit_k):
            return ps[0:KC, unit_k // 2, (unit_k % 2) * T:(unit_k % 2 + 1) * T]

        def l0_ps(u, k):
            return ps[0:KC, 6 * u + k // 2, (k % 2) * T:(k % 2 + 1) * T]

        max_bank = [(2, 4)[h % 2] if h < H // 2 else 2 + h % 4 for h in range(H)]
        max_before = [max([i for i in range(h) if max_bank[i] == max_bank[h]], default=None) for h in range(H)]

        names = """l_x l_p l_w0 l_b0 l_cond l_aw l_ab l_aup l_attnw l_bqk l_mlpw0 l_mlpw1 l_mlpw2 l_mlpw3 l_mlpw4 l_mlpw5 l_gate l_mods l_out l_wg
            m_tanh c_ident c_init c_fix d_chain
            e_silu e_sT e_sTo e_wT e_wTo e_v e_vo e_mod e_modo e_modT e_modTo
            q_pT q_vb q_sn q_sq q_at q_vT q_vTo q_g q_no q_n q_u q_uo q_rt q_rtd
            x_up x_ant x_nr x_nro x_h x_ho x_rT x_sq x_sqo
            z_in z_xT z_xTo z_z z_zo z_zr z_zro z_d z_x z_rm
            n_xn n_T n_h
            t_qk t_qe t_v t_ve t_mx t_mxd t_nm t_nma t_s t_exp t_pv t_pve t_o t_on t_oT t_oTe t_pr t_xd t_lo t_kz t_kzl
            m_f1 m_gelu m_f2 m_upd m_lg m_lge m_lt m_cw""".split()
        s = {n: sem(n) for n in names}
        N_INIT = 13

        block = ctx.enter_context(nc.Block())

        L = [dict(ada="L1_cond_W_ada", adab="L1_cond_b_ada", qkv="L1_cond_W_qkv", qkvb="L1_cond_b_qkv",
                  proj="L1_cond_W_proj", projb="L1_cond_b_proj", w1="L1_cond_W_fc1", b1="L1_cond_b_fc1",
                  w2="L1_cond_W_fc2", b2="L1_cond_b_fc2"),
             dict(ada="L2_cond_ada_w", adab="L2_cond_ada_b", qkv="L2_cond_qkv_w", qkvb="L2_cond_qkv_b",
                  proj="L2_cond_out_w", projb="L2_cond_out_b", w1="L2_cond_w1", b1="L2_cond_b1",
                  w2="L2_cond_w2", b2="L2_cond_b2"),
             dict(ada="L3_cond_w_adaln", adab="L3_cond_b_adaln", qkv="L3_cond_w_qkv", qkvb="L3_cond_b_qkv",
                  proj="L3_cond_w_proj", projb="L3_cond_b_proj", w1="L3_cond_w1", b1="L3_cond_b1",
                  w2="L3_cond_w2", b2="L3_cond_b2")]
        experts = [[0], [1], [0, 1, 2, 3]]
        passes = [CHUNKS * sum(len(experts[i]) for i in range(l)) for l in range(LAYERS + 1)]
        units_a = [l * 2 * B for l in range(LAYERS)]
        units_m = [u + B for u in units_a]
        ATTN_DMAS = 2 * KT + 4
        MLP_DMAS = 4
        order_mlp = [(0, 0, 0), (1, 0, 1), (2, 2, 2), (2, 3, 3), (2, 0, 0), (2, 1, 1)]

        @block.sync
        def _(sp):
            sp.dma_start(cond_sb, a["cond_1152"]).then_inc(s["l_cond"], 16)
            sp.dma_start(p_nat, a["L0_cond_P"].rearrange("(k p) d -> p k d", p=KC)).then_inc(s["l_p"], 16)
            sp.dma_start(w0_nat, a["L0_cond_W"].rearrange("(t p) c -> p t c", p=WROWS)).then_inc(s["l_w0"], 16)
            sp.dma_start(bias_b, a["L0_cond_b"].partition_broadcast(B)).then_inc(s["l_b0"], 16)
            sp.dma_start(ada_w, a[L[0]["ada"]].rearrange("(k p) n -> p k n", p=KC)).then_inc(s["l_aw"], 16)
            sp.dma_start(x_sb[:, 0:B * LT, :], a["x"].rearrange("b (l p) c -> p (b l) c", p=P)).then_inc(s["l_x"], 16)

            def attention_weights(l):
                qkv = a[L[l]["qkv"]]
                for k in range(KT):
                    for which, w in ((0, wq), (1, wk)):
                        sp.dma_start(w[:, k, :, 0:HD],
                                     qkv[k * KC:(k + 1) * KC, which * C:(which + 1) * C].rearrange("p (h d) -> p h d", d=HD)
                                     ).then_inc(s["l_attnw"], 16)
                sp.dma_start(wv[0:KC, :, :], qkv[:, 2 * C:3 * C].rearrange("(k p) n -> p k n", p=KC)).then_inc(s["l_attnw"], 16)
                sp.dma_start(wv[KC:KC + 1, KT - 1, :], a[L[l]["qkvb"]][2 * C:3 * C].rearrange("(o n) -> o n", o=1)
                             ).then_inc(s["l_attnw"], 16)
                sp.dma_start(wp[0:KC, :, :], a[L[l]["proj"]].rearrange("(k p) n -> p k n", p=KC)).then_inc(s["l_attnw"], 16)
                sp.dma_start(wp[KC:KC + 1, KT - 1, :], a[L[l]["projb"]].rearrange("(o n) -> o n", o=1)
                             ).then_inc(s["l_attnw"], 16)
                for j in range(HJ):
                    for which in range(2):
                        src = a[L[l]["qkvb"]][which * C:(which + 1) * C].rearrange("(g j d) -> j d g", g=G, j=HJ)[j]
                        sp.dma_start(bqk[j * HP:j * HP + HD, which, :], src, allow_slow_non_contiguous=True
                                     ).then_inc(s["l_bqk"], 16)

            def mlp_weights(n):
                l, e, buf = order_mlp[n]
                w1, w2, b1, b2 = (a[L[l][n]] for n in ("w1", "w2", "b1", "b2"))
                if l == 2:
                    w1, w2, b1, b2 = w1[e], w2[e], b1[e], b2[e]
                sp.dma_start(w1_sb[buf], w1.rearrange("(k p) f -> p k f", p=KC)).then_inc(s[f"l_mlpw{n}"], 16)
                sp.dma_start(w2_sb[buf], w2.rearrange("(f p) c -> p f c", p=P)).then_inc(s[f"l_mlpw{n}"], 16)
                sp.dma_start(b1_sb[:, buf, :], b1.rearrange("(f p) -> p f", p=P), allow_slow_non_contiguous=True
                             ).then_inc(s[f"l_mlpw{n}"], 16)
                sp.dma_start(b2_sb[:, buf, :], b2.partition_broadcast(P)).then_inc(s[f"l_mlpw{n}"], 16)

            sp.wait_ge(s["c_init"], N_INIT)
            sp.wait_ge(s["e_vo"], 4)
            at = 0
            for i in range(D - 1):
                n = D - 1 - i
                sp.dma_start(aup[i:i + 1, :].rearrange("p (b d) -> p b d", b=B)[:, :, i + 1:D], v0[:, at:at + n],
                             allow_slow_non_contiguous=True).then_inc(s["l_aup"], 16)
                at += n

            sp.dma_start(bias_b[:, 0:MODS], a[L[0]["adab"]].partition_broadcast(B)).then_inc(s["l_ab"], 16)
            sp.wait_ge(s["c_fix"], 2)
            attention_weights(0)
            mlp_weights(0)
            sp.dma_start(wg_sb[:], a["L3_cond_w_gate"].rearrange("(k p) e -> p k e", p=KC)).then_inc(s["l_wg"], 16)

            for l in range(LAYERS):
                if l:
                    sp.wait_ge(s["e_mod"], 4 * l)
                    sp.dma_start(ada_w, a[L[l]["ada"]].rearrange("(k p) n -> p k n", p=KC)).then_inc(s["l_aw"], 16)
                    sp.wait_ge(s["e_modo"], 4 * l)
                    sp.dma_start(bias_b[:, 0:MODS], a[L[l]["adab"]].partition_broadcast(B)).then_inc(s["l_ab"], 16)
                sp.wait_ge(s["e_modo"], 4 * (l + 1))
                sp.dma_start(mods_d[l], mods_sb).then_inc(s["l_mods"], 16)
            sp.wait_ge(s["l_mods"], 16 * LAYERS)
            sp.wait_ge(s["z_d"], LT * B)
            for n in (1, 2, 3):
                mlp_weights(n)

            def store(c):
                sp.dma_start(a["out"].rearrange("b (l p) c -> p (b l) c", p=P)[:, bass.ds(c * CT, CT), :],
                             x_sb[:, bass.ds(c * CT, CT), :]).then_inc(s["l_out"], 16)

            for l in range(LAYERS):
                if l:
                    sp.wait_ge(s["m_upd"], passes[l] * CT + 2)
                with sp.Fori(0, B) as b:
                    t = b + l * B
                    sp.wait_ge(s["t_xd"], t * LT + 1)
                    sp.dma_start(gate[:, 0, :], mods_d[l, b, 2 * C:3 * C].partition_broadcast(P)).then_inc(s["l_gate"], 16)
                sp.wait_ge(s["t_xd"], (l + 1) * B * LT + 1)
                if l + 1 < LAYERS:
                    attention_weights(l + 1)
                ne = len(experts[l])

                def gates(c):
                    if l < 2:
                        sp.wait_ge(s["m_upd"], (c * ne + passes[l]) * CT + 2)
                    else:
                        sp.wait_ge(s["z_x"], c * CT + B * LT)
                    for i in range(CB):
                        sp.dma_start(gate[:, i, :], mods_d[l, c * CB + i, 5 * C:6 * C].partition_broadcast(P)
                                     ).then_inc(s["l_gate"], 16)

                gates(0)
                with sp.Fori(1, CHUNKS) as c:
                    gates(c)
                    if l == 2:
                        store(c - 1)
                sp.wait_ge(s["m_upd"], passes[l + 1] * CT + 2)
                if l + 1 < LAYERS:
                    mlp_weights(4 + l)
            sp.wait_ge(s["z_x"], 2 * B * LT)
            store(CHUNKS - 1)
            sp.wait_ge(s["l_out"], 16 * CHUNKS)

        mlp_loads = [[0], [1], [2, 3, 4, 5]]

        @block.gpsimd
        def _(pool):
            pool.memset(ident[:], 0.0).then_inc(s["c_ident"], 1)
            pool.memset(smask, 1.0).then_inc(s["c_ident"], 1)
            pool.wait_ge(s["c_ident"], 2)
            pool.affine_select(out=ident[:], in_=ident[:], compare_op=ALU.not_equal, fill=1.0, base=0,
                               pattern=[[-1, P]], channel_multiplier=1).then_inc(s["c_init"], 1)
            pool.affine_select(out=smask, in_=smask, compare_op=ALU.is_gt, fill=0.0, base=0,
                               pattern=[[1, D]], channel_multiplier=-1).then_inc(s["c_init"], 1)
            pool.memset(kz[:].bitcast(F32), 0.0).then_inc(s["c_init"], 1)
            pool.memset(kz_lo[:].bitcast(F32), 0.0).then_inc(s["c_init"], 1)
            pool.memset(wq[:], 0.0).then_inc(s["c_init"], 1)
            pool.memset(wk[:], 0.0).then_inc(s["c_init"], 1)
            pool.memset(v_sb[:], 0.0).then_inc(s["c_init"], 1)
            pool.memset(nmax[:], 0.0).then_inc(s["c_init"], 1)
            pool.memset(bqk[:], 0.0).then_inc(s["c_init"], 1)
            pool.memset(aup, 0.0).then_inc(s["c_init"], 1)
            pool.memset(vt_q, 0.0).then_inc(s["c_init"], 1)
            pool.memset(mod_t[:], 0.0).then_inc(s["c_init"], 1)
            pool.memset(sc_small[:], 0.0).then_inc(s["c_init"], 1)

        @block.scalar
        def _(act):
            act.wait_ge(s["c_init"], N_INIT)
            act.wait_ge(s["l_cond"], 16)
            act.activation(silu_sb, cond_sb, ACT.Silu).then_inc(s["e_silu"], 1)
            for n in range(12):
                act.wait_ge(s["e_wT"], n + 1)
                act.activation(w0_t[:, n // 4, (n % 4) * 4 * WROWS:(n % 4 + 1) * 4 * WROWS],
                               ps[0:KC, 1 + n % 4, 0:4 * WROWS], ACT.Copy).then_inc(s["e_wTo"], 1)
            for turns, c0 in ((QR_ALONE, 0), (QR_SERIES, QR_C1), (QR_SQUARED, QR_C2)):
                with act.Fori(0, turns) as m:
                    act.activation(unused, zero, ACT.Sqrt)
                    for half in range(2):
                        j = m * 2 + c0 + half
                        act.wait_ge(s["q_vb"], j + 1)
                        act.activation(sq_junk[:, c0:C], ps[0:D, 6 + half, c0:C], ACT.Square, accum_out=sn
                                       ).then_inc(s["q_sn"], 1)
                        act.wait_ge(s["q_sn"], j + 1)
                        act.activation(y0, sn, ACT.Sqrt, bias=tiny, scale=1.0).then_inc(s["q_sq"], 1)
            act.wait_ge(s["q_rt"], 1)
            act.activation(ddv, ddv, ACT.Sqrt).then_inc(s["q_rtd"], 1)
            with act.Fori(0, B // 2) as pair:
                for u in range(2):
                    act.wait_ge(s["z_xT"], pair * 2 + u + 1)
                    for k in range(KT):
                        last = act.activation(l0_x[u][:, k, :], l0_ps(u, k), ACT.Copy)
                    last.then_inc(s["z_xTo"], 1)
                for u in range(2):
                    act.wait_ge(s["z_z"], pair * 2 + u + 1)
                    act.activation(l0_z[u], ps[0:D, 2 + u, 0:T], ACT.Copy).then_inc(s["z_zo"], 1)
                for u in range(2):
                    act.wait_ge(s["z_zr"], pair * 2 + u + 1)
                    act.activation(l0_zr[u], ps[0:D, 4 + u, 0:T], ACT.Copy).then_inc(s["z_zro"], 1)

            def modulate(l, phase, unit, idx, cb, tiles=range(KT)):
                if tiles[0] == 0:
                    act.wait_ge(s["n_T"], unit + 1)
                for k in tiles:
                    last = act.activation(h_t[0:KC, k, cb * T:(cb + 1) * T], hps(k), ACT.Identity,
                                          bias=mod_t[:, l, 2 * phase, k, bass.ds(idx, 1)],
                                          scale=mod_t[:, l, 2 * phase + 1, k, bass.ds(idx, 1)])
                if k == KT - 1:
                    last.then_inc(s["n_h"], 1)

            for l in range(LAYERS):
                if l == 0:
                    act.wait_ge(s["e_modTo"], 2 * LAYERS)
                    act.wait_ge(s["l_mods"], 16 * LAYERS)
                act.wait_ge(s["l_bqk"], 16 * 2 * HJ * (l + 1))
                if l == 0:
                    modulate(l, 0, units_a[l], 0, 0)

                def output_transposed(t):
                    act.wait_ge(s["t_oT"], t + 1)
                    for k in range(KT):
                        last = act.activation(o_t[0:KC, k, :], hps(k), ACT.Copy)
                    last.then_inc(s["t_oTe"], 1)

                def turn(b, first=False, last_turn=False):
                    t = b + l * B
                    for half in range(2):
                        for which, tile, rounded in ((0, q_t, q_r[:]), (1, k_t, k_r[:])):
                            act.wait_ge(s["t_qk"], t * 4 + half * 2 + which + 1)
                            for g in (2 * half, 2 * half + 1):
                                for to in (rounded, tile):
                                    last = act.activation(to[:, g, :], ps[:, 2 + 2 * which + half, (g % 2) * T:(g % 2 + 1) * T],
                                                          ACT.Identity, bias=bqk[:, which, g:g + 1], scale=1.0)
                            last.then_inc(s["t_qe"], 1)
                            if half == 1 and which == 0 and not first:
                                output_transposed(t - 1)
                    for lt in range(LT):
                        act.wait_ge(s["t_v"], t * LT + lt + 1)
                        act.activation(v_sb[:, lt, :, 0:HD], ps[:, 6 + lt, 0:C].rearrange("p (h d) -> p h d", h=H), ACT.Copy
                                       ).then_inc(s["t_ve"], 1)

                    def spread(h):
                        g, j = h // HJ, h % HJ
                        r = slice(j * HP, (j + 1) * HP)
                        act.activation(kz[r, j, :], k_r[r, g, :], ACT.Copy).then_inc(s["t_kz"], 1)

                    for h in range(HJ):
                        spread(h)
                    for h in range(H):
                        act.wait_ge(s["t_s"], t * H + h + 1)
                        if h >= PSLOTS:
                            act.wait_ge(s["t_pv"], t * H + h - PSLOTS + 1)
                        act.activation(p_t[:, h % PSLOTS, :, :], ps[:, 2 + h % HJ, :].rearrange("p (m t) -> p m t", m=LT),
                                       ACT.Exp, scale=SCALE).then_inc(s["t_exp"], 1)
                        if h + HJ < H:
                            spread(h + HJ)
                        if NEXT_AT < h <= NEXT_AT + KT and not last_turn:
                            modulate(l, 0, b + units_a[l] + 1, b + 1, 0, [h - NEXT_AT - 1])
                        for i in range(CB):
                            if h == NEXT_AT + 1 + 3 * i and last_turn:
                                modulate(l, 1, units_m[l] + i, i, i)
                        if h == H // 2 + 3:
                            act.wait_ge(s["t_pv"], t * H + H // 2)
                            act.activation(o_pad[:, 0:2, :].rearrange("p g t -> p (g t)"), ps[:, 6, :], ACT.Copy
                                           ).then_inc(s["t_pve"], 1)
                    act.wait_ge(s["t_pv"], t * H + H)
                    act.activation(o_pad[:, 2:4, :].rearrange("p g t -> p (g t)"), ps[:, 7, :], ACT.Copy
                                   ).then_inc(s["t_pve"], 1)

                turn(0, first=True)
                with act.Fori(1, B - 1) as b:
                    turn(b)
                turn(B - 1, last_turn=True)
                ne = len(experts[l])
                for n in mlp_loads[l]:
                    act.wait_ge(s[f"l_mlpw{n}"], 16 * MLP_DMAS)

                def chunk(c, first_chunk=False, last_chunk=False):
                    for ei, e in enumerate(experts[l]):
                        n = c * ne + passes[l] + ei
                        for m in range(FT):
                            act.wait_ge(s["m_f1"], n * FT + m + 1)
                            act.activation(mid[:, m, :], ps[:, 2 + m % 3, :], ACT.Gelu_apprx_tanh,
                                           bias=b1_sb[:, e, m:m + 1], scale=1.0).then_inc(s["m_gelu"], 1)
                            if first_chunk and ei == 0 and m == TAIL_T:
                                output_transposed((l + 1) * B - 1)
                            if l == 2 and ei == 0 and m == LOGITS_AT:
                                act.wait_ge(s["m_lg"], c + 1)
                                act.activation(lg4, ps[0:E, 7, :], ACT.Copy).then_inc(s["m_lge"], 1)
                            if l == 2 and ei == 0 and m == FT - 1:
                                act.wait_ge(s["m_cw"], c + 1)
                                act.activation(gm[:, 5, :, 0], gm[:, 4, :, 0], ACT.Tanh, scale=0.5).then_inc(s["m_tanh"], 1)
                    if not last_chunk:
                        for i in range(CB):
                            modulate(l, 1, c * CB + units_m[l] + CB + i, c * CB + CB + i, i)
                    elif l + 1 < LAYERS:
                        modulate(l + 1, 0, units_a[l + 1], 0, 0)

                chunk(0, first_chunk=True)
                with act.Fori(1, CHUNKS - 1) as c:
                    chunk(c)
                chunk(CHUNKS - 1, last_chunk=True)

        @block.vector
        def _(dve):
            V = nc.vector
            chain = {"base": 0, "n": 0}

            def link(ins):
                chain["n"] += 1
                ins.then_inc(s["d_chain"], 1)
                dve.wait_ge(s["d_chain"], chain["base"] + chain["n"])

            def start_link(ins):
                chain["n"] += 1
                ins.then_inc(s["d_chain"], 1)

            def end_link():
                dve.wait_ge(s["d_chain"], chain["base"] + chain["n"])

            class Turns:
                def __init__(self, n, per):
                    self.n, self.per = n, per

                def __enter__(self):
                    self.start = chain["base"] + chain["n"]
                    self.loop = dve.Fori(0, self.n)
                    i = self.loop.__enter__()
                    chain["base"], chain["n"] = i * self.per + self.start, 0
                    return i

                def __exit__(self, *e):
                    if e[0] is None:
                        assert chain["n"] == self.per, (chain["n"], self.per)
                    r = self.loop.__exit__(*e)
                    chain["base"], chain["n"] = self.start + self.n * self.per, 0
                    return r

            dve.wait_ge(s["c_init"], N_INIT)
            V.memset(v_sb[:, :, :, HD:HD + 1], 1.0).then_inc(s["c_fix"], 1)
            V.memset(tiny, 1e-36).then_inc(s["c_fix"], 1)
            link(V.tensor_reduce(kone[:], ident[:, ONE::HP], AX.X, ALU.add))
            V.tensor_scalar(bqk[:, 1, :], bqk[:, 1, :], kone[:, 0:1], None, ALU.add).then_inc(s["c_fix"], 1)
            V.memset(o_t[KC:KC + 1, :, :], 1.0).then_inc(s["c_fix"], 1)
            V.memset(h_t[KC:KC + 1, :, :], 1.0).then_inc(s["c_fix"], 1)
            V.memset(cmp_[:], 0.0).then_inc(s["c_fix"], 1)
            for b in range(B):
                last = V.tensor_copy(ident8[:, b * D:(b + 1) * D], ident[0:D, 0:D])
            last.then_inc(s["c_fix"], 1)
            dve.sem_inc(s["t_xd"], 1)
            dve.sem_inc(s["m_upd"], 2)

            dve.wait_ge(s["e_sT"], 1)
            V.tensor_copy(s_t[:], ps[0:KC, 0, 0:KT * B].rearrange("p (k b) -> p k b", k=KT)).then_inc(s["e_sTo"], 1)
            dve.wait_ge(s["l_b0"], 16)
            for q in range(4):
                dve.wait_ge(s["e_v"], q + 1)
                V.tensor_tensor(v0[:, q * 504:(q + 1) * 504], ps[0:B, 1 + q, 0:504], bias_b[:, q * 504:(q + 1) * 504],
                                ALU.add).then_inc(s["e_vo"], 1)

            def ada_piece(l, q):
                dve.wait_ge(s["e_mod"], q + 4 * l + 1)
                piece = bass.ds(q * ADA_PIECE, ADA_PIECE)
                V.tensor_tensor(mods_sb[:, piece], ps[0:B, 2, 0:ADA_PIECE], bias_b[:, piece], ALU.add).then_inc(s["e_modo"], 1)

            def qr_turns(l, turns, turn, links, each=1):
                with Turns(turns - 4 * each, links) as i:
                    turn(i, lambda: None)
                dve.wait_ge(s["l_ab"], 16 * (l + 1))
                if l:
                    dve.wait_ge(s["l_mods"], 16 * l)
                with Turns(4, each * links) as i:
                    for k in range(each):
                        turn(i * each + (turns - 4 * each + k), (lambda: ada_piece(l, i)) if k == each - 1 else (lambda: None))

            def ada(l):
                dve.wait_ge(s["e_modT"], l + 1)
                mp = ps[0:KC, 5, 0:4 * KT * B].rearrange("p (a k b) -> p a k b", a=4, k=KT)
                for a_ in range(4):
                    last = V.tensor_scalar(mod_t[:, l, a_, :, 0:B], mp[:, a_, :, :], float(a_ % 2), None, ALU.add)
                    if a_ % 2:
                        last.then_inc(s["e_modTo"], 1)

            dve.wait_ge(s["q_pT"], 1)
            V.tensor_copy(at_q, ps[0:D, 0, 0:C]).then_inc(s["q_at"], 1)
            V.tensor_copy(esel, ident[0:D, 0:1]).then_inc(s["q_at"], 1)

            def qr_step(j, half, c0=0):
                vb = ps[0:D, 6 + half, c0:C]
                pj = bass.ds(j, 1)
                dve.wait_ge(s["q_sn"], j + 1)
                V.tensor_copy(rcol, at_q[:, pj])
                V.tensor_tensor_reduce(dot_junk[:, c0:C], vb, at_q[:, c0:C], 1.0, 0.0, ALU.mult, ALU.add, sdot)
                V.tensor_copy(piv, ps[0:D, 6 + half, pj])
                link(V.tensor_scalar(sgnh, ps[0:D, 6 + half, pj], 0.0, -0.5, ALU.is_ge, ALU.add))
                dve.wait_ge(s["q_sq"], j + 1)
                start_link(V.reciprocal(ry, y0))
                V.tensor_scalar(sng, sn, 1e-36, None, ALU.max)
                V.tensor_tensor(pivh, sgnh, piv, ALU.mult)
                end_link()
                start_link(V.scalar_tensor_tensor(nb2, sn, ry, y0, ALU.mult, ALU.add))
                V.tensor_tensor(rcolh, sgnh, rcol, ALU.mult)
                V.tensor_scalar(at_q[:, pj], rcol, 0.0, None, ALU.mult)
                end_link()
                start_link(V.scalar_tensor_tensor(dd, pivh, nb2, sng, ALU.mult, ALU.add))
                V.tensor_scalar(ps[0:D, 6 + half, pj], piv, 0.0, None, ALU.mult)
                end_link()
                start_link(V.reciprocal(rdd, dd))
                V.scalar_tensor_tensor(uu, rcolh, nb2, sdot, ALU.mult, ALU.add)
                start_link(V.scalar_tensor_tensor(vpiv, sgnh, nb2, piv, ALU.mult, ALU.add))
                end_link()
                start_link(V.tensor_scalar(ww, uu, rdd, -1.0, ALU.mult, ALU.mult))
                V.tensor_copy(esel, ident[0:D, bass.ds(j + 1, 1)])
                end_link()
                V.scalar_tensor_tensor(at_q[:, c0:C], vb, ww, at_q[:, c0:C], ALU.mult, ALU.add).then_inc(s["q_at"], 1)
                V.scalar_tensor_tensor(vt_q[:, c0:C], vb, ident[0:D, pj], vt_q[:, c0:C], ALU.mult, ALU.add)
                V.scalar_tensor_tensor(nbv, vpiv, ident[0:D, pj], nbv, ALU.mult, ALU.add)
                link(V.scalar_tensor_tensor(ddv, dd, ident[0:D, pj], ddv, ALU.mult, ALU.add))

            QR_LINKS = 2 * 8

            def alone(m, ada_part):
                for half in range(2):
                    qr_step(m * 2 + half, half)
                    if half == 0:
                        ada_part()

            qr_turns(0, QR_ALONE, alone, QR_LINKS)

            ada(0)

            dve.wait_ge(s["l_aup"], 16 * (D - 1))
            dve.wait_ge(s["x_up"], 1)
            link(V.tensor_tensor(ant, ps[0:D, 3, :], aup, ALU.subtract))
            V.tensor_reduce(nrow, ant.rearrange("p (b d) -> p b d", b=B), AX.X, ALU.add, apply_absolute_value=True
                            ).then_inc(s["x_ant"], 1)
            dve.wait_ge(s["x_nr"], 1)
            link(V.tensor_reduce(nmx8, ps[0:B, 4, 0:D], AX.X, ALU.max))
            V.tensor_scalar(nrep, silu_sb[:, 0:D], 0.0, nmx8, ALU.mult, ALU.add).then_inc(s["x_ant"], 1)
            dve.wait_ge(s["x_nr"], 2)
            link(V.tensor_copy(cur, ps[0:D, 4, 0:B]))
            link(V.tensor_copy(cur2, cur))
            link(V.tensor_scalar(esc, cur, 0.0, 1.0, ALU.mult, ALU.add))
            link(V.tensor_scalar(cur, cur, EXP_NORM * 2.0 ** SQUARINGS, None, ALU.min))
            for k in (16, 8, 4, 2, 1):
                link(V.tensor_scalar(eflag, cur, EXP_NORM * 2.0 ** (k - 1), 2.0 ** -k - 1.0, ALU.is_gt, ALU.mult))
                V.scalar_tensor_tensor(esc, eflag, 1.0, esc, ALU.add, ALU.mult)
                link(V.scalar_tensor_tensor(cur, eflag, 1.0, cur, ALU.add, ALU.mult))
            for b in range(B):
                last = V.tensor_scalar(ant[:, b * D:(b + 1) * D], ant[:, b * D:(b + 1) * D], esc[:, b:b + 1], None, ALU.mult)
            link(last)
            link(V.memset(kcol, float(TAYLOR)))
            V.tensor_copy(ex, ident8).then_inc(s["x_ho"], 1)
            def series(i, ada_part):
                for half in range(2):
                    qr_step((i + QR_ALONE) * 2 + half, half, QR_C1)
                    link(V.reciprocal(krec, kcol))
                    dve.wait_ge(s["x_h"], i * 2 + half + 1)
                    V.scalar_tensor_tensor(ex, ps[0:D, 3, :], krec, ident8, ALU.mult, ALU.add).then_inc(s["x_ho"], 1)
                    link(V.tensor_scalar(kcol, kcol, -1.0, None, ALU.add))
                    if half == 0:
                        ada_part()

            qr_turns(1, QR_SERIES, series, QR_LINKS + 4)
            dve.wait_ge(s["x_rT"], 1)
            V.tensor_copy(ex_t, ps[0:D, 4, :]).then_inc(s["x_sqo"], 1)

            ada(1)

            def square(i):
                dve.wait_ge(s["x_sqo"], i + 1)
                link(V.tensor_scalar(emask[:], cur2, EXP_NORM, None, ALU.is_gt))
                mask = emask[:].unsqueeze(2).broadcast_to((D, B, D))
                dve.wait_ge(s["x_sq"], i * 2 + 2)
                halved = V.tensor_scalar(cur2, cur2, 0.5, None, ALU.mult)
                V.copy_predicated(ex.rearrange("p (b d) -> p b d", b=B), mask,
                                  ps[0:D, 3, :].rearrange("p (b d) -> p b d", b=B))
                V.copy_predicated(ex_t.rearrange("p (b d) -> p b d", b=B), mask,
                                  ps[0:D, 4, :].rearrange("p (b d) -> p b d", b=B)).then_inc(s["x_sqo"], 1)
                link(halved)

            def squared(i, ada_part):
                for half in range(2):
                    qr_step((i + QR_ALONE + QR_SERIES) * 2 + half, half, QR_C2)
                    if half == 0:
                        ada_part()
                square(i)

            qr_turns(2, QR_SQUARED, squared, QR_LINKS + 2, each=KT)
            dve.wait_ge(s["x_sqo"], SQUARINGS + 1)
            link(V.tensor_tensor(ex, ex, ident8, ALU.subtract))
            link(V.scalar_tensor_tensor(vt_q[:, 0:D], ident[0:D, 0:D], nbv, vt_q[:, 0:D], ALU.mult, ALU.add))
            V.reciprocal(ddv, ddv).then_inc(s["q_rt"], 1)
            dve.wait_ge(s["q_rtd"], 1)
            V.tensor_scalar(vt_q, vt_q, ddv, None, ALU.mult).then_inc(s["q_vTo"], 1)
            dve.wait_ge(s["q_vT"], 1)
            V.tensor_copy(v_nat, ps[0:KC, 0, 0:KT * D].rearrange("p (k d) -> p k d", k=KT)).then_inc(s["q_vTo"], 1)
            dve.wait_ge(s["q_g"], 1)
            gq = ps[0:D, 1, 0:D]
            link(V.tensor_tensor(nscr, gq, ident[0:D, 0:D], ALU.mult))
            link(V.tensor_reduce(dg, nscr, AX.X, ALU.add))
            link(V.tensor_scalar(dg, dg, 0.5, None, ALU.mult))
            link(V.reciprocal(rd, dg))
            link(V.scalar_tensor_tensor(nn, gq, rd, smask, ALU.mult, ALU.mult))
            V.tensor_scalar(vd1, vt_q[:, 0:D], rd, None, ALU.mult).then_inc(s["q_no"], 1)
            dve.wait_ge(s["q_n"], 1)
            link(V.tensor_copy(nnt, ps[0:D, 1, 0:D]))
            V.tensor_tensor(pmt, ident[0:D, 0:D], nnt, ALU.subtract).then_inc(s["q_no"], 1)
            for r in range(5):
                dve.wait_ge(s["q_n"], 2 + 2 * r)
                V.tensor_copy(nsm[:, 0:2 * D], ps[0:D, 1, 0:2 * D]).then_inc(s["q_no"], 1)
                dve.wait_ge(s["q_n"], 3 + 2 * r)
                V.tensor_tensor(pmt, ps[0:D, 2, 0:D], pmt, ALU.add).then_inc(s["q_no"], 1)
            dve.wait_ge(s["q_u"], 1)
            V.tensor_copy(tv1, ps[0:D, 1, 0:D]).then_inc(s["q_uo"], 1)
            dve.wait_ge(s["q_u"], 2)
            link(V.tensor_scalar(u_t, ps[0:D, 2, 0:C], -1.0, None, ALU.mult))
            V.tensor_tensor(u_t[:, 0:D], u_t[:, 0:D], ident[0:D, 0:D], ALU.add).then_inc(s["q_uo"], 1)
            dve.wait_ge(s["q_u"], 3)
            V.tensor_copy(u_nat, ps[0:KC, 0, 0:KT * D].rearrange("p (k d) -> p k d", k=KT)).then_inc(s["q_uo"], 1)

            ada(2)

            dve.wait_ge(s["l_x"], 16)

            def l0_in(pair):
                for u in range(2):
                    b = pair * 2 + u
                    V.tensor_copy(xn[:, u * LT:(u + 1) * LT, :], x_sb[:, bass.ds(b * LT, LT), :]).then_inc(s["z_in"], 1)
                for u in range(2):
                    V.tensor_copy(rmi[u][:, 0:D], ex[:, bass.ds((pair * 2 + u) * D, D)])
                    V.tensor_copy(rmi[u][:, D:P], ex[:, bass.ds((pair * 2 + u) * D, D)]).then_inc(s["z_rm"], 1)

            with dve.Fori(0, B // 2) as pair:
                l0_in(pair)
                for u in range(2):
                    for lt in range(LT):
                        b = pair * 2 + u
                        dve.wait_ge(s["z_d"], b * LT + lt + 1)
                        xt = x_sb[:, bass.ds(b * LT + lt, 1), :].rearrange("p o c -> p (o c)")
                        V.tensor_tensor(xt, ps[:, 6 * u + lt, 0:C], xt, ALU.add).then_inc(s["z_x"], 1)
            dve.wait_ge(s["z_x"], LT * B)

            def layer_norm(tile, n, unit):
                dm, m2, q, v, y, y2, z, nmr = [ln[:, i, 0:n] for i in range(8)]
                for i in range(n):
                    ins = V.bn_stats(st[:, i, :], x_sb[:, bass.ds(tile + i, 1), :].rearrange("p o c -> p (o c)"))
                link(ins)
                link(V.tensor_tensor(dm, st[:, 0:n, 1], st[:, 0:n, 4], ALU.subtract))
                link(V.tensor_tensor(m2, st[:, 0:n, 1], st[:, 0:n, 4], ALU.add))
                link(V.tensor_tensor(q, st[:, 0:n, 2], st[:, 0:n, 5], ALU.add))
                link(V.tensor_tensor(dm, dm, dm, ALU.mult))
                link(V.scalar_tensor_tensor(v, q, 4.0 / C, dm, ALU.mult, ALU.add))
                link(V.tensor_scalar(v, v, 0.25, LN_EPS, ALU.mult, ALU.add))
                link(V.tensor_scalar(y.bitcast(I32), v.bitcast(I32), -0.5, RSQRT_SEED, ALU.mult, ALU.add))
                for _ in range(3):
                    link(V.tensor_tensor(y2, y, y, ALU.mult))
                    link(V.scalar_tensor_tensor(z, v, -0.5, y2, ALU.mult, ALU.mult))
                    link(V.scalar_tensor_tensor(y, z, 1.5, y, ALU.add, ALU.mult))
                link(V.scalar_tensor_tensor(nmr, m2, -0.5, y, ALU.mult, ALU.mult))
                for i in range(n):
                    ins = V.tensor_scalar(xn[:, i, :], x_sb[:, bass.ds(tile + i, 1), :].rearrange("p o c -> p (o c)"),
                                          y[:, i:i + 1], nmr[:, i:i + 1], ALU.mult, ALU.add)
                    if i % LT == LT - 1:
                        ins.then_inc(s["n_xn"], 1)

            LN_LINKS = 18

            for l in range(LAYERS):
                if l == 0:
                    layer_norm(0, LT, units_a[l])

                def normalise(t):
                    for lt in range(LT):
                        dve.wait_ge(s["t_o"], t * LT + lt + 1)
                        op = ps[:, 6 + lt, :].rearrange("p (h e) -> p h e", h=H)
                        link(V.reciprocal(rcp[:, lt, :], op[:, :, ONE]))
                        V.tensor_tensor(o_tok[:, lt, :].rearrange("p (h d) -> p h d", h=H), op[:, :, 0:HD],
                                        rcp[:, lt, :].unsqueeze(2).broadcast_to((P, H, HD)), ALU.mult
                                        ).then_inc(s["t_on"], 1)

                def update(b):
                    t = b + l * B
                    dve.wait_ge(s["l_gate"], (b + l * (B + B)) * 16 + 16)
                    for lt in range(LT):
                        dve.wait_ge(s["t_pr"], t * LT + lt + 1)
                        xt = x_sb[:, bass.ds(b * LT + lt, 1), :].rearrange("p o c -> p (o c)")
                        dve.wait_ge(s["t_xd"], t * LT + lt + 1)
                        link(V.tensor_tensor(upd, ps[:, lt, 0:C], gate[:, 0, :], ALU.mult))
                        V.tensor_tensor(xt, xt, upd, ALU.add).then_inc(s["t_xd"], 1)

                def turn(b, first=False, last_turn=False):
                    t = b + l * B
                    dve.wait_ge(s["n_T"], b + units_a[l] + 1)
                    if last_turn:
                        dve.wait_ge(s["t_xd"], (l * B + CB) * LT + 1)
                        layer_norm(0, CT, units_m[l])
                    else:
                        layer_norm((b + 1) * LT, LT, b + units_a[l] + 1)
                    if not first:
                        normalise(t - 1)

                    def add_maxima(i):
                        dve.wait_ge(s["t_nm"], t * 2 + i + 1)
                        qq = q_r[:, 2 * i:2 * i + 2, :].rearrange("p g t -> p (g t)")
                        V.tensor_tensor(qq, ps[:, 6 + i, :], qq, ALU.add).then_inc(s["t_nma"], 1)

                    def query_rests(half):
                        dve.wait_ge(s["t_qe"], t * 4 + half * 2 + 2)
                        gg = slice(2 * half, 2 * half + 2)
                        V.tensor_tensor(q_lo[:, gg, :], q_t[:, gg, :], q_r[:, gg, :], ALU.subtract).then_inc(s["t_lo"], 1)

                    def key_rests(*heads):
                        for h in heads:
                            g, j = h // HJ, h % HJ
                            r = slice(j * HP, (j + 1) * HP)
                            if h >= HJ:
                                dve.wait_ge(s["t_s"], t * H + h - HJ + 1)
                            V.tensor_tensor(kz_lo[r, j, :], k_t[r, g, :], k_r[r, g, :], ALU.subtract).then_inc(s["t_kzl"], 1)

                    for h in range(H):
                        dve.wait_ge(s["t_mx"], t * H + h + 1)
                        V.tensor_reduce(nmax[:, :, h, ONE], ps[:, max_bank[h], :].rearrange("p (l t) -> p l t", l=LT),
                                        AX.X, ALU.max, negate=True).then_inc(s["t_mxd"], 1)
                        if h == 1:
                            query_rests(0)
                        if h == 10:
                            query_rests(1)
                        if h in (3, 5):
                            key_rests(h - 3, h - 2)
                        if h == 9:
                            add_maxima(0)
                    add_maxima(1)
                    key_rests(4, 5, 6, 7)
                    if not first:
                        update(b - 1)
                    key_rests(*range(8, H))

                turn(0, first=True)
                with Turns(B - 2, LN_LINKS + 2 + 2) as i:
                    turn(i + 1)
                turn(B - 1, last_turn=True)
                normalise((l + 1) * B - 1)
                update(B - 1)
                dve.wait_ge(s["t_xd"], (l + 1) * B * LT + 1)
                ne = len(experts[l])

                def chunk(c, last_chunk=False):
                    dve.wait_ge(s["n_T"], c * CB + units_m[l] + CB)
                    if not last_chunk:
                        layer_norm((c + 1) * CT, CT, c * CB + units_m[l] + CB)
                    elif l + 1 < LAYERS:
                        dve.wait_ge(s["m_upd"], passes[l] * CT + CT + 2)
                        layer_norm(0, LT, units_a[l + 1])
                    if l == 2:
                        dve.wait_ge(s["m_lt"], c + 1)
                        lgt = gm[:, 0, :, :]
                        rank, s1, s2, tmp, m1, m2_ = gm[:, 1, :, :], gm[:, 2, :, :], gm[:, 3, :, :], gm[:, 6, :, :], gm[:, 7, :, 0], gm[:, 8, :, 0]
                        link(V.tensor_copy(lgt, ps[:, 7, 0:CT * E].rearrange("p (i e) -> p i e", i=CT)))
                        for j in range(E):
                            for lo, hi, op in ((0, j, ALU.is_gt), (j + 1, E, ALU.is_ge)):
                                if lo < hi:
                                    lj = lgt[:, :, j:j + 1].broadcast_to((P, CT, hi - lo))
                                    ins = V.tensor_tensor(cmp_[:, :, j, lo:hi], lj, lgt[:, :, lo:hi], op)
                        link(ins)
                        link(V.tensor_reduce(rank, cmp_[:].rearrange("p t j i -> p t i j"), AX.X, ALU.add))
                        link(V.tensor_scalar(s1, rank, 0.0, None, ALU.is_equal))
                        link(V.tensor_scalar(s2, rank, 1.0, None, ALU.is_equal))
                        link(V.tensor_tensor(tmp, s1, s2, ALU.subtract))
                        link(V.tensor_tensor(tmp, tmp, lgt, ALU.mult))
                        V.tensor_reduce(gm[:, 4, :, 0:1], tmp, AX.X, ALU.add).then_inc(s["m_cw"], 1)
                        dve.wait_ge(s["m_tanh"], c + 1)
                        link(V.tensor_tensor(tmp, s1, s2, ALU.subtract))
                        link(V.tensor_tensor(tmp, tmp, gm[:, 5, :, 0:1].broadcast_to((P, CT, E)), ALU.mult))
                        link(V.tensor_tensor(tmp, tmp, s1, ALU.add))
                        link(V.tensor_tensor(tmp, tmp, s2, ALU.add))
                        link(V.tensor_scalar(tmp, tmp, 0.5, None, ALU.mult))
                    if l == 2:
                        dve.wait_ge(s["z_x"], c * CT + B * LT)
                    dve.wait_ge(s["l_gate"], (c * CB + l * 2 * B + B + CB) * 16)
                    for ei, e in enumerate(experts[l]):
                        n = c * ne + passes[l] + ei
                        for m in mlp_loads[l] if ei == 0 else ():
                            dve.wait_ge(s[f"l_mlpw{m}"], 16 * MLP_DMAS)
                        for i in range(CT):
                            dve.wait_ge(s["m_f2"], n * CT + i + 1)
                            src = ps[:, 5 + i % 2, 0:C]
                            xt = x_sb[:, bass.ds(c * CT + i, 1), :].rearrange("p o c -> p (o c)")
                            if l < 2:
                                dve.wait_ge(s["m_upd"], n * CT + i + 2)
                                link(V.tensor_tensor(upd, src, b2_sb[:, e, :], ALU.add))
                                link(V.tensor_tensor(upd, upd, gate[:, i // LT, :], ALU.mult))
                                V.tensor_tensor(xt, xt, upd, ALU.add).then_inc(s["m_upd"], 1)
                            else:
                                dve.wait_ge(s["m_upd"], n * CT + i + 2 - CT + 1)
                                if ei == 0:
                                    link(V.tensor_scalar(acc[:, i, :], b2_sb[:, e, :], gm[:, 6, i, e:e + 1], None, ALU.mult))
                                else:
                                    link(V.scalar_tensor_tensor(acc[:, i, :], b2_sb[:, e, :], gm[:, 6, i, e:e + 1],
                                                                acc[:, i, :], ALU.mult, ALU.add))
                                V.scalar_tensor_tensor(acc[:, i, :], src, gm[:, 6, i, e:e + 1], acc[:, i, :], ALU.mult, ALU.add
                                                       ).then_inc(s["m_upd"], 1)
                    if l == 2:
                        dve.wait_ge(s["m_upd"], (c + 1) * ne * CT + passes[l] * CT + 2)
                        for i in range(CT):
                            xt = x_sb[:, bass.ds(c * CT + i, 1), :].rearrange("p o c -> p (o c)")
                            link(V.tensor_tensor(acc[:, i, :], acc[:, i, :], gate[:, i // LT, :], ALU.mult))
                            V.tensor_tensor(xt, xt, acc[:, i, :], ALU.add).then_inc(s["z_x"], 1)

                with Turns(CHUNKS - 1, LN_LINKS + (2 * CT if l < 2 else CT + E * CT + GATE_LINKS)) as c:
                    chunk(c)
                chunk(CHUNKS - 1, last_chunk=True)
                if l < 2:
                    dve.wait_ge(s["m_upd"], passes[l + 1] * CT + 2)

        @block.tensor
        def _(pe):
            pe.wait_ge(s["c_init"], N_INIT)
            pe.wait_ge(s["c_fix"], 7)
            pe.wait_ge(s["e_silu"], 1)
            for k in range(KT):
                last = pe.transpose(ps[0:KC, 0, k * B:(k + 1) * B], silu_sb[:, k * KC:(k + 1) * KC], ident[0:B, 0:B])
            last.then_inc(s["e_sT"], 1)
            pe.wait_ge(s["l_w0"], 16)
            for n in range(12):
                if n >= 4:
                    pe.wait_ge(s["e_wTo"], n - 3)
                for i in range(4):
                    last = pe.transpose(ps[0:KC, 1 + n % 4, i * WROWS:(i + 1) * WROWS],
                                        w0_nat[:, (n % 4) * 4 + i, (n // 4) * KC:(n // 4 + 1) * KC], ident[0:WROWS, 0:WROWS])
                last.then_inc(s["e_wT"], 1)
            pe.wait_ge(s["e_wTo"], 12)
            pe.wait_ge(s["e_sTo"], 1)
            for q in range(4):
                for k in range(KT):
                    last = pe.matmul(ps[0:B, 1 + q, 0:504], s_t[:, k, :], w0_t[:, k, q * 504:(q + 1) * 504],
                                     start=(k == 0), stop=(k == KT - 1))
                last.then_inc(s["e_v"], 1)

            def ada_piece(q, tiles):
                for k in tiles:
                    last = pe.matmul(ps[0:B, 2, 0:ADA_PIECE], s_t[:, k, :], ada_w[:, k, bass.ds(q * ADA_PIECE, ADA_PIECE)],
                                     start=(k == 0), stop=(k == KT - 1))
                if k == KT - 1:
                    last.then_inc(s["e_mod"], 1)

            def qr_turns(l, turns, turn, each=1):
                with pe.Fori(0, turns - 4 * each) as i:
                    turn(i, lambda: None)
                pe.wait_ge(s["l_aw"], 16 * (l + 1))
                if l == 0:
                    pe.wait_ge(s["e_vo"], 4)
                with pe.Fori(0, 4) as i:
                    for k in range(each):
                        tiles = (k,) if each == KT else range(KT)
                        turn(i * each + (turns - 4 * each + k), lambda: ada_piece(i, tiles))

            def ada(l):
                pe.wait_ge(s["e_modo"], 4 * (l + 1))
                for a_, part in enumerate((0, 1, 3, 4)):
                    for k in range(KT):
                        last = pe.transpose(ps[0:KC, 5, (a_ * KT + k) * B:(a_ * KT + k + 1) * B],
                                            mods_sb[:, part * C + k * KC:part * C + (k + 1) * KC], ident[0:B, 0:B])
                last.then_inc(s["e_modT"], 1)
                pe.wait_ge(s["e_modTo"], 2 * (l + 1))

            pe.wait_ge(s["l_p"], 16)
            for k in range(KT):
                last = pe.transpose(ps[0:D, 0, k * KC:(k + 1) * KC], p_nat[:, k, :], ident[0:KC, 0:KC])
            last.then_inc(s["q_pT"], 1)

            def qr_step(j, half, c0=0):
                pe.wait_ge(s["q_at"], j + 2)
                pe.matmul(ps[:, 6 + half, c0:C], esel.broadcast_to((D, P)), at_q[:, c0:C], start=True, stop=True).then_inc(s["q_vb"], 1)

            def alone(m, ada_part):
                for half in range(2):
                    qr_step(m * 2 + half, half)
                    if half == 0:
                        ada_part()

            qr_turns(0, QR_ALONE, alone)

            ada(0)

            pe.wait_ge(s["l_aup"], 16 * (D - 1))
            for b in range(B):
                last = pe.transpose(ps[0:D, 3, b * D:(b + 1) * D], aup[:, b * D:(b + 1) * D], ident[0:D, 0:D])
            last.then_inc(s["x_up"], 1)
            pe.wait_ge(s["x_ant"], 1)
            pe.transpose(ps[0:B, 4, 0:D], nrow, ident[0:D, 0:D]).then_inc(s["x_nr"], 1)
            pe.wait_ge(s["x_ant"], 2)
            pe.matmul(ps[0:D, 4, 0:B], nrep, ident[0:B, 0:B], start=True, stop=True).then_inc(s["x_nr"], 1)
            def series(i, ada_part):
                for half in range(2):
                    qr_step((i + QR_ALONE) * 2 + half, half, QR_C1)
                    pe.wait_ge(s["x_ho"], i * 2 + half + 1)
                    pe.matmul(ps[:, 3, 0:D], ant[:, 0:P], ex[:, 0:D], start=True, stop=True)
                    for b in range(1, B):
                        bb = slice(b * D, (b + 1) * D)
                        last = pe.matmul(ps[0:D, 3, bb], ant[:, bb], ex[:, bb], start=True, stop=True)
                    last.then_inc(s["x_h"], 1)
                    if half == 0:
                        ada_part()

            qr_turns(1, QR_SERIES, series)
            pe.wait_ge(s["x_ho"], TAYLOR + 1)
            for b in range(B):
                last = pe.transpose(ps[0:D, 4, b * D:(b + 1) * D], ex[:, b * D:(b + 1) * D], ident[0:D, 0:D])
            last.then_inc(s["x_rT"], 1)

            pe.wait_ge(s["x_sqo"], 1)
            ada(1)

            def square(i):
                pe.wait_ge(s["x_sqo"], i + 1)
                pe.matmul(ps[:, 3, 0:D], ex_t[:, 0:P], ex[:, 0:D], start=True, stop=True)
                for b in range(1, B):
                    bb = slice(b * D, (b + 1) * D)
                    last = pe.matmul(ps[0:D, 3, bb], ex_t[:, bb], ex[:, bb], start=True, stop=True)
                last.then_inc(s["x_sq"], 1)

            def square_t():
                for b in range(B):
                    bb = slice(b * D, (b + 1) * D)
                    last = pe.matmul(ps[0:D, 4, bb], ex[:, bb], ex_t[:, bb], start=True, stop=True)
                last.then_inc(s["x_sq"], 1)

            def squared(i, ada_part):
                qr_step((i + QR_ALONE + QR_SERIES) * 2, 0, QR_C2)
                square(i)
                ada_part()
                qr_step((i + QR_ALONE + QR_SERIES) * 2 + 1, 1, QR_C2)
                square_t()

            qr_turns(2, QR_SQUARED, squared, each=KT)
            pe.wait_ge(s["x_sqo"], SQUARINGS + 1)
            pe.wait_ge(s["q_vTo"], 1)
            for k in range(KT):
                last = pe.transpose(ps[0:KC, 0, k * D:(k + 1) * D], vt_q[:, k * KC:(k + 1) * KC], ident[0:D, 0:D])
            last.then_inc(s["q_vT"], 1)
            pe.wait_ge(s["q_vTo"], 2)
            for k in range(KT):
                last = pe.matmul(ps[0:D, 1, 0:D], v_nat[:, k, :], v_nat[:, k, :], start=(k == 0), stop=(k == KT - 1))
            last.then_inc(s["q_g"], 1)
            pe.wait_ge(s["q_no"], 1)
            pe.transpose(ps[0:D, 1, 0:D], nn, ident[0:D, 0:D]).then_inc(s["q_n"], 1)
            for r in range(5):
                pe.wait_ge(s["q_no"], 2 + 2 * r)
                pe.matmul(ps[0:D, 1, 0:D], nnt, nn, start=True, stop=True)
                pe.matmul(ps[0:D, 1, D:2 * D], nn, nnt, start=True, stop=True).then_inc(s["q_n"], 1)
                pe.wait_ge(s["q_no"], 3 + 2 * r)
                pe.matmul(ps[0:D, 2, 0:D], nn, pmt, start=True, stop=True).then_inc(s["q_n"], 1)
            pe.wait_ge(s["q_no"], 12)
            pe.matmul(ps[0:D, 1, 0:D], pmt, vd1, start=True, stop=True).then_inc(s["q_u"], 1)
            pe.wait_ge(s["q_uo"], 1)
            pe.matmul(ps[0:D, 2, 0:C], tv1, vt_q, start=True, stop=True).then_inc(s["q_u"], 1)
            pe.wait_ge(s["q_uo"], 2)
            for k in range(KT):
                last = pe.transpose(ps[0:KC, 0, k * D:(k + 1) * D], u_t[:, k * KC:(k + 1) * KC], ident[0:D, 0:D])
            last.then_inc(s["q_u"], 1)
            pe.wait_ge(s["q_uo"], 3)

            ada(2)

            with pe.Fori(0, B // 2) as pair:
                for u in range(2):
                    pe.wait_ge(s["z_in"], pair * 2 + u + 1)
                    for k in range(KT):
                        for lt in range(LT):
                            last = pe.transpose(l0_ps(u, k)[:, lt * P:(lt + 1) * P], xn[:, u * LT + lt, k * KC:(k + 1) * KC], ident[:])
                    last.then_inc(s["z_xT"], 1)
                for u in range(2):
                    pe.wait_ge(s["z_xTo"], pair * 2 + u + 1)
                    for k in range(KT):
                        last = pe.matmul(ps[0:D, 2 + u, 0:T], u_nat[:, k, :], l0_x[u][:, k, :], start=(k == 0), stop=(k == KT - 1))
                    last.then_inc(s["z_z"], 1)
                for u in range(2):
                    pe.wait_ge(s["z_rm"], pair * 2 + u + 1)
                    pe.wait_ge(s["z_zo"], pair * 2 + u + 1)
                    pe.matmul(ps[:, 4 + u, 0:T], rmi[u], l0_z[u], start=True, stop=True).then_inc(s["z_zr"], 1)
                for u in range(2):
                    pe.wait_ge(s["z_zro"], pair * 2 + u + 1)
                    for lt in range(LT):
                        pe.matmul(ps[:, 6 * u + lt, 0:C], l0_zr[u][:, lt * P:(lt + 1) * P], u_t, start=True, stop=True
                                  ).then_inc(s["z_d"], 1)

            def transposes(unit, cb):
                pe.wait_ge(s["n_xn"], unit + 1)
                for k in range(KT):
                    for lt in range(LT):
                        last = pe.transpose(ps[0:KC, k // 2, (k % 2) * T + lt * P:(k % 2) * T + (lt + 1) * P],
                                            xn[:, cb * LT + lt, k * KC:(k + 1) * KC], ident[:])
                last.then_inc(s["n_T"], 1)

            for l in range(LAYERS):
                if l == 0:
                    transposes(units_a[l], 0)
                pe.wait_ge(s["l_attnw"], 16 * ATTN_DMAS * (l + 1))
                if l:
                    pe.wait_ge(s["m_upd"], passes[l] * CT + 2)

                def output(t):
                    pe.wait_ge(s["t_pve"], t * 2 + 2)
                    for lt in range(LT):
                        for g in range(G):
                            last = pe.transpose(ps[:, 6 + lt, g * P:(g + 1) * P], o_pad[:, g, lt * P:(lt + 1) * P], ident[:])
                        last.then_inc(s["t_o"], 1)

                def output_transpose(t):
                    pe.wait_ge(s["t_on"], t * LT + LT)
                    for k in range(KT):
                        for lt in range(LT):
                            last = pe.transpose(ps[0:KC, k // 2, (k % 2) * T + lt * P:(k % 2) * T + (lt + 1) * P],
                                                o_tok[:, lt, k * KC:(k + 1) * KC], ident[:])
                    last.then_inc(s["t_oT"], 1)

                def project(t, lt):
                    pe.wait_ge(s["t_oTe"], t + 1)
                    for k in range(KT):
                        kk = KC + (k == KT - 1)
                        last = pe.matmul(ps[:, lt, 0:C], o_t[0:kk, k, lt * P:(lt + 1) * P], wp[0:kk, k, :],
                                         start=(k == 0), stop=(k == KT - 1))
                    last.then_inc(s["t_pr"], 1)

                def turn(b, first=False, last_turn=False):
                    t = b + l * B

                    def qk(which, g):
                        for k in range(KT):
                            last = pe.matmul(ps[:, 2 + 2 * which + g // 2, (g % 2) * T:(g % 2 + 1) * T],
                                             (wq, wk)[which][:, k, g * HJ:(g + 1) * HJ, :].rearrange("p h d -> p (h d)"),
                                             h_t[0:KC, k, 0:T], start=(k == 0), stop=(k == KT - 1))
                        if g % 2 == 1:
                            last.then_inc(s["t_qk"], 1)

                    def v(lt):
                        for k in range(KT):
                            kk = KC + (k == KT - 1)
                            last = pe.matmul(ps[:, 6 + lt, 0:C], h_t[0:kk, k, lt * P:(lt + 1) * P], wv[0:kk, k, :],
                                             start=(k == 0), stop=(k == KT - 1))
                        last.then_inc(s["t_v"], 1)

                    def scores(*heads):
                        for h in heads:
                            g, r = h // HJ, slice(h % HJ * HP, (h % HJ + 1) * HP)
                            if h == 0 or h == H // 2:
                                pe.wait_ge(s["t_qe"], t * 4 + (2 if h == 0 else 4))
                            if max_before[h] is not None:
                                pe.wait_ge(s["t_mxd"], t * H + max_before[h] + 1)
                            for lt in range(LT):
                                last = pe.matmul(ps[:, max_bank[h], lt * T:(lt + 1) * T], q_r[r, g, lt * P:(lt + 1) * P],
                                                 k_r[r, g, :], start=True, stop=True)
                            last.then_inc(s["t_mx"], 1)

                    def maxima(i):
                        pe.wait_ge(s["t_mxd"], t * H + (i + 1) * H // 2)
                        pe.wait_ge(s["t_ve"], t * LT + i + 1)
                        for g in (2 * i, 2 * i + 1):
                            for lt in range(LT):
                                last = pe.transpose(ps[:, 6 + i, (g % 2) * T + lt * P:(g % 2) * T + (lt + 1) * P],
                                                    nmax[:, lt, g * HJ:(g + 1) * HJ, :].rearrange("p h e -> p (h e)"), ident[:])
                        last.then_inc(s["t_nm"], 1)

                    pe.wait_ge(s["n_h"], b + units_a[l] + 1)
                    qk(0, 0)
                    qk(0, 1)
                    if not first:
                        output(t - 1)
                    qk(1, 0)
                    qk(1, 1)
                    qk(0, 2)
                    qk(0, 3)
                    scores(0, 1)
                    if not first:
                        output_transpose(t - 1)
                    qk(1, 2)
                    scores(2, 3)
                    qk(1, 3)
                    scores(4, 5)
                    v(0)
                    scores(6, 7)
                    v(1)
                    scores(8, 9, 10, 11)
                    maxima(0)
                    if not first:
                        project(t - 1, 0)
                    scores(12, 13)
                    if not first:
                        project(t - 1, 1)
                    scores(14, 15)

                    def values(h):
                        g, r = h // HJ, slice(h % HJ * HP, (h % HJ + 1) * HP)
                        pe.wait_ge(s["t_exp"], t * H + h + 1)
                        for m in range(LT):
                            last = pe.matmul(ps[r, 6 + g // 2, (g % 2) * T:(g % 2 + 1) * T], v_sb[:, m, h, :],
                                             p_t[:, h % PSLOTS, m, :], start=(m == 0), stop=(m == LT - 1))
                        last.then_inc(s["t_pv"], 1)

                    for h in range(H):
                        g, j = h // HJ, h % HJ
                        if h % 8 == 0:
                            pe.wait_ge(s["t_nma"], t * 2 + h // 8 + 1)
                        if h >= HJ:
                            pe.wait_ge(s["t_exp"], t * H + h - HJ + 1)
                        else:
                            pe.wait_ge(s["t_mxd"], t * H + H - HJ + h + 1)
                        if h % 8 == 0:
                            pe.wait_ge(s["t_lo"], t * 2 + h // 8 + 1)
                        pe.wait_ge(s["t_kz"], t * H + h + 1)
                        pe.wait_ge(s["t_kzl"], t * H + h + 1)
                        for m in range(LT):
                            for i, (kk, qq) in enumerate(((kz, q_r), (kz, q_lo), (kz_lo, q_r))):
                                last = pe.matmul(ps[:, 2 + j, m * T:(m + 1) * T], kk[:, j, m * P:(m + 1) * P],
                                                 qq[:, g, :], start=(i == 0), stop=(i == 2))
                        last.then_inc(s["t_s"], 1)
                        if h == 1:
                            maxima(1)
                        if h >= 2:
                            values(h - 2)
                        if h == NEXT_AT:
                            pe.wait_ge(s["t_xd"], t * LT + 1)
                            transposes(units_m[l] if last_turn else b + units_a[l] + 1, 0)
                        if h == NEXT_AT + 3 and last_turn:
                            pe.wait_ge(s["n_h"], units_m[l] + 1)
                            transposes(units_m[l] + 1, 1)
                    values(H - 2)
                    values(H - 1)

                turn(0, first=True)
                with pe.Fori(1, B - 1) as b:
                    turn(b)
                turn(B - 1, last_turn=True)
                output((l + 1) * B - 1)
                ne = len(experts[l])
                for n in mlp_loads[l]:
                    pe.wait_ge(s[f"l_mlpw{n}"], 16 * MLP_DMAS)
                if l == 2:
                    pe.wait_ge(s["l_wg"], 16)

                def logits():
                    for k in range(KT):
                        last = pe.matmul(ps[0:E, 7, :], wg_sb[:, k, :], h_t[0:KC, k, :], start=(k == 0), stop=(k == KT - 1))
                    last.then_inc(s["m_lg"], 1)

                def logits_transposed(c):
                    pe.wait_ge(s["m_lge"], c + 1)
                    for i in range(CT):
                        last = pe.matmul(ps[:, 7, i * E:(i + 1) * E], lg4[:, i * P:(i + 1) * P], ident[0:E, 0:E],
                                         start=True, stop=True)
                    last.then_inc(s["m_lt"], 1)

                def chunk(c, first_chunk=False, last_chunk=False):
                    pe.wait_ge(s["n_h"], c * CB + units_m[l] + CB)
                    for ei, e in enumerate(experts[l]):
                        n = c * ne + passes[l] + ei
                        for m in range(FT):
                            if m >= 3:
                                pe.wait_ge(s["m_gelu"], n * FT + m - 2)
                            for k in range(KT):
                                last = pe.matmul(ps[:, 2 + m % 3, :], w1_sb[e][:, k, m * P:(m + 1) * P], h_t[0:KC, k, :],
                                                 start=(k == 0), stop=(k == KT - 1))
                            last.then_inc(s["m_f1"], 1)
                            if first_chunk and ei == 0:
                                if m == TAIL_T:
                                    output_transpose((l + 1) * B - 1)
                                if m in (TAIL_P, TAIL_P + 1):
                                    project((l + 1) * B - 1, m - TAIL_P)
                            if l == 2 and ei == 0:
                                if m == LOGITS_AT:
                                    logits()
                                if m == FT - 1:
                                    logits_transposed(c)
                        if first_chunk and ei == 0:
                            pe.wait_ge(s["t_xd"], (l + 1) * B * LT + 1)
                        if ei == ne - 1 and not (last_chunk and l == 2):
                            transposes(units_a[l + 1] if last_chunk else c * CB + units_m[l] + CB, 0)
                        pe.wait_ge(s["m_gelu"], n * FT + FT)
                        for i in range(CT):
                            pe.wait_ge(s["m_upd"], n * CT + i + 1)
                            for m in range(FT):
                                last = pe.matmul(ps[:, 5 + i % 2, 0:C], mid[:, m, i * P:(i + 1) * P], w2_sb[e][:, m, :],
                                                 start=(m == 0), stop=(m == FT - 1))
                            last.then_inc(s["m_f2"], 1)
                            if ei == ne - 1 and i == 1 and not last_chunk:
                                pe.wait_ge(s["n_h"], c * CB + units_m[l] + CB + 1)
                                transposes(c * CB + units_m[l] + CB + 1, 1)

                chunk(0, first_chunk=True)
                with pe.Fori(1, CHUNKS - 1) as c:
                    chunk(c)
                chunk(CHUNKS - 1, last_chunk=True)

GATE_LINKS = 12
TAIL_T, TAIL_P, LOGITS_AT = 1, 3, 5


_INS = ['x', 'cond_1152', 'L0_cond_P', 'L0_cond_W', 'L0_cond_b', 'L1_cond_W_qkv', 'L1_cond_b_qkv', 'L1_cond_W_proj',
        'L1_cond_b_proj', 'L1_cond_W_fc1', 'L1_cond_b_fc1', 'L1_cond_W_fc2', 'L1_cond_b_fc2', 'L1_cond_W_ada',
        'L1_cond_b_ada', 'L2_cond_qkv_w', 'L2_cond_qkv_b', 'L2_cond_out_w', 'L2_cond_out_b', 'L2_cond_w1',
        'L2_cond_b1', 'L2_cond_w2', 'L2_cond_b2', 'L2_cond_ada_w', 'L2_cond_ada_b', 'L3_cond_w_adaln',
        'L3_cond_b_adaln', 'L3_cond_w_qkv', 'L3_cond_b_qkv', 'L3_cond_w_proj', 'L3_cond_b_proj', 'L3_cond_w_gate',
        'L3_cond_w1', 'L3_cond_b1', 'L3_cond_w2', 'L3_cond_b2']
_OUTS = [((B, T, C), 'float32')]


def kernel(**inputs):
    import numpy as _np
    import concourse.bacc as _bacc
    from concourse import mybir as _mybir
    from concourse.bass_utils import run_bass_kernel_spmd as _run

    nc = _bacc.Bacc("TRN2", target_bir_lowering=False, num_devices=1)
    arrays, args = {}, {}
    for name in _INS:
        a = _np.ascontiguousarray(inputs[name])
        arrays[f"in_{name}_dram"] = a
        args[name] = nc.dram_tensor(f"in_{name}_dram", a.shape, _mybir.dt.from_np(a.dtype), kind="ExternalInput").ap()
    for i, (shape, dtype) in enumerate(_OUTS):
        dt = _mybir.dt.from_np(_np.dtype(dtype))
        args["out"] = nc.dram_tensor(f"out_{i}_dram", shape, dt, kind="ExternalOutput").ap()
    build(nc, args)
    r = _run(nc, [arrays], core_ids=[0])
    got = tuple(r.results[0][f"out_{i}_dram"] for i in range(len(_OUTS)))
    return got[0]
```
